# Optimizing a Trainium2 kernel written in Bass

```python
import numpy as np
import jax
import jax.numpy as jnp

def _softmax(x, axis=-1):
    return jax.nn.softmax(x, axis=axis)

def _gelu(x):
    return jax.nn.gelu(x, approximate=True)

def _silu(x):
    return jax.nn.silu(x)

def _sigmoid(x):
    return jax.nn.sigmoid(x)

def _layernorm(x, axis=-1, eps=1e-05):
    m = jnp.mean(x, axis=axis, keepdims=True)
    v = jnp.var(x, axis=axis, keepdims=True)
    return (x - m) / jnp.sqrt(v + eps)

def _scatter_add(tgt, idx, src, axis=0):
    return tgt.at[idx].add(src)

def _segment_sum(src, seg, n):
    return jax.ops.segment_sum(src, seg, n)
kernel_name = 'mk_gps_d1_gnn_r16_7db51c'

def setup_inputs(seed: int=0):
    np.random.seed(seed)
    _w = jnp.asarray

    def _rec_inputs():
        import jax
        import jax.numpy as jnp
        _gk = jax.random.key(seed)
        x = -0.0002117 + 1 * jax.random.normal(jax.random.fold_in(_gk, 1), (6250, 256), jnp.float32)
        src = jax.random.randint(jax.random.fold_in(_gk, 2), (100000,), 0, 6250, jnp.int32)
        dst = jnp.minimum((6250 * jax.random.uniform(jax.random.fold_in(_gk, 3), (100000,)) ** 2.0).astype(jnp.int32), 99999)
        _o = jnp.argsort(dst, stable=True)
        src = src[_o]
        dst = dst[_o]
        edge_weight = jax.random.uniform(jax.random.fold_in(_gk, 12), (100000,), jnp.float32, 0.0, 1)
        return (x, src, dst, edge_weight)
    x, src, dst, edge_weight = _rec_inputs()

    def _L0_gnn_setup():
        import jax, jax.numpy as jnp
        import numpy as np
        N_NODES = 6250
        N_EDGES = 100000
        IN_F = 256
        HID = 256
        OUT_F = 256
        BN_EPS = 1e-05

        def make_quaternion_mul(kernel):
            dim = kernel.shape[1] // 4
            r, i, j, k = jnp.split(kernel, 4, axis=1)
            r2 = jnp.concatenate([r, -i, -j, -k], axis=0)
            i2 = jnp.concatenate([i, r, -k, j], axis=0)
            j2 = jnp.concatenate([j, k, r, -i], axis=0)
            k2 = jnp.concatenate([k, -j, i, r], axis=0)
            return jnp.concatenate([r2, i2, j2, k2], axis=1)
        key = jax.random.key(seed)
        ks = jax.random.split(key, 6)
        x = jax.random.normal(ks[0], (N_NODES, IN_F), dtype=jnp.float32)
        rows = jax.random.randint(ks[1], (N_EDGES,), 0, N_NODES, dtype=jnp.int32)
        cols = jax.random.randint(ks[2], (N_EDGES,), 0, N_NODES, dtype=jnp.int32)
        edge_vals = jax.random.uniform(ks[3], (N_EDGES,), dtype=jnp.float32)
        stdv1 = np.sqrt(6.0 / (IN_F // 4 + HID))
        weight1 = jax.random.uniform(ks[4], (IN_F // 4, HID), dtype=jnp.float32, minval=-stdv1, maxval=stdv1)
        stdv2 = np.sqrt(6.0 / (HID // 4 + OUT_F))
        weight2 = jax.random.uniform(ks[5], (HID // 4, OUT_F), dtype=jnp.float32, minval=-stdv2, maxval=stdv2)
        gamma = jnp.ones((HID,), dtype=jnp.float32)
        beta = jnp.zeros((HID,), dtype=jnp.float32)
        return {'x': x, 'rows': rows, 'cols': cols, 'edge_vals': edge_vals, 'weight1': weight1, 'weight2': weight2, 'gamma': gamma, 'beta': beta}
    _L0_gnn_all = _L0_gnn_setup()
    _L0_gnn_in = {k: v for k, v in _L0_gnn_all.items() if k in ('weight1', 'weight2', 'gamma', 'beta')}
    del _L0_gnn_all

    def _L0_mix_setup():
        import jax, jax.numpy as jnp
        import numpy as np
        MIDC = 256
        HEADS = 8
        HEADC = MIDC // HEADS
        EPS = 1e-05

        def _ln(x, gamma, beta):
            mu = jnp.mean(x, axis=-1, keepdims=True)
            var = jnp.var(x, axis=-1, keepdims=True)
            return (x - mu) * jax.lax.rsqrt(var + EPS) * gamma + beta
        key = jax.random.key(seed)
        ks = jax.random.split(key, 8)
        B, HW, C = (8, 256, MIDC)
        s = 1.0 / np.sqrt(C)
        return {'x': jax.random.normal(ks[0], (B, HW, C), jnp.float32), 'w_qkv': jax.random.normal(ks[1], (C, 3 * C), jnp.float32) * s, 'b_qkv': jnp.zeros((3 * C,), jnp.float32), 'kln_g': jnp.ones((HEADC,), jnp.float32), 'kln_b': jnp.zeros((HEADC,), jnp.float32), 'vln_g': jnp.ones((HEADC,), jnp.float32), 'vln_b': jnp.zeros((HEADC,), jnp.float32), 'w1': jax.random.normal(ks[2], (C, C), jnp.float32) * s, 'b1': jnp.zeros((C,), jnp.float32), 'w2': jax.random.normal(ks[3], (C, C), jnp.float32) * s, 'b2': jnp.zeros((C,), jnp.float32)}
    _L0_mix_all = _L0_mix_setup()
    _L0_mix_in = {k: v for k, v in _L0_mix_all.items() if k in ('w_qkv', 'b_qkv', 'kln_g', 'kln_b', 'vln_g', 'vln_b', 'w1', 'b1', 'w2', 'b2')}
    del _L0_mix_all

    def _L0_ffn_setup():
        import jax, jax.numpy as jnp
        import numpy as np
        TOP_K = 2
        LN_EPS = 1e-05
        key = jax.random.key(seed)
        ks = jax.random.split(key, 8)
        B, S, D, E, H = (16, 1024, 256, 8, 1024)
        x = jax.random.normal(ks[0], (B, S, D), dtype=jnp.float32)
        Wr = jax.random.normal(ks[1], (D, E), dtype=jnp.float32) * 0.1
        br = jnp.zeros((E,), dtype=jnp.float32)
        ln_g = jnp.ones((E, D), dtype=jnp.float32)
        ln_b = jnp.zeros((E, D), dtype=jnp.float32)
        W1 = jax.random.normal(ks[2], (E, D, H), dtype=jnp.float32) * (1.0 / np.sqrt(D))
        b1 = jnp.zeros((E, H), dtype=jnp.float32)
        W2 = jax.random.normal(ks[3], (E, H, D), dtype=jnp.float32) * (1.0 / np.sqrt(H))
        b2 = jnp.zeros((E, D), dtype=jnp.float32)
        return {'x': x, 'Wr': Wr, 'br': br, 'ln_g': ln_g, 'ln_b': ln_b, 'W1': W1, 'b1': b1, 'W2': W2, 'b2': b2}
    _L0_ffn_all = _L0_ffn_setup()
    _L0_ffn_in = {k: v for k, v in _L0_ffn_all.items() if k in ('Wr', 'br', 'ln_g', 'ln_b', 'W1', 'b1', 'W2', 'b2')}
    del _L0_ffn_all
    return {'x': x, 'src': src, 'dst': dst, 'edge_weight': edge_weight, 'L0_gnn_weight1': _L0_gnn_in['weight1'], 'L0_gnn_weight2': _L0_gnn_in['weight2'], 'L0_gnn_gamma': _L0_gnn_in['gamma'], 'L0_gnn_beta': _L0_gnn_in['beta'], 'L0_mix_w_qkv': _L0_mix_in['w_qkv'], 'L0_mix_b_qkv': _L0_mix_in['b_qkv'], 'L0_mix_kln_g': _L0_mix_in['kln_g'], 'L0_mix_kln_b': _L0_mix_in['kln_b'], 'L0_mix_vln_g': _L0_mix_in['vln_g'], 'L0_mix_vln_b': _L0_mix_in['vln_b'], 'L0_mix_w1': _L0_mix_in['w1'], 'L0_mix_b1': _L0_mix_in['b1'], 'L0_mix_w2': _L0_mix_in['w2'], 'L0_mix_b2': _L0_mix_in['b2'], 'L0_ffn_Wr': _L0_ffn_in['Wr'], 'L0_ffn_br': _L0_ffn_in['br'], 'L0_ffn_ln_g': _L0_ffn_in['ln_g'], 'L0_ffn_ln_b': _L0_ffn_in['ln_b'], 'L0_ffn_W1': _L0_ffn_in['W1'], 'L0_ffn_b1': _L0_ffn_in['b1'], 'L0_ffn_W2': _L0_ffn_in['W2'], 'L0_ffn_b2': _L0_ffn_in['b2']}

def reference(x, src, dst, edge_weight, L0_gnn_weight1, L0_gnn_weight2, L0_gnn_gamma, L0_gnn_beta, L0_mix_w_qkv, L0_mix_b_qkv, L0_mix_kln_g, L0_mix_kln_b, L0_mix_vln_g, L0_mix_vln_b, L0_mix_w1, L0_mix_b1, L0_mix_w2, L0_mix_b2, L0_ffn_Wr, L0_ffn_br, L0_ffn_ln_g, L0_ffn_ln_b, L0_ffn_W1, L0_ffn_b1, L0_ffn_W2, L0_ffn_b2):
    import jax
    import jax.numpy as jnp

    def _L0_gnn_ref(x, rows, cols, edge_vals, weight1, weight2, gamma, beta):
        import jax, jax.numpy as jnp
        import numpy as np
        N_NODES = 6250
        N_EDGES = 100000
        IN_F = 256
        HID = 256
        OUT_F = 256
        BN_EPS = 1e-05

        def make_quaternion_mul(kernel):
            dim = kernel.shape[1] // 4
            r, i, j, k = jnp.split(kernel, 4, axis=1)
            r2 = jnp.concatenate([r, -i, -j, -k], axis=0)
            i2 = jnp.concatenate([i, r, -k, j], axis=0)
            j2 = jnp.concatenate([j, k, r, -i], axis=0)
            k2 = jnp.concatenate([k, -j, i, r], axis=0)
            return jnp.concatenate([r2, i2, j2, k2], axis=1)
        hamilton1 = make_quaternion_mul(weight1)
        hamilton2 = make_quaternion_mul(weight2)
        gathered = edge_vals[:, None] * x[cols]
        new_x = jax.ops.segment_sum(gathered, rows, num_segments=N_NODES)
        out1 = new_x @ hamilton1
        mean = jnp.mean(out1, axis=0)
        var = jnp.mean(jnp.square(out1 - mean), axis=0)
        out1 = (out1 - mean) * jax.lax.rsqrt(var + BN_EPS) * gamma + beta
        out1 = jnp.tanh(out1)
        return out1 @ hamilton2

    def _L0_mix_ref(x, w_qkv, b_qkv, kln_g, kln_b, vln_g, vln_b, w1, b1, w2, b2):
        import jax, jax.numpy as jnp
        import numpy as np
        MIDC = 256
        HEADS = 8
        HEADC = MIDC // HEADS
        EPS = 1e-05

        def _ln(x, gamma, beta):
            mu = jnp.mean(x, axis=-1, keepdims=True)
            var = jnp.var(x, axis=-1, keepdims=True)
            return (x - mu) * jax.lax.rsqrt(var + EPS) * gamma + beta
        B, HW, C = x.shape
        bias = x
        qkv = (x @ w_qkv + b_qkv).reshape(B, HW, HEADS, 3 * HEADC)
        qkv = qkv.transpose(0, 2, 1, 3)
        q, k, v = jnp.split(qkv, 3, axis=-1)
        k = _ln(k, kln_g, kln_b)
        v = _ln(v, vln_g, vln_b)
        kv = jnp.einsum('bhnd,bhne->bhde', k, v) / HW
        out = jnp.einsum('bhnd,bhde->bhne', q, kv)
        out = out.transpose(0, 2, 1, 3).reshape(B, HW, C)
        ret = out + bias
        h = jax.nn.gelu(ret @ w1 + b1, approximate=False)
        return h @ w2 + b2 + bias

    def _L0_ffn_ref(x, Wr, br, ln_g, ln_b, W1, b1, W2, b2):
        import jax, jax.numpy as jnp
        import numpy as np
        TOP_K = 2
        LN_EPS = 1e-05
        B, S, D = x.shape
        N = B * S
        xt = x.reshape(N, D)
        logits = xt @ Wr + br
        probs = jax.nn.softmax(logits, axis=-1)
        top_p, top_idx = jax.lax.top_k(probs, TOP_K)
        weights = top_p / top_p.sum(axis=-1, keepdims=True)
        mu = xt.mean(axis=-1, keepdims=True)
        var = ((xt - mu) ** 2).mean(axis=-1, keepdims=True)
        xn = (xt - mu) * jax.lax.rsqrt(var + LN_EPS)
        xe = xn[None, :, :] * ln_g[:, None, :] + ln_b[:, None, :]
        h = jax.nn.gelu(jnp.einsum('end,edh->enh', xe, W1) + b1[:, None, :], approximate=False)
        y = jnp.einsum('enh,ehd->end', h, W2) + b2[:, None, :]
        y_tok = jnp.transpose(y, (1, 0, 2))
        sel = jnp.take_along_axis(y_tok, top_idx[:, :, None], axis=1)
        out = (weights[:, :, None] * sel).sum(axis=1)
        return out.reshape(B, S, D)
    xn = _layernorm(x, axis=-1)
    x = x + _L0_gnn_ref(xn, src, dst, edge_weight, L0_gnn_weight1, L0_gnn_weight2, L0_gnn_gamma, L0_gnn_beta) + _L0_mix_ref(xn[None], L0_mix_w_qkv, L0_mix_b_qkv, L0_mix_kln_g, L0_mix_kln_b, L0_mix_vln_g, L0_mix_vln_b, L0_mix_w1, L0_mix_b1, L0_mix_w2, L0_mix_b2)[0]
    x = x + _L0_ffn_ref(_layernorm(x, axis=-1)[None], L0_ffn_Wr, L0_ffn_br, L0_ffn_ln_g, L0_ffn_ln_b, L0_ffn_W1, L0_ffn_b1, L0_ffn_W2, L0_ffn_b2)[0]
    return x

_drawn_inputs = setup_inputs


def setup_inputs(seed=0):
    import zlib

    import numpy as np

    out = dict(_drawn_inputs(seed))
    spreads = {'L0_gnn_gamma': (1.0, 0.2),
     'L0_gnn_beta': (0.0, 0.1),
     'L0_mix_b_qkv': (0.0, 0.1),
     'L0_mix_kln_g': (1.0, 0.2),
     'L0_mix_kln_b': (0.0, 0.306),
     'L0_mix_vln_g': (1.0, 0.2),
     'L0_mix_vln_b': (0.0, 0.282),
     'L0_mix_b1': (0.0, 0.1),
     'L0_mix_b2': (0.0, 0.1),
     'L0_ffn_br': (0.0, 0.1),
     'L0_ffn_ln_g': (1.0, 0.2),
     'L0_ffn_ln_b': (0.0, 0.348),
     'L0_ffn_b1': (0.0, 0.341),
     'L0_ffn_b2': (0.0, 0.1)}
    factors = {}
    for name, (base, spread) in spreads.items():
        noise = np.random.default_rng([zlib.crc32(name.encode()), seed]).standard_normal(out[name].shape)
        drawn = base * np.exp(spread * noise) if base else spread * noise
        out[name] = jnp.asarray(drawn.astype(out[name].dtype))
    for name, factor in factors.items():
        out[name] = (out[name] * factor).astype(out[name].dtype)
    return out
```

```python
from contextlib import ExitStack

import concourse.bass as bass
from concourse import mybir

P = 128
ALU = mybir.AluOpType
ACT = mybir.ActivationFunctionType
F32 = mybir.dt.float32
I32 = mybir.dt.int32
U32 = mybir.dt.uint32
AX = mybir.AxisListType
EPS = 1e-5
N_ACC = 4
G_RING = 8
S_RING = 16
M_RING = 8
IDX_BATCH = 8
SLOTS = 256
GATHER_AHEAD = 5


class Program:

    def __init__(self, nc, ctx):
        self.nc, self.ctx = nc, ctx
        self.sems, self.count, self.seen = {}, {}, {}
        self.engines = {"sp": nc.sync, "act": nc.scalar, "pool": nc.gpsimd, "dve": nc.vector, "pe": nc.tensor}

    def sem(self, name):
        if name not in self.sems:
            self.sems[name] = self.ctx.enter_context(self.nc.semaphore("s_" + name))
            self.count[name] = 0
        return self.sems[name]

    def wait(self, engine, *tokens):
        for name, value in tokens:
            if self.seen.get((engine, name), 0) < value:
                self.seen[engine, name] = value
                self.engines[engine].wait_ge(self.sems[name], value)

    def run(self, engine, done, step, *after, by=1):
        self.wait(engine, *after)
        instruction = step(self.engines[engine])
        if done is None:
            return None
        instruction.then_inc(self.sem(done), by)
        self.count[done] += by
        return (done, self.count[done])

    def dma(self, engine, done, out, in_, *after):
        return self.run(engine, done, lambda e: e.dma_start(out, in_), *after, by=16)


def gps_layer(nc, x, src, dst, ew, w_gnn1, w_gnn2, w_qkv, row_bkv, kv_ln, w_mix1, w_mix2, cols_mix,
              row_b2, w_router, row_br, w_up, w_down, cols_expert, row_be, out):
    N, D = x.shape
    E = src.shape[0]
    NX, _, H = w_up.shape
    NT = -(-N // P)
    NP_ = NT * P
    TAIL = N - (NT - 1) * P
    ET = -(-E // P)
    EG = -(-ET // P)
    E_TAIL = E - (ET - 1) * P
    KC = D // P
    HC = H // P
    HEADS, HD = 8, D // 8
    CH = 512
    NCH = -(-NP_ // CH)
    TRASH = NP_
    ACC_ROWS = NP_ + P
    MT = (N * 2 + NX * (SLOTS - 1)) // SLOTS
    MT = max(MT, (NP_ * 2 + NX * (SLOTS - 1)) // SLOTS)
    XS_ROWS = MT * SLOTS
    CT = 7
    assert ET % 2 == 0 and NT % CT == 0 and D == 2 * P and XS_ROWS % 256 == 0

    xn_dram = nc.dram_tensor("xn_dram", (NP_, D), F32, kind="Internal").ap()
    acc_dram = [nc.dram_tensor(f"acc{i}_dram", (ACC_ROWS, D), F32, kind="Internal").ap() for i in range(N_ACC)]
    xs_dram = nc.dram_tensor("xs_dram", (XS_ROWS, D), F32, kind="Internal").ap()
    y_dram = nc.dram_tensor("y_dram", (XS_ROWS, D), F32, kind="Internal").ap()

    with ExitStack() as ctx:
        pr = Program(nc, ctx)
        run, wait, dma = pr.run, pr.wait, pr.dma

        def region(name, words):
            t = ctx.enter_context(nc.sbuf_tensor(name, [P, words], F32))
            at = [0]

            def carve(*shape, dtype=F32):
                n = 1
                for s in shape:
                    n *= s
                ap = t[:, at[0]:at[0] + n]
                at[0] += n
                assert at[0] <= words, (name, at[0], words)
                if dtype != F32:
                    ap = ap.bitcast(dtype)
                if len(shape) == 2:
                    ap = ap.rearrange("p (a b) -> p a b", a=shape[0])
                if len(shape) == 3:
                    ap = ap.rearrange("p (a b c) -> p a b c", a=shape[0], b=shape[1])
                return ap

            def again():
                at[0] = 0
            carve.again = again
            return carve

        bank = [ctx.enter_context(nc.psum_tensor(f"bank{i}", [P, 512], F32)) for i in range(8)]

        fixed = region("fixed", 3 * P + 512 + 8 * KC + 2 * 8 + 64)
        ident = fixed(P)
        before = fixed(P)
        after_ = fixed(P)
        zeros = fixed(512)
        cols = fixed(8, KC)
        iota8 = fixed(8)
        trash_col = fixed(1)
        ones = ctx.enter_context(nc.sbuf_tensor("ones", [P, P], F32))

        node = region("node", NT * D)
        X = node(NT, D)
        turned = region("turned", NT * D)
        xnT = turned(KC, NP_)
        third = region("third", NT * D)

        small = region("small", 6 * NT + 2 * NT + 4 * NT)
        stats = small(NT, 6)
        mv = small(NT, 2)
        rstd = small(NT)
        ve = small(NT)
        rs1 = small(NT)
        nmr = small(NT)

        work = region("work", 12600)

        src_f = third(EG, P)
        src_c = third(EG * P)
        dst_ci = third(EG * P, dtype=I32)
        w_c = third(EG * P)
        trash_minus = third(EG * P)
        dup = third(EG * P)
        put_i = third(EG * P, dtype=I32)
        S = third(S_RING, P)
        third_at = S_RING * P + 7 * EG * P
        G = third(G_RING, D)
        M = third(M_RING, D)
        raw = ctx
        third.again()
        third(third_at)
        raw_src = third(EG, P, dtype=I32)
        raw_dst = third(EG, P, dtype=I32)
        raw_w = third(EG, P)
        dst_f = third(EG, P)

        Wqkv = work(KC, 3 * D)
        Wm1 = work(KC, D)
        Wm2 = work(KC, D)
        bkv = work(2 * D)
        b2row = work(D)
        kvln = work(2, 2, HD)
        KV = work(KC, P)
        Hm = [work(KC, D), work(KC, D)]
        tmp_at = KC * (3 * D + 2 * D + P + 2 * D) + 2 * D + D + 4 * HD
        xn_ring = work(2, CT, D)
        work.again()
        work(tmp_at)
        kvs = work(2, 2 * D)
        kvd = work(2 * D)
        kvq = work(2 * D)
        kvn = work(2, 2 * D)
        ksum = work(16)
        kvar = work(16)
        kve = work(16)
        krs = work(16)
        qT = work(KC, CH)
        ret = work(KC, CH)
        hT_mix = work(KC, CH)

        def iota_mask(ap, op, base, cm, step):
            def f(e):
                return e.affine_select(out=ap, in_=ones[:, :], compare_op=op, fill=0.0, base=base,
                                       pattern=[[step, P]], channel_multiplier=cm)
            return f
        t_ones = run("dve", "ones", lambda e: e.memset(ones[:, :], 1.0))
        t_zero = run("dve", "zeros", lambda e: e.memset(zeros, 0.0))
        run("pool", "masks", iota_mask(ident, ALU.is_equal, 0, 1, -1), t_ones)
        run("pool", "masks", iota_mask(before, ALU.is_gt, 0, -1, 1))
        t_mask = run("pool", "masks", iota_mask(after_, ALU.is_gt, 0, 1, -1))
        run("pool", "masks", lambda e: e.iota(trash_col, [[0, 1]], base=TRASH, channel_multiplier=1,
                                              allow_small_or_imprecise_dtypes=True))
        t_iota = run("pool", "masks", lambda e: e.iota(iota8, [[1, 8]], base=0, channel_multiplier=0,
                                                       allow_small_or_imprecise_dtypes=True))

        xt = x[0:(NT - 1) * P, :].rearrange("(t p) d -> p t d", p=P)
        t_xpad = run("dve", "xpad", lambda e: e.memset(X[:, NT - 1, :], 0.0))
        t_x = []
        for c in range(NT // CT):
            n = CT if (c + 1) * CT < NT else CT - 1
            t_x.append(dma("sp", f"x{c}", X[:, c * CT:c * CT + n, :], xt[:, c * CT:c * CT + n, :]))
        t_x[-1] = dma("sp", f"x{NT // CT - 1}", X[0:TAIL, NT - 1, :], x[(NT - 1) * P:N, :], t_xpad)

        full = (ET - 1) // P
        last_rows = ET - 1 - full * P
        e_full = full * P * P

        pads = []
        for ap, v in ((raw_src, NP_ - 1), (raw_dst, 0), (raw_w, 0.0)):
            pads.append(run("dve", "epad", lambda e, ap=ap, v=v: e.memset(ap[:, full, :], v)))
        for ap, dram in ((raw_src, src), (raw_dst, dst), (raw_w, ew)):
            d3 = dram[0:e_full].rearrange("(g t j) -> t g j", t=P, j=P)
            dma("act", "edges", ap[:, 0:full, :], d3)
            dma("act", "edges", ap[0:last_rows, full, :],
                dram[e_full:e_full + last_rows * P].rearrange("(t j) -> t j", j=P), pads[-1])
            t_edges = dma("act", "edges", ap[last_rows:last_rows + 1, full, 0:E_TAIL],
                          dram[E - E_TAIL:E].rearrange("(t j) -> t j", t=1))

        t_wz = run("dve", "wz", lambda e: e.memset(bkv, 0.0))
        t_wz = run("dve", "wz", lambda e: e.memset(b2row, 0.0))
        dma("act", "w", Wqkv, w_qkv.rearrange("(k p) n -> p k n", p=P))
        dma("act", "w", Wm1, w_mix1.rearrange("(k p) n -> p k n", p=P))
        dma("act", "w", Wm2, w_mix2.rearrange("(k p) n -> p k n", p=P))
        dma("act", "w", bkv[0:1, :], row_bkv.rearrange("(a n) -> a n", a=1), t_wz)
        dma("act", "w", b2row[0:1, :], row_b2.rearrange("(a n) -> a n", a=1))
        dma("act", "w", kvln.rearrange("p a b c -> p (a b c)"), kv_ln.partition_broadcast(P))
        t_w = dma("act", "w", cols[:, 0:4, :].rearrange("p a b -> p (a b)"), cols_mix)

        for a in acc_dram:
            dma("sp", "acc0", a.rearrange("(p r) d -> p (r d)", p=P).rearrange("p (a b) -> p a b", b=512),
                zeros.unsqueeze(1).broadcast_to((P, ACC_ROWS * D // P // 512, 512)), t_zero)
        t_acc0 = ("acc0", pr.count["acc0"])
        t_xs0 = dma("sp", "xs0", xs_dram.rearrange("(p r) d -> p (r d)", p=P).rearrange("p (a b) -> p a b", b=512),
                    zeros.unsqueeze(1).broadcast_to((P, XS_ROWS * D // P // 512, 512)))

        def norm_stats(t_in, t):
            a = run("dve", "st", lambda e: e.bn_stats(stats[:, t, :], t_in), *dep_stats)
            return run("dve", "st", lambda e: e.bn_aggr(mv[:, t, :], stats[:, t, :]), a)

        def norm_rstd(a, b, after):
            k = run("dve", "rstd", lambda e: e.tensor_scalar(ve[:, a:b], mv[:, a:b, 1], EPS, None, ALU.add), after)
            k = run("act", "rstd_a", lambda e: e.activation(ve[:, a:b], ve[:, a:b], ACT.Sqrt), k)
            return run("dve", "rstd", lambda e: e.reciprocal(rstd[:, a:b], ve[:, a:b]), k)

        t_xnT, t_xnd = [], []
        ring_free = [[], []]
        for c in range(NT // CT):
            dep_stats = [t_x[c]]
            if c == NT // CT - 1:
                dep_stats = [t_x[c]]
            a, b = c * CT, (c + 1) * CT
            for t in range(a, b):
                k = norm_stats(X[:, t, :], t)
            k = norm_rstd(a, b, k)
            m1 = run("dve", "rstd", lambda e, a=a, b=b: e.tensor_scalar(rs1[:, a:b], rstd[:, a:b], 1.0, None, ALU.add), k)
            m2 = run("dve", "rstd", lambda e, a=a, b=b: e.scalar_tensor_tensor(
                out=nmr[:, a:b], in0=mv[:, a:b, 0], scalar=-1.0, in1=rstd[:, a:b], op0=ALU.mult, op1=ALU.mult))
            ring = xn_ring[:, c % 2]
            for t in range(a, b):
                i = t - a
                k = run("dve", "xn", lambda e, t=t, i=i, ring=ring: e.tensor_scalar(
                    ring[:, i, :], X[:, t, :], mv[:, t, 0:1], rstd[:, t:t + 1], ALU.subtract, ALU.mult),
                    m2, *ring_free[c % 2])
                run("dve", "xplus", lambda e, t=t: e.tensor_scalar(
                    X[:, t, :], X[:, t, :], rs1[:, t:t + 1], nmr[:, t:t + 1], ALU.mult, ALU.add), k)
                s = t % 4
                ps = bank[4 + s][:, 0:2 * P]
                free = [t_xnT[t - 4]] if t >= 4 else []
                for q in range(KC):
                    p_ = run("pe", "xnT_pe", lambda e, q=q, ps=ps, ring=ring, i=i: e.transpose(
                        ps[:, q * P:(q + 1) * P], ring[:, i, q * P:(q + 1) * P], ident), k, t_mask, *free)
                t_xnT.append(run("act", "xnT", lambda e, ps=ps, t=t: e.activation(
                    xnT[:, :, t * P:(t + 1) * P], ps.rearrange("p (k n) -> p k n", k=KC), ACT.Copy), p_))
            d = dma("sp", f"xnd{c % 2}", xn_dram[a * P:b * P, :].rearrange("(t p) d -> p t d", p=P), ring, k)
            ring_free[c % 2] = [d, p_]
            t_xnd = [ring_free[0][0], ring_free[1][0]] if c else [d]
        t_ring_done = ring_free[0] + ring_free[1]

        k_src = run("dve", "etab", lambda e: e.tensor_copy(src_f, raw_src), t_edges)
        k_dst = run("dve", "etab", lambda e: e.tensor_copy(dst_f, raw_dst))
        t_tab = []
        prev = t_xnT[-1]
        for n, (rows, col) in enumerate(((src_f, src_c), (raw_w, w_c), (dst_f, dst_ci))):
            for h in range(2):
                g0, g1 = (0, 4) if h == 0 else (4, EG)
                ps = bank[(2 * n + h) % 4]
                for g in range(g0, g1):
                    p_ = run("pe", "etab_pe", lambda e, g=g, g0=g0, rows=rows, ps=ps: e.transpose(
                        ps[:, (g - g0) * P:(g - g0 + 1) * P], rows[:, g, :], ident), k_dst, t_edges, t_mask,
                        *([t_tab[2 * n + h - 4]] if 2 * n + h >= 4 else []))
                t_tab.append(run("dve", "etab", lambda e, g0=g0, g1=g1, col=col, ps=ps: e.tensor_copy(
                    col[:, g0 * P:g1 * P], ps[:, 0:(g1 - g0) * P]), p_))
        t_tables = t_tab[-1]
        t_tm = run("dve", "etab", lambda e: e.tensor_scalar(
            trash_minus, src_c, -1.0, trash_col, ALU.mult, ALU.add), t_tables, t_iota)

        t_sel, t_dup, t_bc, t_sum, t_row, t_put, t_got, t_idx = {}, {}, {}, {}, {}, {}, {}, {}

        def spread(t):
            b = (t // 4) % 2
            ps = bank[b][:, (t % 4) * P:(t % 4 + 1) * P]
            free = [t_dup[t // 4 * 4 - 5]] if t >= 8 else []
            t_bc[t] = run("pe", "spread", lambda e: e.matmul(
                ps, ident[:, t % P:t % P + 1].broadcast_to((P, P)), src_f[:, t // P, :], start=True, stop=True),
                t_tables, t_tm, *free)

        def select(t):
            ps = bank[(t // 4) % 2][:, (t % 4) * P:(t % 4 + 1) * P]
            free = [t_sum[t - S_RING]] if t >= S_RING else []
            t_sel[t] = run("dve", "select", lambda e: e.tensor_scalar(
                S[:, t % S_RING, :], ps, src_c[:, t:t + 1], w_c[:, t:t + 1], ALU.is_equal, ALU.mult),
                t_bc[min(t // 4 * 4 + 3, ET - 1)], *free)
            t_dup[t] = run("dve", "dup", lambda e: e.scalar_tensor_tensor(
                out=ps, in0=ps, scalar=src_c[:, t:t + 1], in1=after_, op0=ALU.is_equal, op1=ALU.mult,
                accum_out=dup[:, t:t + 1]), t_sel[t])

        def indices(b):
            lo, hi = b * IDX_BATCH, min((b + 1) * IDX_BATCH, ET)
            k = run("dve", "idx", lambda e: e.scalar_tensor_tensor(
                out=dup[:, lo:hi], in0=dup[:, lo:hi], scalar=1.0, in1=trash_minus[:, lo:hi],
                op0=ALU.min, op1=ALU.mult), t_dup[hi - 1], t_tm)
            k = run("dve", "idx", lambda e: e.tensor_tensor(put_i[:, lo:hi], dup[:, lo:hi], src_c[:, lo:hi], ALU.add), k)
            for t in range(lo, hi):
                t_idx[t] = k

        def gather(t):
            free = [t_sum[t - G_RING]] if t >= G_RING else [t_tm]
            t_got[t] = run("pool", f"got{t % G_RING}", lambda e: e.indirect_dma_start(
                G[:, t % G_RING, :], None, xn_dram, bass.IndirectOffsetOnAxis(dst_ci[:, t:t + 1], 0)),
                *t_xnd, t_tables, *free, by=16)

        def combine(t):
            for u in (t, t + 1):
                ps = bank[2 + (t // 2) % 2][:, (u - t) * D:(u - t + 1) * D]
                free = [t_row[t - 4]] if t >= 4 else []
                t_sum[u] = run("pe", "sum", lambda e, u=u, ps=ps: e.matmul(
                    ps, S[:, u % S_RING, :], G[:, u % G_RING, :], start=True, stop=True),
                    t_got[u], t_sel[u], *free)
            free = [t_put[t - M_RING], t_put[t + 1 - M_RING]] if t >= M_RING else []
            t_row[t] = t_row[t + 1] = run("act", "row", lambda e: e.activation(
                M[:, t % M_RING:t % M_RING + 2, :].rearrange("p a b -> p (a b)"), bank[2 + (t // 2) % 2][:, :],
                ACT.Copy), t_sum[t + 1], *free)

        def put(t):
            t_put[t] = run("pool", f"put{t % N_ACC}", lambda e: e.indirect_dma_start(
                acc_dram[t % N_ACC], bass.IndirectOffsetOnAxis(put_i[:, t:t + 1], 0), M[:, t % M_RING, :], None,
                compute_op=ALU.add),
                t_row[t], t_idx[t], t_acc0, *([t_put[t - N_ACC]] if t >= N_ACC else []), by=16)

        scale_kv = 1.0 / N

        def mix():
            t_acc, t_kvn, t_cp, t_fr = [], {}, {}, {}
            first = [t_w, *t_ring_done, t_xnT[-1]]

            def kv_add(t):
                rows = TAIL if t == NT - 1 else P
                for g in range(2):
                    k = run("pe", "kvacc", lambda e, g=g: e.matmul(
                        bank[6 + g][:, 0:P], kvn[0:rows, t % 2, g * P:(g + 1) * P],
                        kvn[0:rows, t % 2, D + g * P:D + (g + 1) * P], start=(t == 0), stop=(t == NT - 1)),
                        t_kvn[t])
                t_acc.append(k)

            for t in range(NT):
                ps = bank[4 + t % 2][:, :]
                for q in range(KC):
                    run("pe", None, lambda e, q=q, ps=ps, t=t: e.matmul(
                        ps, xnT[:, q, t * P:(t + 1) * P], Wqkv[:, q, D:3 * D], start=(q == 0), stop=False),
                        *first, *([t_cp[t - 2]] if t >= 2 else []))
                p_ = run("pe", "kvp", lambda e, ps=ps: e.matmul(ps, ones[:, :], bkv, start=False, stop=True))
                free = [t_fr[t - 2]] if t >= 2 else []
                t_cp[t] = run("act", "kvcp", lambda e, ps=ps, t=t: e.activation(kvs[:, t % 2, :], ps, ACT.Copy),
                              p_, *free, *t_ring_done)
                g3 = kvs[:, t % 2, :].rearrange("p (g d) -> p g d", d=HD)
                d3 = kvd.rearrange("p (g d) -> p g d", d=HD)
                q3 = kvq.rearrange("p (g d) -> p g d", d=HD)
                n3 = kvn[:, t % 2, :].rearrange("p (g d) -> p g d", d=HD)
                k = run("dve", "kvln", lambda e: e.tensor_reduce(ksum, g3, AX.X, ALU.add), t_cp[t])
                k = run("dve", "kvln", lambda e: e.tensor_scalar(ksum, ksum, 1.0 / HD, None, ALU.mult), k)
                k = run("dve", "kvln", lambda e: e.tensor_tensor(
                    d3, g3, ksum.unsqueeze(2).broadcast_to((P, 16, HD)), ALU.subtract), k)
                t_fr[t] = k
                yield
                k = run("act", "kvsq", lambda e: e.activation(kvq, kvd, ACT.Square), k)
                k = run("dve", "kvln", lambda e: e.tensor_reduce(kvar, q3, AX.X, ALU.add), k)
                k = run("dve", "kvln", lambda e: e.tensor_scalar(kve, kvar, 1.0 / HD, EPS, ALU.mult, ALU.add), k)
                k = run("act", "kvsq", lambda e: e.activation(kve, kve, ACT.Sqrt), k)
                yield
                k = run("dve", "kvln", lambda e: e.reciprocal(krs, kve), k)
                k = run("dve", "kvln", lambda e: e.tensor_tensor(
                    d3, d3, krs.unsqueeze(2).broadcast_to((P, 16, HD)), ALU.mult), k)
                for i, op in ((0, ALU.mult), (1, ALU.add)):
                    wv = kvln[:, i].unsqueeze(2).broadcast_to((P, 2, 8, HD))
                    o4 = kvd if i == 0 else kvn[:, t % 2, :]
                    free = [t_acc[t - 2]] if i and t >= 2 else []
                    k = run("dve", "kvln", lambda e, wv=wv, o4=o4, op=op: e.tensor_tensor(
                        o4.rearrange("p (s h d) -> p s h d", s=2, d=HD),
                        kvd.rearrange("p (s h d) -> p s h d", s=2, d=HD), wv, op), k, *free)
                t_kvn[t] = k
                if t:
                    kv_add(t - 1)
                yield
            kv_add(NT - 1)
            k = run("dve", "KV", lambda e: e.memset(KV, 0.0), t_acc[-1])
            for g in range(2):
                for h in range(4):
                    r = slice(h * HD, (h + 1) * HD)
                    t_KV = run("dve", "KV", lambda e, g=g, r=r: e.tensor_scalar(
                        KV[r, g, r], bank[6 + g][r, r], scale_kv, None, ALU.mult), k)
            yield
            t_h, t_ret, t_q, t_fin, t_o = {}, {}, {}, {}, {}
            for c in range(NCH):
                lo, hi = c * CH, min((c + 1) * CH, NP_)
                w = hi - lo
                for m in range(KC):
                    psq, pso = bank[4 + m], bank[6 + m]
                    for q in range(KC):
                        p_ = run("pe", "mq", lambda e, q=q, m=m, psq=psq: e.matmul(
                            psq[:, 0:w], Wqkv[:, q, m * P:(m + 1) * P], xnT[:, q, lo:hi],
                            start=(q == 0), stop=(q == KC - 1)), t_KV, t_cp[NT - 1],
                            *([t_h[c - 1, m], t_fin[c - 1]] if c else []))
                    t_q[m] = run("act", "mqa", lambda e, m=m, psq=psq: e.activation(
                        qT[:, m, 0:w], psq[:, 0:w], ACT.Identity, bias=cols[:, 0, m:m + 1]), p_,
                        *([t_o[m]] if c else []))
                    yield
                for m in range(KC):
                    pso = bank[6 + m]
                    t_o[m] = run("pe", "mo", lambda e, m=m, pso=pso: e.matmul(
                        pso[:, 0:w], KV[:, m, :], qT[:, m, 0:w], start=True, stop=True), t_q[m])
                    t_ret[m] = run("dve", "mret", lambda e, m=m, pso=pso: e.tensor_tensor(
                        ret[:, m, 0:w], pso[:, 0:w], xnT[:, m, lo:hi], ALU.add), t_o[m],
                        *([t_hp] if c else []))
                    yield
                for m in range(KC):
                    psh = bank[4 + m]
                    for q in range(KC):
                        t_hp = run("pe", "mh", lambda e, q=q, m=m, psh=psh: e.matmul(
                            psh[:, 0:w], Wm1[:, q, m * P:(m + 1) * P], ret[:, q, 0:w],
                            start=(q == 0), stop=(q == KC - 1)), t_ret[q], t_q[m])
                    t_h[c, m] = run("act", "mha", lambda e, m=m, psh=psh: e.activation(
                        hT_mix[:, m, 0:w], psh[:, 0:w], ACT.Gelu, bias=cols[:, 1, m:m + 1]), t_hp,
                        *([t_fp] if c else []))
                    yield
                for j in range(w // P):
                    t = c * 4 + j
                    psy = bank[6 + j % 2][:, 256:512] if False else bank[6 + j % 2][:, 0:D]
                    for q in range(KC):
                        run("pe", None, lambda e, q=q, j=j, psy=psy: e.matmul(
                            psy, hT_mix[:, q, j * P:(j + 1) * P], Wm2[:, q, :], start=(q == 0), stop=False),
                            t_h[c, q], t_ret[j % 2], *([t_fin[c, j - 2]] if j >= 2 else []))
                    t_fp = run("pe", "mfp", lambda e, psy=psy: e.matmul(psy, ones[:, :], b2row, start=False, stop=True))
                    t_fin[c, j] = t_fin[c] = run("dve", "mfin", lambda e, t=t, psy=psy: e.tensor_tensor(
                        X[:, t, :], X[:, t, :], psy, ALU.add), t_fp, *([] if c else [("xplus", pr.count["xplus"])]))
                    if j % 2:
                        yield
            t_mix_done.append(t_fin[NCH - 1])
            t_mix_done.append(t_hp)
            t_mix_done.append(t_fp)
            while True:
                yield

        t_mix_done = []
        mixer = mix()
        done_sel = 0
        for t in range(ET):
            while done_sel < ET and min(done_sel + 4, ET) <= t + S_RING:
                q4 = min(done_sel + 4, ET)
                for u in range(done_sel, q4):
                    spread(u)
                for u in range(done_sel, q4):
                    select(u)
                    if (u + 1) % IDX_BATCH == 0 or u == ET - 1:
                        indices(u // IDX_BATCH)
                done_sel = q4
            for u in range(t if t else 0, min(t + GATHER_AHEAD + 1, ET)):
                if u not in t_got:
                    gather(u)
            if t % 2 == 0:
                combine(t)
            put(t)
            next(mixer)
        while not t_mix_done:
            next(mixer)

        quat = [[(0, 1), (1, 1), (2, 1), (3, 1)], [(1, -1), (0, 1), (3, 1), (2, -1)],
                [(2, -1), (3, -1), (0, 1), (1, 1)], [(3, -1), (2, 1), (1, -1), (0, 1)]]
        Q4 = D // 4
        hraw = qT.rearrange("p a b -> p (a b)")
        for i, wd in enumerate((w_gnn1, w_gnn2)):
            for half in range(2):
                t_hr = dma("sp", "hraw", hraw[half * Q4:(half + 1) * Q4, i * D:(i + 1) * D], wd, *t_mix_done)
        for i in range(2):
            for a in range(4):
                for b in range(4):
                    comp, sign = quat[a][b]
                    r = slice((a % 2) * Q4, (a % 2 + 1) * Q4)
                    t_H = run("dve", "ham", lambda e, i=i, a=a, b=b, r=r, comp=comp, sign=sign: e.tensor_scalar(
                        Hm[i][r, a // 2, b * Q4:(b + 1) * Q4], hraw[r, i * D + comp * Q4:i * D + (comp + 1) * Q4],
                        float(sign), None, ALU.mult), t_hr, *t_ring_done)

        third.again()
        out1T = third(KC, NP_)
        newT = xnT
        third_free = [t_put[ET - 1 - i] for i in range(min(N_ACC, ET))] + [t_sum[ET - 1], t_idx[ET - 1]]
        work.again()
        work(tmp_at)
        accs = work(2, N_ACC, D)
        bst = work(KC, NCH, 6)
        bmv = work(KC, 2)
        bsc = work(KC)
        bbi = work(KC)
        assert 2 * N_ACC * D <= 2 * 2 * D + 2 * D + 2 * D + 2 * 2 * D + 64 + KC * CH

        t_sumd, t_newT, t_accp = {}, {}, {}
        t_load = {}
        pso_free, t_bn = {}, []
        for t in range(NT):
            for i in range(N_ACC):
                t_load[t] = dma("sp", f"accl{t % 2}", accs[:, t % 2, i, :], acc_dram[i][t * P:(t + 1) * P, :],
                                *third_free, *t_mix_done, t_H, *([t_accp[t - 2]] if t >= 2 else []))
            k = run("dve", "accs", lambda e, t=t: e.tensor_tensor(
                accs[:, t % 2, 0:2, :], accs[:, t % 2, 0:2, :], accs[:, t % 2, 2:4, :], ALU.add), t_load[t])
            k = run("dve", "accs", lambda e, t=t: e.tensor_tensor(
                accs[:, t % 2, 0, :], accs[:, t % 2, 0, :], accs[:, t % 2, 1, :], ALU.add), k)
            ps = bank[t % 4][:, 0:2 * P]
            for q in range(KC):
                p_ = run("pe", "newp", lambda e, q=q, ps=ps, t=t: e.transpose(
                    ps[:, q * P:(q + 1) * P], accs[:, t % 2, 0, q * P:(q + 1) * P], ident), k,
                    *([t_newT[t - 4]] if t >= 4 else []))
            t_accp[t] = p_
            t_newT[t] = run("act", "newT", lambda e, ps=ps, t=t: e.activation(
                newT[:, :, t * P:(t + 1) * P], ps.rearrange("p (k n) -> p k n", k=KC), ACT.Copy), p_)
            if t % 4 == 3 or t == NT - 1:
                c = t // 4
                lo, hi = c * CH, min((c + 1) * CH, NP_)
                w = hi - lo
                v = min(hi, N) - lo
                for m in range(KC):
                    ps = bank[4 + (2 * c + m) % 4]
                    for q in range(KC):
                        p_ = run("pe", "o1p", lambda e, q=q, m=m, ps=ps, w=w, lo=lo, hi=hi: e.matmul(
                            ps[:, 0:w], Hm[0][:, q, m * P:(m + 1) * P], newT[:, q, lo:hi],
                            start=(q == 0), stop=(q == KC - 1)), t_newT[t], t_H, *pso_free.get((2 * c + m) % 4, []))
                    ka = run("act", "o1", lambda e, m=m, ps=ps, w=w, lo=lo, hi=hi: e.activation(
                        out1T[:, m, lo:hi], ps[:, 0:w], ACT.Copy), p_)
                    kb = run("dve", "bst", lambda e, m=m, c=c, v=v, lo=lo: e.bn_stats(
                        bst[:, m, c, :], out1T[:, m, lo:lo + v]), ka)
                    pso_free[(2 * c + m) % 4] = [ka]
        for m in range(KC):
            k = run("dve", "bst", lambda e, m=m: e.bn_aggr(bmv[:, m, :], bst[:, m].rearrange("p a b -> p (a b)")), kb)
        k = run("dve", "bst", lambda e: e.tensor_scalar(bsc, bmv[:, :, 1], EPS, None, ALU.add), k)
        k = run("act", "bsq", lambda e: e.activation(bsc, bsc, ACT.Sqrt), k)
        k = run("dve", "bst", lambda e: e.reciprocal(bsc, bsc), k)
        k = run("dve", "bst", lambda e: e.tensor_tensor(bsc, bsc, cols[:, 2, :], ALU.mult), k)
        k = run("dve", "bst", lambda e: e.scalar_tensor_tensor(
            out=bbi, in0=bmv[:, :, 0], scalar=-1.0, in1=bsc, op0=ALU.mult, op1=ALU.mult), k)
        t_bn = run("dve", "bst", lambda e: e.tensor_tensor(bbi, bbi, cols[:, 3, :], ALU.add), k)

        turned.again()
        Xh = turned(NT, D)
        work.again()
        work(tmp_at)
        Wr = work(KC, NX)
        brow = work(NX)
        L = work(NT, NX)
        zT = work(2, KC, P)
        top = work(NT, 8)
        topi = work(NT, 8, dtype=U32)
        oh1 = work(NT, NX)
        oh2 = work(NT, NX)
        ohs = work(NT, NX)
        place = work(NT, NX)
        cnt = work(NT, NX)
        prob = work(NT, 2)
        psum_ = work(NT)
        wts = work(NT, 2)
        idf = work(NT, 2)
        posf = work(NT, 2)
        pos_i = work(NT, 2, dtype=I32)
        tot = work(NX)
        toti = work(NX, dtype=I32)
        endf = work(NX)
        base = work(NX)
        tile_start = work(MT)
        tcmp = work(MT, NX)
        tex = work(MT)
        tex_i = work(MT, dtype=I32)

        t_stage4 = [t_bn, p_, ka]
        t_th, t_x2, t_ps, t_st = {}, {}, {}, []
        for c in range(NCH):
            lo, hi = c * CH, min((c + 1) * CH, NP_)
            for m in range(KC):
                t_th[c] = run("act", "tanh", lambda e, m=m, lo=lo, hi=hi: e.activation(
                    out1T[:, m, lo:hi], out1T[:, m, lo:hi], ACT.Tanh, bias=bbi[:, m:m + 1], scale=bsc[:, m:m + 1]),
                    *t_stage4)
            for j in range((hi - lo) // P):
                t = 4 * c + j
                ps = bank[t % 4][:, 0:D]
                for q in range(KC):
                    p_ = run("pe", "o2p", lambda e, q=q, t=t, ps=ps: e.matmul(
                        ps, out1T[:, q, t * P:(t + 1) * P], Hm[1][:, q, :], start=(q == 0), stop=(q == KC - 1)),
                        t_th[c], *([t_x2[t - 4]] if t >= 4 else []))
                t_x2[t] = run("dve", "x2", lambda e, t=t, ps=ps: e.tensor_tensor(
                    X[:, t, :], X[:, t, :], ps, ALU.add), p_)
                dep_stats = [t_x2[t]]
                k = norm_stats(X[:, t, :], t)
        t_o2p = p_
        k = norm_rstd(0, NT, k)
        for t in range(NT):
            k2 = run("dve", "z", lambda e, t=t: e.tensor_scalar(
                Xh[:, t, :], X[:, t, :], mv[:, t, 0:1], rstd[:, t:t + 1], ALU.subtract, ALU.mult), k, t_o2p)
            t_ps[t] = k2
        t_rw = run("dve", "brz", lambda e: e.memset(brow, 0.0), t_o2p)
        dma("sp", "rw", brow[0:1, :], row_br.rearrange("(a n) -> a n", a=1), t_rw)
        t_rw = dma("sp", "rw", Wr, w_router.rearrange("(k p) n -> p k n", p=P))
        t_zT, t_lg = {}, {}
        for t in range(NT):
            ps = bank[t % 4][:, 0:2 * P]
            for q in range(KC):
                p_ = run("pe", "zp", lambda e, q=q, t=t, ps=ps: e.transpose(
                    ps[:, q * P:(q + 1) * P], Xh[:, t, q * P:(q + 1) * P], ident), t_ps[t],
                    *([t_zT[t - 4]] if t >= 4 else []))
            t_zT[t] = run("act", "zT", lambda e, t=t, ps=ps: e.activation(
                zT[:, t % 2], ps.rearrange("p (k n) -> p k n", k=KC), ACT.Copy), p_,
                *([t_lg[t - 2]] if t >= 2 else []))
            pl = bank[4][:, t * NX:(t + 1) * NX]
            for q in range(KC):
                run("pe", None, lambda e, q=q, t=t, pl=pl: e.matmul(
                    pl, zT[:, t % 2, q, :], Wr[:, q, :], start=(q == 0), stop=False), t_zT[t], t_rw)
            t_lg[t] = run("pe", "lg", lambda e, pl=pl: e.matmul(pl, ones[:, :], brow, start=False, stop=True))
        t_L = run("dve", "L", lambda e: e.tensor_copy(L.rearrange("p a b -> p (a b)"), bank[4][:, 0:NT * NX]),
                  t_lg[NT - 1])
        for t in range(NT):
            k = run("dve", "max", lambda e, t=t: e.max(top[:, t, :], L[:, t, :]), t_L)
            k = run("dve", "max", lambda e, t=t: e.max_index(topi[:, t, :], top[:, t, :], L[:, t, :]), k)
        t_max = k
        k = run("dve", "rt", lambda e: e.tensor_copy(idf, topi[:, :, 0:2]), t_max)
        t_oh = []
        for i, oh in enumerate((oh1, oh2)):
            t_oh.append(run("dve", "rt", lambda e, i=i, oh=oh: e.tensor_tensor(
                oh, iota8.unsqueeze(1).broadcast_to((P, NT, NX)),
                idf[:, :, i:i + 1].broadcast_to((P, NT, NX)), ALU.is_equal), k))
        k = run("dve", "rt", lambda e: e.tensor_tensor(ohs, oh1, oh2, ALU.add), *t_oh)
        flat = ohs.rearrange("p a b -> p (a b)")
        run("pe", None, lambda e: e.matmul(bank[5][:, 0:NT * NX], ones[:, :], flat, start=True, stop=True), k)
        p_ = run("pe", "rank", lambda e: e.matmul(bank[6][:, 0:NT * NX], before, flat, start=True, stop=True))
        k = run("dve", "rt", lambda e: e.tensor_copy(cnt.rearrange("p a b -> p (a b)"), bank[5][:, 0:NT * NX]), p_)
        for x_ in range(NX):
            k2 = run("dve", "rt", lambda e, x_=x_: e.tensor_tensor_scan(
                place[:, :, x_], ones[:, 0:NT], cnt[:, :, x_], 0.0, ALU.mult, ALU.add), k)
        k = run("dve", "rt", lambda e: e.tensor_scalar(toti, place[:, NT - 1, :], float(SLOTS - 1), None, ALU.add), k2)
        k = run("dve", "rt", lambda e: e.tensor_scalar(
            toti, toti, SLOTS.bit_length() - 1, None, ALU.logical_shift_right), k)
        k = run("dve", "rt", lambda e: e.tensor_scalar(tot, toti, float(SLOTS), None, ALU.mult), k)
        k = run("dve", "rt", lambda e: e.tensor_tensor_scan(endf, ones[:, 0:NX], tot, 0.0, ALU.mult, ALU.add), k)
        t_end = k
        k = run("dve", "rt", lambda e: e.tensor_tensor(base, endf, tot, ALU.subtract), k)
        k = run("dve", "rt", lambda e: e.tensor_tensor(place, place, cnt, ALU.subtract), k)
        k = run("dve", "rt", lambda e: e.tensor_tensor(
            place, place, bank[6][:, 0:NT * NX].rearrange("p (a b) -> p a b", b=NX), ALU.add), k)
        k = run("dve", "rt", lambda e: e.tensor_tensor(
            place, place, base.unsqueeze(1).broadcast_to((P, NT, NX)), ALU.add), k)
        for i, oh in enumerate((oh1, oh2)):
            kk = run("dve", "rt", lambda e, oh=oh: e.tensor_tensor(ohs, oh, place, ALU.mult), k, p_)
            k = run("dve", "rt", lambda e, i=i: e.tensor_reduce(posf[:, :, i], ohs, AX.X, ALU.add), kk)
        t_pos = run("dve", "rt", lambda e: e.tensor_copy(pos_i, posf), k)
        k = run("pool", "tst", lambda e: e.iota(tile_start, [[SLOTS, MT]], base=0, channel_multiplier=0,
                                                allow_small_or_imprecise_dtypes=True), t_end)
        k = run("dve", "rt", lambda e: e.tensor_tensor(
            tcmp, tile_start.unsqueeze(2).broadcast_to((P, MT, NX)),
            endf.unsqueeze(1).broadcast_to((P, MT, NX)), ALU.is_ge), k)
        k = run("dve", "rt", lambda e: e.tensor_reduce(tex, tcmp, AX.X, ALU.add), k)
        t_tex = run("dve", "rt", lambda e: e.tensor_scalar(tex_i, tex, float(NX - 1), None, ALU.min), k)
        for t in range(NT):
            dep_stats = [t_zT[NT - 1]]
            k = norm_stats(Xh[:, t, :], t)
        k = norm_rstd(0, NT, k)
        t_xs = []
        for t in range(NT):
            k2 = run("dve", "xh", lambda e, t=t: e.tensor_scalar(
                Xh[:, t, :], Xh[:, t, :], mv[:, t, 0:1], rstd[:, t:t + 1], ALU.subtract, ALU.mult), k)
            for i in range(2):
                t_xs.append(run("pool", "xs", lambda e, t=t, i=i: e.indirect_dma_start(
                    xs_dram, bass.IndirectOffsetOnAxis(pos_i[:, t, i:i + 1], 0), Xh[:, t, :], None),
                    k2, t_pos, t_xs0, by=16))
        k = run("dve", "sm", lambda e: e.tensor_tensor(
            L, L, top[:, :, 0:1].broadcast_to((P, NT, NX)), ALU.subtract), t_max)
        k = run("dve", "sm", lambda e: e.tensor_tensor(
            prob, top[:, :, 0:2], top[:, :, 0:1].broadcast_to((P, NT, 2)), ALU.subtract), k)
        run("act", None, lambda e: e.activation(L, L, ACT.Exp), k)
        k = run("act", "sma", lambda e: e.activation(prob, prob, ACT.Exp))
        k = run("dve", "sm", lambda e: e.tensor_reduce(psum_, L, AX.X, ALU.add), k)
        k = run("dve", "sm", lambda e: e.reciprocal(psum_, psum_), k)
        k = run("dve", "sm", lambda e: e.tensor_tensor(
            prob, prob, psum_.unsqueeze(2).broadcast_to((P, NT, 2)), ALU.mult), k)
        k = run("dve", "sm", lambda e: e.tensor_tensor(psum_, prob[:, :, 0], prob[:, :, 1], ALU.add), k)
        k = run("dve", "sm", lambda e: e.reciprocal(psum_, psum_), k)
        t_wts = run("dve", "sm", lambda e: e.tensor_tensor(
            wts, prob, psum_.unsqueeze(2).broadcast_to((P, NT, 2)), ALU.mult), k)

        third.again()
        W1 = third(2, KC, H)
        W2 = third(2, HC, D)
        ecol = third(2, 2 * KC + HC)
        erow = third(2, D)
        xe = third(2, 2, D)
        xeT = third(2, KC, SLOTS)
        turned_free = t_xs[-1]
        turned.again()
        hT = turned(2, HC, SLOTS)
        yb = turned(2, 2, D)
        t_er = run("dve", "erz", lambda e: e.memset(erow, 0.0), t_o2p)
        t_l1, t_l2, t_wl, t_xl, t_y, t_ys, t_xT, t_g = {}, {}, {}, {}, {}, {}, {}, {}
        t_xp, t_hb, t_yb = {}, {}, {}

        def weights(i):
            b = i % 2
            free = [t_l2[i - 2]] if i >= 2 else [t_o2p, t_er]
            wait("sp", *free, t_tex)
            name = f"wl{b}"

            wait("sp", turned_free)
            x_ = nc.sync.value_load(tex_i[0:1, i:i + 1], min_val=0, max_val=NX - 1)
            dma("sp", name, W1[:, b], w_up[bass.ds(x_, 1), :, :].rearrange("a (k p) n -> p (a k) n", p=P))
            dma("sp", name, W2[:, b], w_down[bass.ds(x_, 1), :, :].rearrange("a (k p) n -> p (a k) n", p=P))
            dma("sp", name, ecol[:, b, :], cols_expert[bass.ds(x_, 1), :, :].rearrange("a p n -> (a p) n"))
            dma("sp", name, erow[0:1, b, :], row_be[bass.ds(x_, 1), :])
            dma("sp", name, xe[:, b], xs_dram[i * SLOTS:(i + 1) * SLOTS, :].rearrange("(c p) d -> p c d", p=P))
            t_wl[i] = (name, pr.count[name])

        weights(0)
        for i in range(MT):
            b = i % 2
            if i + 1 < MT:
                weights(i + 1)
            for q in range(KC):
                ps = bank[q][:, 0:SLOTS]
                for c in range(2):
                    p_ = run("pe", "xeT", lambda e, q=q, c=c, ps=ps, b=b: e.transpose(
                        ps[:, c * P:(c + 1) * P], xe[:, b, c, q * P:(q + 1) * P], ident), t_wl[i], t_L,
                        *([t_xT[i - 1]] if i else []))
                k = run("dve", "xeTd", lambda e, q=q, ps=ps, b=b: e.tensor_scalar(
                    xeT[:, b, q, :], ps, ecol[:, b, q:q + 1], ecol[:, b, KC + q:KC + q + 1], ALU.mult, ALU.add), p_,
                    *([t_l1[i - 2]] if i >= 2 else []))
            t_xT[i] = k
            for h in range(HC):
                ps = bank[2 + h % 4][:, 0:SLOTS]
                n = i * HC + h
                for q in range(KC):
                    p_ = run("pe", "l1", lambda e, q=q, h=h, ps=ps, b=b: e.matmul(
                        ps, W1[:, b, q, h * P:(h + 1) * P], xeT[:, b, q, :], start=(q == 0), stop=(q == KC - 1)),
                        t_xT[i], t_pos, *([t_g[n - 4]] if n >= 4 else []))
                t_g[n] = run("act", "g", lambda e, h=h, ps=ps, b=b: e.activation(
                    hT[:, b, h, :], ps, ACT.Gelu, bias=ecol[:, b, 2 * KC + h:2 * KC + h + 1]), p_,
                    *([t_l2[i - 2]] if i >= 2 else [turned_free]))
            t_l1[i] = p_
            for c in range(2):
                ps = bank[6 + c][:, 0:D]
                for h in range(HC):
                    run("pe", None, lambda e, h=h, c=c, ps=ps, b=b: e.matmul(
                        ps, hT[:, b, h, c * P:(c + 1) * P], W2[:, b, h, :], start=(h == 0), stop=False),
                        t_g[i * HC + h], *([t_y[i - 1, c]] if i else []))
                p_ = run("pe", "l2", lambda e, ps=ps, b=b: e.matmul(ps, ones[:, :], erow[:, b, :], start=False, stop=True))
                t_y[i, c] = run("dve", "y", lambda e, c=c, ps=ps, b=b: e.tensor_copy(yb[:, b, c, :], ps), p_,
                                *([t_ys[i - 2]] if i >= 2 else []), turned_free)
            t_l2[i] = p_
            t_ys[i] = dma("act", f"ys{b}", y_dram[i * SLOTS:(i + 1) * SLOTS, :].rearrange("(c p) d -> p c d", p=P),
                          yb[:, b], t_y[i, 1])

        turned.again()
        turned(4 * D + 2 * HC * SLOTS)
        yg = turned(4, 2, D)
        t_c, t_o = {}, {}
        for t in range(NT):
            s = t % 4
            for i in range(2):
                k = run("pool", f"yg{s}", lambda e, t=t, i=i, s=s: e.indirect_dma_start(
                    yg[:, s, i, :], None, y_dram, bass.IndirectOffsetOnAxis(pos_i[:, t, i:i + 1], 0)),
                    t_ys[MT - 1], t_ys[MT - 2], *([t_c[t - 4]] if t >= 4 else []), by=16)
            for i in range(2):
                k = run("dve", "fin", lambda e, t=t, i=i, s=s: e.scalar_tensor_tensor(
                    out=X[:, t, :], in0=yg[:, s, i, :], scalar=wts[:, t, i:i + 1], in1=X[:, t, :],
                    op0=ALU.mult, op1=ALU.add), k, t_wts)
            t_c[t] = k
            rows = TAIL if t == NT - 1 else P
            k = dma("sp", "out", out[t * P:t * P + rows, :], X[0:rows, t, :], k)
        wait("sp", k)


def kernel(x, src, dst, edge_weight, L0_gnn_weight1, L0_gnn_weight2, L0_gnn_gamma, L0_gnn_beta, L0_mix_w_qkv,
           L0_mix_b_qkv, L0_mix_kln_g, L0_mix_kln_b, L0_mix_vln_g, L0_mix_vln_b, L0_mix_w1, L0_mix_b1, L0_mix_w2,
           L0_mix_b2, L0_ffn_Wr, L0_ffn_br, L0_ffn_ln_g, L0_ffn_ln_b, L0_ffn_W1, L0_ffn_b1, L0_ffn_W2, L0_ffn_b2):
    import numpy as np
    import concourse.bacc as bacc
    from concourse.bass_utils import run_bass_kernel_spmd

    D, heads = 256, 8
    hd = D // heads

    def col(v):
        return np.asarray(v).reshape(-1, P).T
    bq3 = np.asarray(L0_mix_b_qkv).reshape(heads, 3, hd)
    NX = L0_ffn_W1.shape[0]
    arrays = {
        "x": x, "src": src, "dst": dst, "ew": edge_weight, "w_gnn1": L0_gnn_weight1, "w_gnn2": L0_gnn_weight2,
        "w_qkv": np.asarray(L0_mix_w_qkv).reshape(D, heads, 3, hd).transpose(0, 2, 1, 3).reshape(D, 3 * D),
        "row_bkv": bq3[:, 1:].transpose(1, 0, 2).reshape(2 * D),
        "kv_ln": np.concatenate([np.asarray(v) for v in (L0_mix_kln_g, L0_mix_vln_g, L0_mix_kln_b, L0_mix_vln_b)]),
        "w_mix1": L0_mix_w1, "w_mix2": L0_mix_w2,
        "cols_mix": np.concatenate([col(bq3[:, 0].reshape(D)), col(L0_mix_b1), col(L0_gnn_gamma), col(L0_gnn_beta)], 1),
        "row_b2": L0_mix_b2, "w_router": L0_ffn_Wr, "row_br": L0_ffn_br, "w_up": L0_ffn_W1, "w_down": L0_ffn_W2,
        "cols_expert": np.concatenate([np.asarray(v).reshape(NX, -1, P).transpose(0, 2, 1)
                                       for v in (L0_ffn_ln_g, L0_ffn_ln_b, L0_ffn_b1)], 2),
        "row_be": L0_ffn_b2,
    }
    arrays = {f"in_{n}": np.ascontiguousarray(a) for n, a in arrays.items()}
    nc = bacc.Bacc("TRN2", target_bir_lowering=False, num_devices=1)
    args = [nc.dram_tensor(n, a.shape, mybir.dt.from_np(a.dtype), kind="ExternalInput").ap() for n, a in arrays.items()]
    out = nc.dram_tensor("out", tuple(x.shape), F32, kind="ExternalOutput").ap()
    gps_layer(nc, *args, out)
    r = run_bass_kernel_spmd(nc, [arrays], core_ids=[0])
    return r.results[0]["out"]
```

```python
from contextlib import ExitStack

import concourse.bass as bass
from concourse import mybir

P = 128
ALU = mybir.AluOpType
ACT = mybir.ActivationFunctionType
F32 = mybir.dt.float32
BF16 = mybir.dt.bfloat16
I32 = mybir.dt.int32
U32 = mybir.dt.uint32
AX = mybir.AxisListType
EPS = 1e-5
N_ACC = 4
QUAD = 4
MIX_FIRST = 20
S_QUADS = 3
SLOTS = 256


class Program:

    def __init__(self, nc, ctx):
        self.nc, self.ctx = nc, ctx
        self.sems, self.count, self.seen = {}, {}, {}
        self.engines = {"sp": nc.sync, "act": nc.scalar, "pool": nc.gpsimd, "dve": nc.vector, "pe": nc.tensor}

    def sem(self, name):
        if name not in self.sems:
            self.sems[name] = self.ctx.enter_context(self.nc.semaphore("s_" + name))
            self.count[name] = 0
        return self.sems[name]

    def wait(self, engine, *tokens):
        for name, value in tokens:
            if self.seen.get((engine, name), 0) < value:
                self.seen[engine, name] = value
                self.engines[engine].wait_ge(self.sems[name], value)

    def run(self, engine, done, step, *after, by=1):
        self.wait(engine, *after)
        instruction = step(self.engines[engine])
        if done is None:
            return None
        instruction.then_inc(self.sem(done), by)
        self.count[done] += by
        return (done, self.count[done])

    def dma(self, engine, done, out, in_, *after):
        return self.run(engine, done, lambda e: e.dma_start(out, in_), *after, by=16)


def gps_layer(nc, x, src, dst, ew, w_gnn1, w_gnn2, w_qkv, row_bkv, kv_ln, w_mix1, w_mix2, cols_mix,
              row_b2, w_router, row_br, w_up, w_down, cols_expert, row_be, out):
    N, D = x.shape
    E = src.shape[0]
    NX, _, H = w_up.shape
    NT = -(-N // P)
    NP_ = NT * P
    TAIL = N - (NT - 1) * P
    ET = -(-E // P)
    EG = -(-ET // P)
    E_TAIL = E - (ET - 1) * P
    KC = D // P
    HC = H // P
    HEADS, HD = 8, D // 8
    CH = 512
    NCH = -(-NP_ // CH)
    TRASH = NP_
    ACC_ROWS = NP_ + P
    MT = (N * 2 + NX * (SLOTS - 1)) // SLOTS
    MT = max(MT, (NP_ * 2 + NX * (SLOTS - 1)) // SLOTS)
    XS_ROWS = MT * SLOTS
    CT = 7
    NQ = -(-ET // QUAD)
    assert ET % 2 == 0 and NT % CT == 0 and D == 2 * P and XS_ROWS % 256 == 0

    xn_dram = nc.dram_tensor("xn_dram", (NP_, D), F32, kind="Internal").ap()
    acc_dram = [nc.dram_tensor(f"acc{i}_dram", (ACC_ROWS, D), F32, kind="Internal").ap() for i in range(N_ACC)]
    xs_dram = nc.dram_tensor("xs_dram", (XS_ROWS, D), F32, kind="Internal").ap()
    y_dram = nc.dram_tensor("y_dram", (XS_ROWS, D), F32, kind="Internal").ap()

    with ExitStack() as ctx:
        pr = Program(nc, ctx)
        run, wait, dma = pr.run, pr.wait, pr.dma

        def region(name, words):
            t = ctx.enter_context(nc.sbuf_tensor(name, [P, words], F32))
            at = [0]

            def carve(*shape, dtype=F32):
                n = 1
                for s in shape:
                    n *= s
                ap = t[:, at[0]:at[0] + n]
                at[0] += n
                assert at[0] <= words, (name, at[0], words)
                if dtype != F32:
                    ap = ap.bitcast(dtype)
                if len(shape) == 2:
                    ap = ap.rearrange("p (a b) -> p a b", a=shape[0])
                if len(shape) == 3:
                    ap = ap.rearrange("p (a b c) -> p a b c", a=shape[0], b=shape[1])
                return ap

            def again():
                at[0] = 0
            carve.again = again
            return carve

        bank = [ctx.enter_context(nc.psum_tensor(f"bank{i}", [P, 512], F32)) for i in range(8)]

        fixed = region("fixed", 4 * P + 512 + 8 * KC + 16 + 4 + 3 * P // 2)
        ident = fixed(P)
        before = fixed(P)
        after_ = fixed(P)
        zeros = fixed(512)
        cols = fixed(8, KC)
        iota8 = fixed(8)
        iota_p = fixed(P)
        missed = fixed(1)
        missed_i = fixed(1, dtype=I32)
        ident_b = fixed(P // 2).bitcast(BF16)
        ones_b = fixed(P // 2).bitcast(BF16)
        trash_col = fixed(1)
        ones = ctx.enter_context(nc.sbuf_tensor("ones", [P, P], F32))

        node = region("node", NT * D)
        X = node(NT, D)
        turned = region("turned", NT * D)
        xnT = turned(KC, NP_)
        third = region("third", NT * D)

        small = region("small", 6 * NT + 2 * NT + 4 * NT)
        stats = small(NT, 6)
        mv = small(NT, 2)
        rstd = small(NT)
        ve = small(NT)

        work = region("work", 12992)

        src_hi = third(EG * P // 2).bitcast(BF16).rearrange("p (a b) -> p a b", a=EG)
        src_lo = third(EG * P // 2).bitcast(BF16).rearrange("p (a b) -> p a b", a=EG)
        src_c = third(EG * P)
        w_c = third(EG * P)
        trash_minus = third(EG * P)
        dup = third(EG * P)
        put_i = third(EG * P, dtype=I32)
        dst_rel = third(EG * P)
        tables_end = 7 * EG * P
        S = third(S_QUADS * QUAD, P)
        OH = third(2 * QUAD, P)
        B = third(2 * QUAD, P)
        M = third(2 * QUAD, D)
        third.again()
        third(tables_end)
        raw_src = third(EG, P, dtype=I32)
        raw_dst = third(EG, P, dtype=I32)
        raw_w = third(EG, P)
        src_f = third(EG, P)
        dst_f = third(EG, P)

        Wqkv = work(KC, 3 * D)
        Wm1 = work(KC, D)
        Wm2 = work(KC, D)
        bkv = work(2 * D)
        b2row = work(D)
        kvln = work(2, 2, HD)
        KV = work(KC, P)
        Hm = [work(KC, D), work(KC, D)]
        tmp_at = KC * (3 * D + 2 * D + P + 2 * D) + 2 * D + D + 4 * HD
        xn_ring = work(2, CT, D)
        raw_dstq = work(2, QUAD * P, dtype=I32)
        diag = work(2, P)
        least = work(2)
        base_row = work(2 * P)
        dst_c = work(EG * P)
        assert QUAD * P == 512
        work.again()
        work(tmp_at)
        kvs = work(2, 2 * D)
        kvd = work(2 * D)
        kvq = work(2 * D)
        kvn = work(2, 2 * D)
        ksum = work(16)
        kvar = work(16)
        kve = work(16)
        krs = work(16)
        qT = work(KC, CH)
        ret = work(KC, CH)
        hT_mix = work(KC, CH)
        base_i = work(2 * P, dtype=I32)
        win = work(3, D)
        bkv_b = work(D).bitcast(BF16)
        b2_b = work(D // 2).bitcast(BF16)

        def iota_mask(ap, op, base, cm, step):
            def f(e):
                return e.affine_select(out=ap, in_=ones[:, :], compare_op=op, fill=0.0, base=base,
                                       pattern=[[step, P]], channel_multiplier=cm)
            return f
        t_ones = run("dve", "ones", lambda e: e.memset(ones[:, :], 1.0))
        t_zero = run("dve", "zeros", lambda e: e.memset(zeros, 0.0))
        run("pool", "masks", iota_mask(ident, ALU.is_equal, 0, 1, -1), t_ones)
        run("pool", "masks", iota_mask(before, ALU.is_gt, 0, -1, 1))
        t_mask = run("pool", "masks", iota_mask(after_, ALU.is_gt, 0, 1, -1))
        run("pool", "masks", lambda e: e.iota(trash_col, [[0, 1]], base=TRASH, channel_multiplier=1,
                                              allow_small_or_imprecise_dtypes=True))
        t_iota = run("pool", "masks", lambda e: e.iota(iota8, [[1, 8]], base=0, channel_multiplier=0,
                                                       allow_small_or_imprecise_dtypes=True))
        t_iota = run("pool", "masks", lambda e: e.iota(iota_p, [[1, P]], base=0, channel_multiplier=0,
                                                       allow_small_or_imprecise_dtypes=True))
        run("dve", "identb", lambda e: e.tensor_copy(ident_b, ident), t_mask)
        t_identb = run("dve", "identb", lambda e: e.memset(ones_b, 1.0))

        xt = x[0:(NT - 1) * P, :].rearrange("(t p) d -> p t d", p=P)
        t_xpad = run("dve", "xpad", lambda e: e.memset(X[:, NT - 1, :], 0.0))
        t_x = []
        for c in range(NT // CT):
            n = CT if (c + 1) * CT < NT else CT - 1
            t_x.append(dma("sp", f"x{c}", X[:, c * CT:c * CT + n, :], xt[:, c * CT:c * CT + n, :]))
        t_x[-1] = dma("sp", f"x{NT // CT - 1}", X[0:TAIL, NT - 1, :], x[(NT - 1) * P:N, :], t_xpad)

        full = (ET - 1) // P
        last_rows = ET - 1 - full * P
        e_full = full * P * P

        pads = []
        for ap, v in ((raw_src, NP_ - 1), (raw_dst, N - 1), (raw_w, 0.0)):
            pads.append(run("dve", "epad", lambda e, ap=ap, v=v: e.memset(ap[:, full, :], v)))
        for ap, dram in ((raw_src, src), (raw_dst, dst), (raw_w, ew)):
            d3 = dram[0:e_full].rearrange("(g t j) -> t g j", t=P, j=P)
            dma("act", "edges", ap[:, 0:full, :], d3)
            dma("act", "edges", ap[0:last_rows, full, :],
                dram[e_full:e_full + last_rows * P].rearrange("(t j) -> t j", j=P), pads[-1])
            t_edges = dma("act", "edges", ap[last_rows:last_rows + 1, full, 0:E_TAIL],
                          dram[E - E_TAIL:E].rearrange("(t j) -> t j", t=1))

        QE = QUAD * P
        q_full = E // QE
        k = run("dve", "epad", lambda e: e.memset(raw_dstq[:, 1, :], N - 1))
        dma("act", "edges", raw_dstq[:, 0, :], dst[0:P * QE].rearrange("(q j) -> q j", j=QE))
        dma("act", "edges", raw_dstq[0:q_full - P, 1, :], dst[P * QE:q_full * QE].rearrange("(q j) -> q j", j=QE), k)
        t_edges = dma("act", "edges", raw_dstq[q_full - P:q_full - P + 1, 1, 0:E - q_full * QE],
                      dst[q_full * QE:E].rearrange("(q j) -> q j", q=1))

        t_wz = run("dve", "wz", lambda e: e.memset(bkv, 0.0))
        t_wz = run("dve", "wz", lambda e: e.memset(b2row, 0.0))
        dma("act", "w", Wqkv, w_qkv.rearrange("(k p) n -> p k n", p=P))
        dma("act", "w", Wm1, w_mix1.rearrange("(k p) n -> p k n", p=P))
        dma("act", "w", Wm2, w_mix2.rearrange("(k p) n -> p k n", p=P))
        dma("act", "w", bkv[0:3, :], row_bkv.partition_broadcast(3), t_wz)
        dma("act", "w", b2row[0:3, :], row_b2.partition_broadcast(3))
        dma("act", "w", kvln.rearrange("p a b c -> p (a b c)"), kv_ln.partition_broadcast(P))
        t_w = dma("act", "w", cols[:, 0:4, :].rearrange("p a b -> p (a b)"), cols_mix)

        def norm_stats(t_in, t):
            a = run("dve", "st", lambda e: e.bn_stats(stats[:, t, :], t_in), *dep_stats)
            return run("dve", "st", lambda e: e.bn_aggr(mv[:, t, :], stats[:, t, :]), a)

        def norm_rstd(a, b, after):
            k = run("dve", "rstd", lambda e: e.tensor_scalar(ve[:, a:b], mv[:, a:b, 1], EPS, None, ALU.add), after)
            k = run("act", "rstd_a", lambda e: e.activation(ve[:, a:b], ve[:, a:b], ACT.Sqrt), k)
            return run("dve", "rstd", lambda e: e.reciprocal(rstd[:, a:b], ve[:, a:b]), k)

        t_xnT, t_xnd = [], []
        ring_free = [[], []]
        for c in range(NT // CT):
            dep_stats = [t_x[c]]
            if c == NT // CT - 1:
                dep_stats = [t_x[c]]
            a, b = c * CT, (c + 1) * CT
            for t in range(a, b):
                k = norm_stats(X[:, t, :], t)
            k0 = norm_rstd(a, b, k)
            ring = xn_ring[:, c % 2]
            for t in range(a, b):
                i = t - a
                k = run("dve", "xn", lambda e, t=t, i=i, ring=ring: e.tensor_scalar(
                    ring[:, i, :], X[:, t, :], mv[:, t, 0:1], rstd[:, t:t + 1], ALU.subtract, ALU.mult),
                    k0, *ring_free[c % 2])
                s = t % 4
                ps = bank[4 + s][:, 0:2 * P]
                free = [t_xnT[t - 4]] if t >= 4 else []
                for q in range(KC):
                    p_ = run("pe", "xnT_pe", lambda e, q=q, ps=ps, ring=ring, i=i: e.transpose(
                        ps[:, q * P:(q + 1) * P], ring[:, i, q * P:(q + 1) * P], ident), k, t_mask, *free)
                t_xnT.append(run("act", "xnT", lambda e, ps=ps, t=t: e.activation(
                    xnT[:, :, t * P:(t + 1) * P], ps.rearrange("p (k n) -> p k n", k=KC), ACT.Copy), p_))
            d = dma("sp", f"xnd{c % 2}", xn_dram[a * P:b * P, :].rearrange("(t p) d -> p t d", p=P), ring, k)
            t_xplus = run("dve", "xplus", lambda e: e.tensor_tensor(
                X[:, a:b, :], X[:, a:b, :], ring, ALU.add), k)
            ring_free[c % 2] = [d, p_, t_xplus]
        t_xnd = [ring_free[0][0], ring_free[1][0]]
        t_ring_done = ring_free[0] + ring_free[1]

        for a in acc_dram:
            dma("sp", "acc0", a.rearrange("(p r) d -> p (r d)", p=P).rearrange("p (a b) -> p a b", b=512),
                zeros.unsqueeze(1).broadcast_to((P, ACC_ROWS * D // P // 512, 512)), t_zero)
        t_acc0 = ("acc0", pr.count["acc0"])

        tmp_i = dst_f.bitcast(I32)
        k = run("dve", "etab", lambda e: e.tensor_scalar(
            tmp_i, raw_src, 6, 6, ALU.logical_shift_right, ALU.logical_shift_left), t_edges)
        k = run("dve", "etab", lambda e: e.tensor_copy(src_hi, tmp_i), k)
        k = run("dve", "etab", lambda e: e.tensor_scalar(tmp_i, raw_src, 63, None, ALU.bitwise_and), k)
        k = run("dve", "etab", lambda e: e.tensor_copy(src_lo, tmp_i), k)
        run("dve", "etab", lambda e: e.tensor_copy(src_f, raw_src))
        k = run("dve", "etab", lambda e: e.tensor_copy(dst_f, raw_dst), k)
        t_split = k
        k = run("dve", "etab", lambda e: e.tensor_reduce(least, raw_dstq, AX.X, ALU.min), k)
        k = run("dve", "etab", lambda e: e.tensor_scalar(least, least, float(NP_ - P), None, ALU.min), k)
        for h in range(2):
            k2 = run("dve", "etab", lambda e: e.tensor_scalar(
                diag[:, h, :], ident, least[:, h:h + 1], None, ALU.mult), k, t_mask)
        p_ = run("pe", "etab_pe", lambda e: e.matmul(
            bank[2][:, 0:2 * P], ones[:, :], diag.rearrange("p a b -> p (a b)"), start=True, stop=True), k2)
        run("dve", "etab", lambda e: e.tensor_copy(base_row, bank[2][:, 0:2 * P]), p_)
        t_base = run("dve", "etab", lambda e: e.tensor_copy(base_i, bank[2][:, 0:2 * P]))
        evac = {}
        for n, (rows, col) in enumerate(((src_f, src_c), (raw_w, w_c), (dst_f, dst_c))):
            for h in range(2):
                g0, g1 = (0, 4) if h == 0 else (4, EG)
                use = 2 * n + h
                ps = bank[use % 2]
                for g in range(g0, g1):
                    p_ = run("pe", "etab_pe", lambda e: e.transpose(
                        ps[:, (g - g0) * P:(g - g0 + 1) * P], rows[:, g, :], ident), t_split, t_edges,
                        *([evac[use - 2]] if use >= 2 else []))
                evac[use] = run("dve", "etab", lambda e: e.tensor_copy(col[:, g0 * P:g1 * P], ps[:, 0:(g1 - g0) * P]), p_)
        t_cols = evac[5]
        run("dve", "etab", lambda e: e.tensor_scalar(trash_minus, src_c, -1.0, trash_col, ALU.mult, ALU.add),
            t_cols, t_iota)
        t_tables = run("dve", "etab", lambda e: e.tensor_tensor(
            dst_rel.rearrange("p (q j) -> p q j", j=QUAD), dst_c.rearrange("p (q j) -> p q j", j=QUAD),
            base_row[:, 0:EG * P // QUAD].unsqueeze(2).broadcast_to((P, EG * P // QUAD, QUAD)), ALU.subtract), t_base)

        t_sel, t_dup, t_oh, t_idx, t_bt, t_Bs, t_sum, t_row, t_put, t_win = ({} for _ in range(10))

        def tiles(q):
            return range(q * QUAD, min((q + 1) * QUAD, ET))

        def spread(q, dep=()):
            for t in tiles(q):
                ps = bank[q % 2][:, (t % QUAD) * P:(t % QUAD + 1) * P]
                row = ident_b[:, t % P:t % P + 1].broadcast_to((P, P))
                run("pe", None, lambda e: e.matmul(ps, row, src_hi[:, t // P, :], start=True, stop=False),
                    t_tables, t_identb, *([t_dup[q - 2]] if q >= 2 else []), *dep)
                k = run("pe", "spread", lambda e: e.matmul(ps, row, src_lo[:, t // P, :], start=False, stop=True))
            return k

        def select(q, t_spread):
            for t in tiles(q):
                ps = bank[q % 2][:, (t % QUAD) * P:(t % QUAD + 1) * P]
                t_sel[q] = run("dve", "select", lambda e: e.tensor_scalar(
                    S[:, t % (S_QUADS * QUAD), :], ps, src_c[:, t:t + 1], w_c[:, t:t + 1], ALU.is_equal, ALU.mult),
                    t_spread, *([t_bt[q - S_QUADS]] if q >= S_QUADS else []))
            for t in tiles(q):
                ps = bank[q % 2][:, (t % QUAD) * P:(t % QUAD + 1) * P]
                t_dup[q] = run("dve", "dup", lambda e: e.scalar_tensor_tensor(
                    out=ps, in0=ps, scalar=src_c[:, t:t + 1], in1=after_, op0=ALU.is_equal, op1=ALU.mult,
                    accum_out=dup[:, t:t + 1]), t_sel[q])
            for t in tiles(q):
                t_oh[q] = run("dve", "oh", lambda e: e.tensor_scalar(
                    OH[:, t % (2 * QUAD), :], iota_p, dst_rel[:, t:t + 1], None, ALU.is_equal),
                    *([t_bt[q - 2]] if q >= 2 else []))

        def indices(q):
            lo, hi = tiles(q)[0], tiles(q)[-1] + 1
            k = run("dve", "idx", lambda e: e.scalar_tensor_tensor(
                out=dup[:, lo:hi], in0=dup[:, lo:hi], scalar=1.0, in1=trash_minus[:, lo:hi],
                op0=ALU.min, op1=ALU.mult), t_dup[q])
            t_idx[q] = run("dve", "idx", lambda e: e.tensor_tensor(put_i[:, lo:hi], dup[:, lo:hi], src_c[:, lo:hi], ALU.add), k)

        def window(q):
            wait("sp", t_base, *t_xnd, *([t_sum[q - 3]] if q >= 3 else []), *t_ring_done)
            row = nc.sync.value_load(base_i[0:1, q:q + 1], min_val=0, max_val=NP_ - P)
            t_win[q] = dma("sp", f"win{q % 3}", win[:, q % 3, :], xn_dram[bass.ds(row, P), :])

        def between(q):
            n = len(tiles(q))
            for t in tiles(q):
                t_bt[q] = run("pe", "bt", lambda e: e.matmul(
                    bank[2][:, (t % QUAD) * P:(t % QUAD + 1) * P], OH[:, t % (2 * QUAD), :],
                    S[:, t % (S_QUADS * QUAD), :], start=True, stop=True),
                    t_oh[q], t_sel[q], *([t_Bs[q - 1]] if q else [t_base]))
            t_Bs[q] = run("act", "Bs", lambda e: e.activation(
                B[:, (q % 2) * QUAD:(q % 2) * QUAD + n, :].rearrange("p a b -> p (a b)"), bank[2][:, 0:n * P], ACT.Copy),
                t_bt[q], *([t_sum[q - 2]] if q >= 2 else []))

        def combine(q):
            for h, t in enumerate(tiles(q)[::2]):
                ps = bank[3 + h]
                for u in (t, t + 1):
                    t_sum[q] = run("pe", "sum", lambda e: e.matmul(
                        ps[:, (u - t) * D:(u - t + 1) * D], B[:, u % (2 * QUAD), :], win[:, q % 3, :],
                        start=True, stop=True), t_Bs[q], t_win[q], *([t_row[t - QUAD]] if q else []))
                t_row[t] = t_row[t + 1] = run("act", "row", lambda e: e.activation(
                    M[:, t % (2 * QUAD):t % (2 * QUAD) + 2, :].rearrange("p a b -> p (a b)"), ps[:, :], ACT.Copy),
                    t_sum[q], *([t_put[t - 2 * QUAD], t_put[t + 1 - 2 * QUAD]] if q >= 2 else []))

        def put(t):
            t_put[t] = run("pool", f"put{t % N_ACC}", lambda e: e.indirect_dma_start(
                acc_dram[t % N_ACC], bass.IndirectOffsetOnAxis(put_i[:, t:t + 1], 0), M[:, t % (2 * QUAD), :], None,
                compute_op=ALU.add),
                t_row[t], t_idx[t // QUAD], t_acc0, *([t_put[t - N_ACC]] if t >= N_ACC else []), by=16)

        scale_kv = 1.0 / N

        def mix():
            t_acc, t_kvn, t_cp, t_fr = [], {}, {}, {}
            first = [t_w, *t_ring_done, t_xnT[-1], t_tables]
            for row, row_b in ((bkv, bkv_b), (b2row, b2_b)):
                n = row.shape[1]
                p1, r = kvd.bitcast(BF16)[:, 0:n], kvq[:, 0:n]
                k = run("dve", "bias", lambda e: e.tensor_copy(p1, row), *first)
                run("dve", "bias", lambda e: e.tensor_scalar(row_b, p1, ident[:, 0:1], None, ALU.mult), k)
                k = run("dve", "bias", lambda e: e.tensor_tensor(r, row, p1, ALU.subtract), k)
                k = run("dve", "bias", lambda e: e.tensor_copy(p1, r), k)
                run("dve", "bias", lambda e: e.scalar_tensor_tensor(
                    out=row_b, in0=p1, scalar=ident[:, 1:2], in1=row_b, op0=ALU.mult, op1=ALU.add), k)
                k = run("dve", "bias", lambda e: e.tensor_tensor(r, r, p1, ALU.subtract), k)
                k = run("dve", "bias", lambda e: e.scalar_tensor_tensor(
                    out=row_b, in0=r, scalar=ident[:, 2:3], in1=row_b, op0=ALU.mult, op1=ALU.add), k)
                t_bias = k
            yield

            def kv_add(t):
                rows = TAIL if t == NT - 1 else P
                for g in range(2):
                    k = run("pe", "kvacc", lambda e: e.matmul(
                        bank[6 + g][:, 0:P], kvn[0:rows, t % 2, g * P:(g + 1) * P],
                        kvn[0:rows, t % 2, D + g * P:D + (g + 1) * P], start=(t == 0), stop=(t == NT - 1)),
                        t_kvn[t])
                t_acc.append(k)

            for t in range(NT):
                ps = bank[5][:, :]
                for q in range(KC):
                    run("pe", None, lambda e: e.matmul(
                        ps, xnT[:, q, t * P:(t + 1) * P], Wqkv[:, q, D:3 * D], start=(q == 0), stop=False),
                        *first, *([t_cp[t - 1]] if t else []))
                p_ = run("pe", "kvp", lambda e: e.matmul(ps, ones_b, bkv_b, start=False, stop=True), t_bias)
                t_cp[t] = run("act", "kvcp", lambda e: e.activation(kvs[:, t % 2, :], ps, ACT.Copy),
                              p_, *([t_fr[t - 2]] if t >= 2 else []))
                yield
                g3 = kvs[:, t % 2, :].rearrange("p (g d) -> p g d", d=HD)
                d3 = kvd.rearrange("p (g d) -> p g d", d=HD)
                q3 = kvq.rearrange("p (g d) -> p g d", d=HD)
                k = run("dve", "kvln", lambda e: e.tensor_reduce(ksum, g3, AX.X, ALU.add), t_cp[t])
                k = run("dve", "kvln", lambda e: e.tensor_scalar(ksum, ksum, 1.0 / HD, None, ALU.mult), k)
                k = run("dve", "kvln", lambda e: e.tensor_tensor(
                    d3, g3, ksum.unsqueeze(2).broadcast_to((P, 16, HD)), ALU.subtract), k)
                t_fr[t] = k
                k = run("act", "kvsq", lambda e: e.activation(kvq, kvd, ACT.Square), k)
                yield
                k = run("dve", "kvln", lambda e: e.tensor_reduce(kvar, q3, AX.X, ALU.add), k)
                k = run("dve", "kvln", lambda e: e.tensor_scalar(kve, kvar, 1.0 / HD, EPS, ALU.mult, ALU.add), k)
                k = run("act", "kvsq", lambda e: e.activation(kve, kve, ACT.Sqrt), k)
                yield
                k = run("dve", "kvln", lambda e: e.reciprocal(krs, kve), k)
                k = run("dve", "kvln", lambda e: e.tensor_tensor(
                    d3, d3, krs.unsqueeze(2).broadcast_to((P, 16, HD)), ALU.mult), k)
                for i, op in ((0, ALU.mult), (1, ALU.add)):
                    wv = kvln[:, i].unsqueeze(2).broadcast_to((P, 2, 8, HD))
                    o4 = kvd if i == 0 else kvn[:, t % 2, :]
                    k = run("dve", "kvln", lambda e: e.tensor_tensor(
                        o4.rearrange("p (s h d) -> p s h d", s=2, d=HD),
                        kvd.rearrange("p (s h d) -> p s h d", s=2, d=HD), wv, op), k,
                        *([t_acc[t - 2]] if i and t >= 2 else []))
                t_kvn[t] = k
                if t:
                    kv_add(t - 1)
                yield
            kv_add(NT - 1)
            k = run("dve", "KV", lambda e: e.memset(KV, 0.0))
            for g in range(2):
                for h in range(4):
                    r = slice(h * HD, (h + 1) * HD)
                    t_KV = run("dve", "KV", lambda e: e.tensor_scalar(
                        KV[r, g, r], bank[6 + g][r, r], 1.0 / N, None, ALU.mult), k, t_acc[-1])
            yield

            uses = []

            def next_bank():
                n = len(uses)
                return bank[5 + n % 3], ([uses[n - 3]] if n >= 3 else [t_KV, t_cp[NT - 1]])

            t_retp, t_hp, t_fp = {}, {}, {}
            for c in range(NCH):
                lo, hi = c * CH, min((c + 1) * CH, NP_)
                w = hi - lo
                t_q, t_ret, t_h = {}, {}, {}
                for m in range(KC):
                    ps, free = next_bank()
                    for q in range(KC):
                        p_ = run("pe", "mq", lambda e: e.matmul(
                            ps[:, 0:w], Wqkv[:, q, m * P:(m + 1) * P], xnT[:, q, lo:hi],
                            start=(q == 0), stop=(q == KC - 1)), *free)
                    t_q[m] = run("act", "mqa", lambda e: e.activation(
                        qT[:, m, 0:w], ps[:, 0:w], ACT.Identity, bias=cols[:, 0, m:m + 1]), p_,
                        *([t_retp[c - 1, m]] if c else []))
                    uses.append(t_q[m])
                    yield
                for m in range(KC):
                    ps, free = next_bank()
                    t_retp[c, m] = run("pe", "mo", lambda e: e.matmul(
                        ps[:, 0:w], KV[:, m, :], qT[:, m, 0:w], start=True, stop=True), t_q[m], *free)
                    t_ret[m] = run("dve", "mret", lambda e: e.tensor_tensor(
                        ret[:, m, 0:w], ps[:, 0:w], xnT[:, m, lo:hi], ALU.add), t_retp[c, m],
                        *([t_hp[c - 1]] if c else []))
                    uses.append(t_ret[m])
                    yield
                for m in range(KC):
                    ps, free = next_bank()
                    for q in range(KC):
                        t_hp[c] = run("pe", "mh", lambda e: e.matmul(
                            ps[:, 0:w], Wm1[:, q, m * P:(m + 1) * P], ret[:, q, 0:w],
                            start=(q == 0), stop=(q == KC - 1)), t_ret[q], *free)
                    t_h[m] = run("act", "mha", lambda e: e.activation(
                        hT_mix[:, m, 0:w], ps[:, 0:w], ACT.Gelu, bias=cols[:, 1, m:m + 1]), t_hp[c],
                        *([t_fp[c - 1]] if c else []))
                    uses.append(t_h[m])
                    yield
                for j in range(w // P):
                    t = c * 4 + j
                    ps, free = next_bank()
                    for q in range(KC):
                        run("pe", None, lambda e: e.matmul(
                            ps[:, 0:D], hT_mix[:, q, j * P:(j + 1) * P], Wm2[:, q, :], start=(q == 0), stop=False),
                            t_h[q], *free)
                    t_fp[c] = run("pe", "mfp", lambda e: e.matmul(ps[:, 0:D], ones_b, b2_b, start=False, stop=True))
                    uses.append(run("dve", "mfin", lambda e: e.tensor_tensor(
                        X[:, t, :], X[:, t, :], ps[:, 0:D], ALU.add), t_fp[c], t_xplus))
                    if j % 2:
                        yield
            t_mix_done.extend([uses[-1], t_hp[NCH - 1], t_fp[NCH - 1], t_h[1]])
            while True:
                yield

        t_mix_done = []
        mixer = mix()
        for q in range(3):
            window(q)
        for q in range(2):
            select(q, spread(q))
            indices(q)
        for _ in range(MIX_FIRST):
            next(mixer)
        between(0)
        steps = 0.0
        for q in range(NQ):
            if q + 2 < NQ:
                select(q + 2, spread(q + 2))
                indices(q + 2)
            if steps >= 1 or q % 2 == 0:
                next(mixer)
            if q + 1 < NQ:
                between(q + 1)
            combine(q)
            if q + 3 < NQ:
                window(q + 3)
            for t in tiles(q):
                put(t)
            next(mixer)
        while not t_mix_done:
            next(mixer)

        all_put = [t_put[ET - 1 - i] for i in range(N_ACC)]
        w_missed, tmp_c = S.rearrange("p a b -> p (a b)")[:, 0:EG * P], M.rearrange("p a b -> p (a b)")[:, 0:EG * P]
        dst_ci = B.rearrange("p a b -> p (a b)")[:, 0:EG * P].bitcast(I32)
        k = run("dve", "miss", lambda e: e.tensor_scalar(tmp_c, dst_rel, float(P), None, ALU.is_ge), *all_put, t_sum[NQ - 1])
        k = run("dve", "miss", lambda e: e.scalar_tensor_tensor(
            out=tmp_c, in0=dst_rel, scalar=0.0, in1=tmp_c, op0=ALU.is_lt, op1=ALU.add), k)
        k2 = run("dve", "miss", lambda e: e.tensor_tensor(w_missed, w_c, tmp_c, ALU.mult), k)
        k = run("dve", "miss", lambda e: e.tensor_reduce(missed, tmp_c[:, 0:ET], AX.X, ALU.add), k)
        p_ = run("pe", "missp", lambda e: e.matmul(bank[2][:, 0:1], ones[:, :], missed, start=True, stop=True), k)
        t_miss = run("dve", "miss", lambda e: e.tensor_copy(missed_i, bank[2][:, 0:1]), p_)
        k = run("dve", "miss", lambda e: e.tensor_tensor(
            tmp_c.rearrange("p (q j) -> p q j", j=QUAD), dst_rel.rearrange("p (q j) -> p q j", j=QUAD),
            base_i[:, 0:EG * P // QUAD].unsqueeze(2).broadcast_to((P, EG * P // QUAD, QUAD)), ALU.add), k2, t_miss)
        t_dci = run("dve", "miss", lambda e: e.tensor_copy(dst_ci, tmp_c), k)
        every = ("sp", "act", "pool", "dve", "pe")
        for name in every:
            wait(name, t_dci, t_miss)
        second = {n: pr.sem("second_" + n) for n in ("spread", "select", "sum", "row")}
        got = [pr.sem(f"second_got{i}") for i in range(3)]
        added = [pr.sem(f"second_put{i}") for i in range(N_ACC)]

        def if_missed(e):
            return e.If(e.value_load(missed_i[0:1, 0:1], min_val=0, max_val=E) != 0)

        def wait_added(e, t):
            e.wait_ge(added[t % N_ACC], 16 * (t // N_ACC + 1))


        with nc.Block() as block:
            @block.tensor
            def _(e):
                with if_missed(e):
                    def sum_missed(t):
                        e.wait_ge(second["select"], t + 1)
                        e.wait_ge(got[t % 3], 16 * (t // 3 + 1))
                        if t >= 2:
                            e.wait_ge(second["row"], t - 1)
                        e.matmul(bank[3 + t % 2][:, 0:D], OH[:, t % 2, :], win[:, t % 3, :],
                                 start=True, stop=True).then_inc(second["sum"], 1)
                    for t in range(ET):
                        if t >= 2:
                            e.wait_ge(second["select"], t - 1)
                        row = ident_b[:, t % P:t % P + 1].broadcast_to((P, P))
                        e.matmul(bank[t % 2][:, 0:P], row, src_hi[:, t // P, :], start=True, stop=False)
                        e.matmul(bank[t % 2][:, 0:P], row, src_lo[:, t // P, :], start=False, stop=True)\
                            .then_inc(second["spread"], 1)
                        if t:
                            sum_missed(t - 1)
                    sum_missed(ET - 1)

            @block.vector
            def _(e):
                with if_missed(e):
                    for t in range(ET):
                        e.wait_ge(second["spread"], t + 1)
                        if t >= 2:
                            e.wait_ge(second["sum"], t - 1)
                        e.tensor_scalar(OH[:, t % 2, :], bank[t % 2][:, 0:P], src_c[:, t:t + 1], w_missed[:, t:t + 1],
                                        ALU.is_equal, ALU.mult).then_inc(second["select"], 1)

            @block.scalar
            def _(e):
                with if_missed(e):
                    for t in range(ET):
                        e.wait_ge(second["sum"], t + 1)
                        if t >= 2:
                            wait_added(e, t - 2)
                        e.activation(M[:, QUAD + t % 2, :], bank[3 + t % 2][:, 0:D], ACT.Copy).then_inc(second["row"], 1)

            @block.gpsimd
            def _(e):
                with if_missed(e):
                    def put_missed(t):
                        e.wait_ge(second["row"], t + 1)
                        if t >= N_ACC:
                            wait_added(e, t - N_ACC)
                        e.indirect_dma_start(acc_dram[t % N_ACC], bass.IndirectOffsetOnAxis(put_i[:, t:t + 1], 0),
                                             M[:, QUAD + t % 2, :], None, compute_op=ALU.add).then_inc(added[t % N_ACC], 16)
                    for t in range(ET):
                        if t >= 3:
                            e.wait_ge(second["sum"], t - 2)
                        e.indirect_dma_start(win[:, t % 3, :], None, xn_dram,
                                             bass.IndirectOffsetOnAxis(dst_ci[:, t:t + 1], 0)).then_inc(got[t % 3], 16)
                        if t:
                            put_missed(t - 1)
                    put_missed(ET - 1)

            @block.sync
            def _(e):
                with if_missed(e):
                    for t in range(ET - N_ACC, ET):
                        wait_added(e, t)


        t_xs0 = dma("sp", "xs0", xs_dram.rearrange("(p r) d -> p (r d)", p=P).rearrange("p (a b) -> p a b", b=512),
                    zeros.unsqueeze(1).broadcast_to((P, XS_ROWS * D // P // 512, 512)))

        quat = [[(0, 1), (1, 1), (2, 1), (3, 1)], [(1, -1), (0, 1), (3, 1), (2, -1)],
                [(2, -1), (3, -1), (0, 1), (1, 1)], [(3, -1), (2, 1), (1, -1), (0, 1)]]
        Q4 = D // 4
        hraw = qT.rearrange("p a b -> p (a b)")
        for i, wd in enumerate((w_gnn1, w_gnn2)):
            for half in range(2):
                t_hr = dma("sp", "hraw", hraw[half * Q4:(half + 1) * Q4, i * D:(i + 1) * D], wd, *t_mix_done)
        for i in range(2):
            for a in range(4):
                for b in range(4):
                    comp, sign = quat[a][b]
                    r = slice((a % 2) * Q4, (a % 2 + 1) * Q4)
                    t_H = run("dve", "ham", lambda e, i=i, a=a, b=b, r=r, comp=comp, sign=sign: e.tensor_scalar(
                        Hm[i][r, a // 2, b * Q4:(b + 1) * Q4], hraw[r, i * D + comp * Q4:i * D + (comp + 1) * Q4],
                        float(sign), None, ALU.mult), t_hr, *t_ring_done)

        third.again()
        out1T = third(KC, NP_)
        newT = xnT
        third_free = [t_dci, *all_put]
        work.again()
        work(tmp_at)
        accs = work(2, N_ACC, 2 * D)
        bst = work(KC, NCH, 6)
        bmv = work(KC, 2)
        bsc = work(KC)
        bbi = work(KC)
        assert 2 * N_ACC * 2 * D <= 5 * 2 * D + 2 * D + 64 + KC * CH
        pairs = -(-NT // 2)
        t_newT, t_accp, t_o1 = {}, {}, []
        for u in range(pairs):
            n = min(2, NT - 2 * u)
            for i in range(N_ACC):
                t_load = dma("sp", f"accl{u % 2}", accs[:, u % 2, i, 0:n * D].rearrange("p (t d) -> p t d", d=D),
                             acc_dram[i][2 * u * P:(2 * u + n) * P, :].rearrange("(t p) d -> p t d", p=P),
                             *third_free, *t_mix_done, *([t_accp[u - 2]] if u >= 2 else [t_H]))
            k = run("dve", "accs", lambda e: e.tensor_tensor(
                accs[:, u % 2, 0:2, 0:n * D], accs[:, u % 2, 0:2, 0:n * D], accs[:, u % 2, 2:4, 0:n * D], ALU.add), t_load)
            k = run("dve", "accs", lambda e: e.tensor_tensor(
                accs[:, u % 2, 0, 0:n * D], accs[:, u % 2, 0, 0:n * D], accs[:, u % 2, 1, 0:n * D], ALU.add), k)
            for t in range(2 * u, 2 * u + n):
                ps = bank[t % 4][:, 0:2 * P]
                at = (t % 2) * D
                for q in range(KC):
                    t_accp[u] = run("pe", "newp", lambda e: e.transpose(
                        ps[:, q * P:(q + 1) * P], accs[:, u % 2, 0, at + q * P:at + (q + 1) * P], ident), k,
                        *([t_newT[t - 4]] if t >= 4 else []))
                t_newT[t] = run("act", "newT", lambda e: e.activation(
                    newT[:, :, t * P:(t + 1) * P], ps.rearrange("p (k n) -> p k n", k=KC), ACT.Copy), t_accp[u])
                if t % 4 != 3 and t != NT - 1:
                    continue
                c = t // 4
                lo, hi = c * CH, min((c + 1) * CH, NP_)
                w, v = hi - lo, min(hi, N) - lo
                for m in range(KC):
                    ps = bank[4 + (2 * c + m) % 4]
                    for q in range(KC):
                        p_ = run("pe", "o1p", lambda e: e.matmul(
                            ps[:, 0:w], Hm[0][:, q, m * P:(m + 1) * P], newT[:, q, lo:hi],
                            start=(q == 0), stop=(q == KC - 1)), t_newT[t], t_H, *([t_o1[-4]] if len(t_o1) >= 4 else []))
                    ka = run("act", "o1", lambda e: e.activation(out1T[:, m, lo:hi], ps[:, 0:w], ACT.Copy), p_)
                    t_o1.append(ka)
                    kb = run("dve", "bst", lambda e: e.bn_stats(bst[:, m, c, :], out1T[:, m, lo:lo + v]), ka)
        for m in range(KC):
            k = run("dve", "bst", lambda e, m=m: e.bn_aggr(bmv[:, m, :], bst[:, m].rearrange("p a b -> p (a b)")), kb)
        k = run("dve", "bst", lambda e: e.tensor_scalar(bsc, bmv[:, :, 1], EPS, None, ALU.add), k)
        k = run("act", "bsq", lambda e: e.activation(bsc, bsc, ACT.Sqrt), k)
        k = run("dve", "bst", lambda e: e.reciprocal(bsc, bsc), k)
        k = run("dve", "bst", lambda e: e.tensor_tensor(bsc, bsc, cols[:, 2, :], ALU.mult), k)
        k = run("dve", "bst", lambda e: e.scalar_tensor_tensor(
            out=bbi, in0=bmv[:, :, 0], scalar=-1.0, in1=bsc, op0=ALU.mult, op1=ALU.mult), k)
        t_bn = run("dve", "bst", lambda e: e.tensor_tensor(bbi, bbi, cols[:, 3, :], ALU.add), k)

        turned.again()
        Xh = turned(NT, D)
        work.again()
        work(tmp_at)
        Wr = work(KC, NX)
        brow = work(NX)
        L = work(NT, NX)
        zT = work(2, KC, P)
        top = work(NT, 8)
        topi = work(NT, 8, dtype=U32)
        oh1 = work(NT, NX)
        oh2 = work(NT, NX)
        ohs = work(NT, NX)
        place = work(NT, NX)
        cnt = work(NT, NX)
        prob = work(NT, 2)
        psum_ = work(NT)
        wts = work(NT, 2)
        idf = work(NT, 2)
        posf = work(NT, 2)
        pos_i = work(NT, 2, dtype=I32)
        tot = work(NX)
        toti = work(NX, dtype=I32)
        endf = work(NX)
        base = work(NX)
        tile_start = work(MT)
        tcmp = work(MT, NX)
        tex = work(MT)
        tex_i = work(MT, dtype=I32)

        t_stage4 = [t_bn, p_, ka]
        t_th, t_x2, t_ps, t_st = {}, {}, {}, []
        for c in range(NCH):
            lo, hi = c * CH, min((c + 1) * CH, NP_)
            for m in range(KC):
                t_th[c] = run("act", "tanh", lambda e, m=m, lo=lo, hi=hi: e.activation(
                    out1T[:, m, lo:hi], out1T[:, m, lo:hi], ACT.Tanh, bias=bbi[:, m:m + 1], scale=bsc[:, m:m + 1]),
                    *t_stage4)
            for j in range((hi - lo) // P):
                t = 4 * c + j
                ps = bank[t % 4][:, 0:D]
                for q in range(KC):
                    p_ = run("pe", "o2p", lambda e, q=q, t=t, ps=ps: e.matmul(
                        ps, out1T[:, q, t * P:(t + 1) * P], Hm[1][:, q, :], start=(q == 0), stop=(q == KC - 1)),
                        t_th[c], *([t_x2[t - 4]] if t >= 4 else []))
                t_x2[t] = run("dve", "x2", lambda e, t=t, ps=ps: e.tensor_tensor(
                    X[:, t, :], X[:, t, :], ps, ALU.add), p_)
                dep_stats = [t_x2[t]]
                k = norm_stats(X[:, t, :], t)
        t_o2p = p_
        k = norm_rstd(0, NT, k)
        for t in range(NT):
            k2 = run("dve", "z", lambda e, t=t: e.tensor_scalar(
                Xh[:, t, :], X[:, t, :], mv[:, t, 0:1], rstd[:, t:t + 1], ALU.subtract, ALU.mult), k, t_o2p)
            t_ps[t] = k2
        t_rw = run("dve", "brz", lambda e: e.memset(brow, 0.0), t_o2p)
        dma("sp", "rw", brow[0:1, :], row_br.rearrange("(a n) -> a n", a=1), t_rw)
        t_rw = dma("sp", "rw", Wr, w_router.rearrange("(k p) n -> p k n", p=P))
        t_zT, t_lg = {}, {}
        for t in range(NT):
            ps = bank[t % 4][:, 0:2 * P]
            for q in range(KC):
                p_ = run("pe", "zp", lambda e, q=q, t=t, ps=ps: e.transpose(
                    ps[:, q * P:(q + 1) * P], Xh[:, t, q * P:(q + 1) * P], ident), t_ps[t],
                    *([t_zT[t - 4]] if t >= 4 else []))
            t_zT[t] = run("act", "zT", lambda e, t=t, ps=ps: e.activation(
                zT[:, t % 2], ps.rearrange("p (k n) -> p k n", k=KC), ACT.Copy), p_,
                *([t_lg[t - 2]] if t >= 2 else []))
            pl = bank[4][:, t * NX:(t + 1) * NX]
            for q in range(KC):
                run("pe", None, lambda e, q=q, t=t, pl=pl: e.matmul(
                    pl, zT[:, t % 2, q, :], Wr[:, q, :], start=(q == 0), stop=False), t_zT[t], t_rw)
            t_lg[t] = run("pe", "lg", lambda e, pl=pl: e.matmul(pl, ones[:, :], brow, start=False, stop=True))
        t_L = run("dve", "L", lambda e: e.tensor_copy(L.rearrange("p a b -> p (a b)"), bank[4][:, 0:NT * NX]),
                  t_lg[NT - 1])
        for t in range(NT):
            k = run("dve", "max", lambda e, t=t: e.max(top[:, t, :], L[:, t, :]), t_L)
            k = run("dve", "max", lambda e, t=t: e.max_index(topi[:, t, :], top[:, t, :], L[:, t, :]), k)
        t_max = k
        k = run("dve", "rt", lambda e: e.tensor_copy(idf, topi[:, :, 0:2]), t_max)
        t_oh = []
        for i, oh in enumerate((oh1, oh2)):
            t_oh.append(run("dve", "rt", lambda e, i=i, oh=oh: e.tensor_tensor(
                oh, iota8.unsqueeze(1).broadcast_to((P, NT, NX)),
                idf[:, :, i:i + 1].broadcast_to((P, NT, NX)), ALU.is_equal), k))
        k = run("dve", "rt", lambda e: e.tensor_tensor(ohs, oh1, oh2, ALU.add), *t_oh)
        flat = ohs.rearrange("p a b -> p (a b)")
        run("pe", None, lambda e: e.matmul(bank[5][:, 0:NT * NX], ones[:, :], flat, start=True, stop=True), k)
        p_ = run("pe", "rank", lambda e: e.matmul(bank[6][:, 0:NT * NX], before, flat, start=True, stop=True))
        k = run("dve", "rt", lambda e: e.tensor_copy(cnt.rearrange("p a b -> p (a b)"), bank[5][:, 0:NT * NX]), p_)
        for x_ in range(NX):
            k2 = run("dve", "rt", lambda e, x_=x_: e.tensor_tensor_scan(
                place[:, :, x_], ones[:, 0:NT], cnt[:, :, x_], 0.0, ALU.mult, ALU.add), k)
        k = run("dve", "rt", lambda e: e.tensor_scalar(toti, place[:, NT - 1, :], float(SLOTS - 1), None, ALU.add), k2)
        k = run("dve", "rt", lambda e: e.tensor_scalar(
            toti, toti, SLOTS.bit_length() - 1, None, ALU.logical_shift_right), k)
        k = run("dve", "rt", lambda e: e.tensor_scalar(tot, toti, float(SLOTS), None, ALU.mult), k)
        k = run("dve", "rt", lambda e: e.tensor_tensor_scan(endf, ones[:, 0:NX], tot, 0.0, ALU.mult, ALU.add), k)
        t_end = k
        k = run("dve", "rt", lambda e: e.tensor_tensor(base, endf, tot, ALU.subtract), k)
        k = run("dve", "rt", lambda e: e.tensor_tensor(place, place, cnt, ALU.subtract), k)
        k = run("dve", "rt", lambda e: e.tensor_tensor(
            place, place, bank[6][:, 0:NT * NX].rearrange("p (a b) -> p a b", b=NX), ALU.add), k)
        k = run("dve", "rt", lambda e: e.tensor_tensor(
            place, place, base.unsqueeze(1).broadcast_to((P, NT, NX)), ALU.add), k)
        for i, oh in enumerate((oh1, oh2)):
            kk = run("dve", "rt", lambda e, oh=oh: e.tensor_tensor(ohs, oh, place, ALU.mult), k, p_)
            k = run("dve", "rt", lambda e, i=i: e.tensor_reduce(posf[:, :, i], ohs, AX.X, ALU.add), kk)
        t_pos = run("dve", "rt", lambda e: e.tensor_copy(pos_i, posf), k)
        k = run("pool", "tst", lambda e: e.iota(tile_start, [[SLOTS, MT]], base=0, channel_multiplier=0,
                                                allow_small_or_imprecise_dtypes=True), t_end)
        k = run("dve", "rt", lambda e: e.tensor_tensor(
            tcmp, tile_start.unsqueeze(2).broadcast_to((P, MT, NX)),
            endf.unsqueeze(1).broadcast_to((P, MT, NX)), ALU.is_ge), k)
        k = run("dve", "rt", lambda e: e.tensor_reduce(tex, tcmp, AX.X, ALU.add), k)
        t_tex = run("dve", "rt", lambda e: e.tensor_scalar(tex_i, tex, float(NX - 1), None, ALU.min), k)
        for t in range(NT):
            dep_stats = [t_zT[NT - 1]]
            k = norm_stats(Xh[:, t, :], t)
        k = norm_rstd(0, NT, k)
        t_xs = []
        for t in range(NT):
            k2 = run("dve", "xh", lambda e, t=t: e.tensor_scalar(
                Xh[:, t, :], Xh[:, t, :], mv[:, t, 0:1], rstd[:, t:t + 1], ALU.subtract, ALU.mult), k)
            for i in range(2):
                t_xs.append(run("pool", "xs", lambda e, t=t, i=i: e.indirect_dma_start(
                    xs_dram, bass.IndirectOffsetOnAxis(pos_i[:, t, i:i + 1], 0), Xh[:, t, :], None),
                    k2, t_pos, t_xs0, by=16))
        k = run("dve", "sm", lambda e: e.tensor_tensor(
            L, L, top[:, :, 0:1].broadcast_to((P, NT, NX)), ALU.subtract), t_max)
        k = run("dve", "sm", lambda e: e.tensor_tensor(
            prob, top[:, :, 0:2], top[:, :, 0:1].broadcast_to((P, NT, 2)), ALU.subtract), k)
        run("act", None, lambda e: e.activation(L, L, ACT.Exp), k)
        k = run("act", "sma", lambda e: e.activation(prob, prob, ACT.Exp))
        k = run("dve", "sm", lambda e: e.tensor_reduce(psum_, L, AX.X, ALU.add), k)
        k = run("dve", "sm", lambda e: e.reciprocal(psum_, psum_), k)
        k = run("dve", "sm", lambda e: e.tensor_tensor(
            prob, prob, psum_.unsqueeze(2).broadcast_to((P, NT, 2)), ALU.mult), k)
        k = run("dve", "sm", lambda e: e.tensor_tensor(psum_, prob[:, :, 0], prob[:, :, 1], ALU.add), k)
        k = run("dve", "sm", lambda e: e.reciprocal(psum_, psum_), k)
        t_wts = run("dve", "sm", lambda e: e.tensor_tensor(
            wts, prob, psum_.unsqueeze(2).broadcast_to((P, NT, 2)), ALU.mult), k)

        third.again()
        W1 = third(2, KC, H)
        W2 = third(2, HC, D)
        ecol = third(2, 2 * KC + HC)
        erow = third(2, D)
        xe = third(2, 2, D)
        xeT = third(2, KC, SLOTS)
        turned_free = t_xs[-1]
        turned.again()
        hT = turned(2, HC, SLOTS)
        yb = turned(2, 2, D)
        t_er = run("dve", "erz", lambda e: e.memset(erow, 0.0), t_o2p)
        t_l1, t_l2, t_wl, t_xl, t_y, t_ys, t_xT, t_g = {}, {}, {}, {}, {}, {}, {}, {}
        t_xp, t_hb, t_yb = {}, {}, {}

        def weights(i):
            b = i % 2
            free = [t_l2[i - 2]] if i >= 2 else [t_o2p, t_er]
            wait("sp", *free, t_tex)
            name = f"wl{b}"

            wait("sp", turned_free)
            x_ = nc.sync.value_load(tex_i[0:1, i:i + 1], min_val=0, max_val=NX - 1)
            dma("sp", name, W1[:, b], w_up[bass.ds(x_, 1), :, :].rearrange("a (k p) n -> p (a k) n", p=P))
            dma("sp", name, W2[:, b], w_down[bass.ds(x_, 1), :, :].rearrange("a (k p) n -> p (a k) n", p=P))
            dma("sp", name, ecol[:, b, :], cols_expert[bass.ds(x_, 1), :, :].rearrange("a p n -> (a p) n"))
            dma("sp", name, erow[0:1, b, :], row_be[bass.ds(x_, 1), :])
            dma("sp", name, xe[:, b], xs_dram[i * SLOTS:(i + 1) * SLOTS, :].rearrange("(c p) d -> p c d", p=P))
            t_wl[i] = (name, pr.count[name])

        weights(0)
        for i in range(MT):
            b = i % 2
            if i + 1 < MT:
                weights(i + 1)
            for q in range(KC):
                ps = bank[q][:, 0:SLOTS]
                for c in range(2):
                    p_ = run("pe", "xeT", lambda e, q=q, c=c, ps=ps, b=b: e.transpose(
                        ps[:, c * P:(c + 1) * P], xe[:, b, c, q * P:(q + 1) * P], ident), t_wl[i], t_L,
                        *([t_xT[i - 1]] if i else []))
                k = run("dve", "xeTd", lambda e, q=q, ps=ps, b=b: e.tensor_scalar(
                    xeT[:, b, q, :], ps, ecol[:, b, q:q + 1], ecol[:, b, KC + q:KC + q + 1], ALU.mult, ALU.add), p_,
                    *([t_l1[i - 2]] if i >= 2 else []))
            t_xT[i] = k
            for h in range(HC):
                ps = bank[2 + h % 4][:, 0:SLOTS]
                n = i * HC + h
                for q in range(KC):
                    p_ = run("pe", "l1", lambda e, q=q, h=h, ps=ps, b=b: e.matmul(
                        ps, W1[:, b, q, h * P:(h + 1) * P], xeT[:, b, q, :], start=(q == 0), stop=(q == KC - 1)),
                        t_xT[i], t_pos, *([t_g[n - 4]] if n >= 4 else []))
                t_g[n] = run("act", "g", lambda e, h=h, ps=ps, b=b: e.activation(
                    hT[:, b, h, :], ps, ACT.Gelu, bias=ecol[:, b, 2 * KC + h:2 * KC + h + 1]), p_,
                    *([t_l2[i - 2]] if i >= 2 else [turned_free]))
            t_l1[i] = p_
            for c in range(2):
                ps = bank[6 + c][:, 0:D]
                for h in range(HC):
                    run("pe", None, lambda e, h=h, c=c, ps=ps, b=b: e.matmul(
                        ps, hT[:, b, h, c * P:(c + 1) * P], W2[:, b, h, :], start=(h == 0), stop=False),
                        t_g[i * HC + h], *([t_y[i - 1, c]] if i else []))
                p_ = run("pe", "l2", lambda e, ps=ps, b=b: e.matmul(ps, ones[:, :], erow[:, b, :], start=False, stop=True))
                t_y[i, c] = run("dve", "y", lambda e, c=c, ps=ps, b=b: e.tensor_copy(yb[:, b, c, :], ps), p_,
                                *([t_ys[i - 2]] if i >= 2 else []), turned_free)
            t_l2[i] = p_
            t_ys[i] = dma("act", f"ys{b}", y_dram[i * SLOTS:(i + 1) * SLOTS, :].rearrange("(c p) d -> p c d", p=P),
                          yb[:, b], t_y[i, 1])

        turned.again()
        turned(4 * D + 2 * HC * SLOTS)
        yg = turned(4, 2, D)
        t_c, t_o = {}, {}
        for t in range(NT):
            s = t % 4
            for i in range(2):
                k = run("pool", f"yg{s}", lambda e, t=t, i=i, s=s: e.indirect_dma_start(
                    yg[:, s, i, :], None, y_dram, bass.IndirectOffsetOnAxis(pos_i[:, t, i:i + 1], 0)),
                    t_ys[MT - 1], t_ys[MT - 2], *([t_c[t - 4]] if t >= 4 else []), by=16)
            for i in range(2):
                k = run("dve", "fin", lambda e, t=t, i=i, s=s: e.scalar_tensor_tensor(
                    out=X[:, t, :], in0=yg[:, s, i, :], scalar=wts[:, t, i:i + 1], in1=X[:, t, :],
                    op0=ALU.mult, op1=ALU.add), k, t_wts)
            t_c[t] = k
            rows = TAIL if t == NT - 1 else P
            k = dma("sp", "out", out[t * P:t * P + rows, :], X[0:rows, t, :], k)
        wait("sp", k)


def kernel(x, src, dst, edge_weight, L0_gnn_weight1, L0_gnn_weight2, L0_gnn_gamma, L0_gnn_beta, L0_mix_w_qkv,
           L0_mix_b_qkv, L0_mix_kln_g, L0_mix_kln_b, L0_mix_vln_g, L0_mix_vln_b, L0_mix_w1, L0_mix_b1, L0_mix_w2,
           L0_mix_b2, L0_ffn_Wr, L0_ffn_br, L0_ffn_ln_g, L0_ffn_ln_b, L0_ffn_W1, L0_ffn_b1, L0_ffn_W2, L0_ffn_b2):
    import numpy as np
    import concourse.bacc as bacc
    from concourse.bass_utils import run_bass_kernel_spmd

    D, heads = 256, 8
    hd = D // heads

    def col(v):
        return np.asarray(v).reshape(-1, P).T
    bq3 = np.asarray(L0_mix_b_qkv).reshape(heads, 3, hd)
    NX = L0_ffn_W1.shape[0]
    arrays = {
        "x": x, "src": src, "dst": dst, "ew": edge_weight, "w_gnn1": L0_gnn_weight1, "w_gnn2": L0_gnn_weight2,
        "w_qkv": np.asarray(L0_mix_w_qkv).reshape(D, heads, 3, hd).transpose(0, 2, 1, 3).reshape(D, 3 * D),
        "row_bkv": bq3[:, 1:].transpose(1, 0, 2).reshape(2 * D),
        "kv_ln": np.concatenate([np.asarray(v) for v in (L0_mix_kln_g, L0_mix_vln_g, L0_mix_kln_b, L0_mix_vln_b)]),
        "w_mix1": L0_mix_w1, "w_mix2": L0_mix_w2,
        "cols_mix": np.concatenate([col(bq3[:, 0].reshape(D)), col(L0_mix_b1), col(L0_gnn_gamma), col(L0_gnn_beta)], 1),
        "row_b2": L0_mix_b2, "w_router": L0_ffn_Wr, "row_br": L0_ffn_br, "w_up": L0_ffn_W1, "w_down": L0_ffn_W2,
        "cols_expert": np.concatenate([np.asarray(v).reshape(NX, -1, P).transpose(0, 2, 1)
                                       for v in (L0_ffn_ln_g, L0_ffn_ln_b, L0_ffn_b1)], 2),
        "row_be": L0_ffn_b2,
    }
    arrays = {f"in_{n}": np.ascontiguousarray(a) for n, a in arrays.items()}
    nc = bacc.Bacc("TRN2", target_bir_lowering=False, num_devices=1)
    args = [nc.dram_tensor(n, a.shape, mybir.dt.from_np(a.dtype), kind="ExternalInput").ap() for n, a in arrays.items()]
    out = nc.dram_tensor("out", tuple(x.shape), F32, kind="ExternalOutput").ap()
    gps_layer(nc, *args, out)
    r = run_bass_kernel_spmd(nc, [arrays], core_ids=[0])
    return r.results[0]["out"]
```

```python
from contextlib import ExitStack

import concourse.bass as bass
from concourse import mybir

P = 128
ALU = mybir.AluOpType
ACT = mybir.ActivationFunctionType
F32 = mybir.dt.float32
F32R = mybir.dt.float32r
BF16 = mybir.dt.bfloat16
I32 = mybir.dt.int32
U32 = mybir.dt.uint32
AX = mybir.AxisListType
EPS = 1e-5
N_ACC = 4
QUAD = 4
MIX_FIRST = 10
MIX_KV = 1.8
MIX_DENSE = 1.05
FILLS = 1
EARLY = 12
S_QUADS = 3
SLOTS = 256


class Program:

    def __init__(self, nc, ctx):
        self.nc, self.ctx = nc, ctx
        self.sems, self.count, self.seen = {}, {}, {}
        self.engines = {"sp": nc.sync, "act": nc.scalar, "pool": nc.gpsimd, "dve": nc.vector, "pe": nc.tensor}

    def sem(self, name):
        if name not in self.sems:
            self.sems[name] = self.ctx.enter_context(self.nc.semaphore("s_" + name))
            self.count[name] = 0
        return self.sems[name]

    def wait(self, engine, *tokens):
        for name, value in tokens:
            if self.seen.get((engine, name), 0) < value:
                self.seen[engine, name] = value
                self.engines[engine].wait_ge(self.sems[name], value)

    def run(self, engine, done, step, *after, by=1):
        self.wait(engine, *after)
        instruction = step(self.engines[engine])
        if done is None:
            return None
        instruction.then_inc(self.sem(done), by)
        self.count[done] += by
        return (done, self.count[done])

    def dma(self, engine, done, out, in_, *after):
        return self.run(engine, done, lambda e: e.dma_start(out, in_), *after, by=16)


def gps_layer(nc, x, src, dst, ew, w_gnn1, w_gnn2, w_qkv, row_bkv, kv_ln, w_mix1, w_mix2, cols_mix,
              row_b2, w_router, row_br, w_up, w_down, cols_expert, row_be, out):
    N, D = x.shape
    E = src.shape[0]
    NX, _, H = w_up.shape
    NT = -(-N // P)
    NP_ = NT * P
    TAIL = N - (NT - 1) * P
    ET = -(-E // P)
    EG = -(-ET // P)
    E_TAIL = E - (ET - 1) * P
    KC = D // P
    HC = H // P
    HD = D // 8
    CH = 512
    NCH = -(-NP_ // CH)
    TRASH = NP_
    ACC_ROWS = NP_ + P
    MT = (NP_ * 2 + NX * (SLOTS - 1)) // SLOTS
    LISTS = MT * SLOTS // P
    DX = D + 4
    CT = 7
    NQ = -(-ET // QUAD)
    assert ACC_ROWS * D // P // 512 % 5 == 0
    assert ET % 2 == 0 and NT % CT == 0 and D == 2 * P and TRASH % 64 == 0 and LISTS <= P

    xn_dram = nc.dram_tensor("xn_dram", (NP_, D), F32, kind="Internal").ap()
    acc_dram = [nc.dram_tensor(f"acc{i}_dram", (ACC_ROWS, D), F32, kind="Internal").ap() for i in range(N_ACC)]
    xh_dram = nc.dram_tensor("xh_dram", (ACC_ROWS, DX), F32, kind="Internal").ap()
    sum_dram = nc.dram_tensor("sum_dram", (ACC_ROWS, D), F32, kind="Internal").ap()

    with ExitStack() as ctx:
        pr = Program(nc, ctx)
        run, wait, dma = pr.run, pr.wait, pr.dma

        late = ctx.enter_context(ExitStack())

        def region(name, words, stack=ctx):
            t = stack.enter_context(nc.sbuf_tensor(name, [P, words], F32))
            at = [0]

            def carve(*shape, dtype=F32):
                n = 1
                for s in shape:
                    n *= s
                ap = t[:, at[0]:at[0] + n]
                at[0] += n
                assert at[0] <= words, (name, at[0], words)
                if dtype != F32:
                    ap = ap.bitcast(dtype)
                if len(shape) == 2:
                    ap = ap.rearrange("p (a b) -> p a b", a=shape[0])
                if len(shape) == 3:
                    ap = ap.rearrange("p (a b c) -> p a b c", a=shape[0], b=shape[1])
                return ap

            def again():
                at[0] = 0
            carve.again = again
            return carve

        bank = [ctx.enter_context(nc.psum_tensor(f"bank{i}", [P, 512], F32)) for i in range(8)]

        fixed = region("fixed", 4 * P + 512 + 8 * KC + 16 + 4 + 3 * P // 2)
        ident = fixed(P)
        before = fixed(P)
        after_ = fixed(P)
        zeros = fixed(512)
        cols = fixed(8, KC)
        iota8 = fixed(8)
        iota_p = fixed(P)
        missed = fixed(1)
        missed_i = fixed(1, dtype=I32)
        ident_b = fixed(P // 2).bitcast(BF16)
        ones_b = fixed(P // 2).bitcast(BF16)
        trash_col = fixed(1)
        eps_col = fixed(1)
        ones = ctx.enter_context(nc.sbuf_tensor("ones", [P, P], F32))

        node = region("node", NT * D)
        X = node(NT, D)
        turned = region("turned", NT * D)
        xnT = turned(KC, NP_)

        small = region("small", 10 * NT + LISTS + 2 * MT)
        stats = small(NT, 6)
        mv = small(NT, 2)
        rstd = small(NT)
        ve = small(NT)
        slot_i = small(LISTS, dtype=I32)
        tex = small(MT)
        tex_i = small(MT, dtype=I32)

        third = region("third", NT * D, late)
        work = region("work", 12992, late)

        src_hi = third(EG * P // 2).bitcast(BF16).rearrange("p (a b) -> p a b", a=EG)
        src_lo = third(EG * P // 2).bitcast(BF16).rearrange("p (a b) -> p a b", a=EG)
        src_c = third(EG * P)
        w_c = third(EG * P)
        trash_minus = third(EG * P)
        dup = third(EG * P)
        put_i = third(EG * P, dtype=I32)
        dst_rel = third(EG * P)
        tables_end = 7 * EG * P
        S = third(S_QUADS * QUAD, P)
        OH = third(2 * QUAD, P)
        B = third(2 * QUAD, P)
        M = third(2 * QUAD, D)
        unread = third(QUAD * P // 2).bitcast(BF16).rearrange("p (a b) -> p a b", a=QUAD)
        third.again()
        third(tables_end)
        raw_src = third(EG, P, dtype=I32)
        raw_dst = third(EG, P, dtype=I32)
        raw_w = third(EG, P)
        src_f = third(EG, P)
        dst_f = third(EG, P)

        Wqkv = work(KC, 3 * D)
        Wm1 = work(KC, D)
        Wm2 = work(KC, D)
        bkv = work(2 * D)
        b2row = work(D)
        kvln = work(2, 2, HD)
        KV = work(KC, P)
        Hm = [work(KC, D), work(KC, D)]
        tmp_at = KC * (3 * D + 2 * D + P + 2 * D) + 2 * D + D + 4 * HD
        xn_ring = work(2, CT, D)
        raw_dstq = work(2, QUAD * P, dtype=I32)
        diag = work(2, P)
        least = work(2)
        base_row = work(2 * P)
        dst_c = work(EG * P)
        assert QUAD * P == 512
        work.again()
        work(tmp_at)
        kvs = work(2, 2 * D)
        kvd = work(2 * D)
        kvq = work(2 * D)
        kvn = work(2, 2 * D)
        ksum = work(16)
        kvar = work(16)
        kve = work(16)
        krs = work(16)
        qT = work(KC, CH)
        ret = work(KC, CH)
        hT_mix = work(KC, CH)
        base_i = work(2 * P, dtype=I32)
        win = work(3, D)
        bkv_b = work(D).bitcast(BF16)
        b2_b = work(D // 2).bitcast(BF16)

        def iota_mask(ap, op, base, cm, step):
            def f(e):
                return e.affine_select(out=ap, in_=ones[:, :], compare_op=op, fill=0.0, base=base,
                                       pattern=[[step, P]], channel_multiplier=cm)
            return f
        t_ones = run("dve", "ones", lambda e: e.memset(ones[:, :], 1.0))
        t_zero = run("dve", "zeros", lambda e: e.memset(zeros, 0.0))
        run("pool", "masks", iota_mask(ident, ALU.is_equal, 0, 1, -1), t_ones)
        run("pool", "masks", iota_mask(before, ALU.is_gt, 0, -1, 1))
        t_mask = run("pool", "masks", iota_mask(after_, ALU.is_gt, 0, 1, -1))
        run("pool", "masks", lambda e: e.iota(trash_col, [[0, 1]], base=TRASH, channel_multiplier=1,
                                              allow_small_or_imprecise_dtypes=True))
        t_iota = run("pool", "masks", lambda e: e.iota(iota8, [[1, 8]], base=0, channel_multiplier=0,
                                                       allow_small_or_imprecise_dtypes=True))
        t_iota = run("pool", "masks", lambda e: e.iota(iota_p, [[1, P]], base=0, channel_multiplier=0,
                                                       allow_small_or_imprecise_dtypes=True))
        run("dve", "identb", lambda e: e.tensor_copy(ident_b, ident), t_mask)
        t_identb = run("dve", "identb", lambda e: e.memset(ones_b, 1.0))
        t_identb = run("dve", "identb", lambda e: e.memset(eps_col, EPS))

        xt = x[0:(NT - 1) * P, :].rearrange("(t p) d -> p t d", p=P)
        t_xpad = run("dve", "xpad", lambda e: e.memset(X[:, NT - 1, :], 0.0))
        t_x = []
        for c in range(NT // CT):
            n = CT if (c + 1) * CT < NT else CT - 1
            t_x.append(dma("sp", f"x{c}", X[:, c * CT:c * CT + n, :], xt[:, c * CT:c * CT + n, :]))
        t_x[-1] = dma("sp", f"x{NT // CT - 1}", X[0:TAIL, NT - 1, :], x[(NT - 1) * P:N, :], t_xpad)

        full = (ET - 1) // P
        last_rows = ET - 1 - full * P
        e_full = full * P * P

        pads = []
        for ap, v in ((raw_src, NP_ - 1), (raw_dst, N - 1), (raw_w, 0.0)):
            pads.append(run("dve", "epad", lambda e, ap=ap, v=v: e.memset(ap[:, full, :], v)))
        for ap, dram in ((raw_src, src), (raw_dst, dst), (raw_w, ew)):
            d3 = dram[0:e_full].rearrange("(g t j) -> t g j", t=P, j=P)
            dma("act", "edges", ap[:, 0:full, :], d3)
            dma("act", "edges", ap[0:last_rows, full, :],
                dram[e_full:e_full + last_rows * P].rearrange("(t j) -> t j", j=P), pads[-1])
            t_edges = dma("act", "edges", ap[last_rows:last_rows + 1, full, 0:E_TAIL],
                          dram[E - E_TAIL:E].rearrange("(t j) -> t j", t=1))

        QE = QUAD * P
        q_full = E // QE
        k = run("dve", "epad", lambda e: e.memset(raw_dstq[:, 1, :], N - 1))
        dma("act", "edges", raw_dstq[:, 0, :], dst[0:P * QE].rearrange("(q j) -> q j", j=QE))
        dma("act", "edges", raw_dstq[0:q_full - P, 1, :], dst[P * QE:q_full * QE].rearrange("(q j) -> q j", j=QE), k)
        t_edges = dma("act", "edges", raw_dstq[q_full - P:q_full - P + 1, 1, 0:E - q_full * QE],
                      dst[q_full * QE:E].rearrange("(q j) -> q j", q=1))

        t_wz = run("dve", "wz", lambda e: e.memset(bkv, 0.0))
        t_wz = run("dve", "wz", lambda e: e.memset(b2row, 0.0))
        dma("act", "w", Wqkv, w_qkv.rearrange("(k p) n -> p k n", p=P))
        dma("act", "w", Wm1, w_mix1.rearrange("(k p) n -> p k n", p=P))
        dma("act", "w", Wm2, w_mix2.rearrange("(k p) n -> p k n", p=P))
        dma("act", "w", bkv[0:3, :], row_bkv.partition_broadcast(3), t_wz)
        dma("act", "w", b2row[0:3, :], row_b2.partition_broadcast(3))
        dma("act", "w", kvln.rearrange("p a b c -> p (a b c)"), kv_ln.partition_broadcast(P))
        t_w = dma("act", "w", cols[:, 0:4, :].rearrange("p a b -> p (a b)"), cols_mix)

        def row_stats(t_in, t, *after):
            return run("dve", "st", lambda e: e.bn_stats(stats[:, t, :], t_in), *after)

        def row_aggregate(t, after):
            return run("dve", "st", lambda e: e.bn_aggr(mv[:, t, :], stats[:, t, :]), after)

        def norm_root(a, b, after):
            k = run("dve", "rstd", lambda e: e.tensor_scalar(ve[:, a:b], mv[:, a:b, 1], EPS, None, ALU.add), after)
            return run("act", "rstd_a", lambda e: e.activation(ve[:, a:b], ve[:, a:b], ACT.Sqrt), k)

        def norm_inverse(a, b, after):
            return run("dve", "rstd", lambda e: e.reciprocal(rstd[:, a:b], ve[:, a:b]), after)

        def norm_rstd(a, b, after):
            return norm_inverse(a, b, norm_root(a, b, after))

        PIECE = ACC_ROWS * D // P // 512 // 5
        fills = [(i, j) for i in range(N_ACC) for j in range(5)]
        t_acc0 = {}

        def fill():
            i, j = fills.pop(0)
            rows = acc_dram[i].rearrange("(p r) d -> p (r d)", p=P).rearrange("p (a b) -> p a b", b=512)
            t_acc0[i] = dma("sp", f"acc0_{i}", rows[:, j * PIECE:(j + 1) * PIECE, :],
                            zeros.unsqueeze(1).broadcast_to((P, PIECE, 512)), t_zero)

        t_xnT, t_xnd = [], []
        ring_free = [[], []]
        for c in range(NT // CT):
            a, b = c * CT, (c + 1) * CT
            t_part = [row_stats(X[:, t, :], t, t_x[c]) for t in range(a, b)]
            for t in range(a, b):
                k = row_aggregate(t, t_part[t - a])
            k0 = norm_rstd(a, b, k)
            ring = xn_ring[:, c % 2]
            for t in range(a, b):
                i = t - a
                k = run("dve", "xn", lambda e, t=t, i=i, ring=ring: e.tensor_scalar(
                    ring[:, i, :], X[:, t, :], mv[:, t, 0:1], rstd[:, t:t + 1], ALU.subtract, ALU.mult),
                    k0, *ring_free[c % 2])
                s = t % 4
                ps = bank[4 + s][:, 0:2 * P]
                free = [t_xnT[t - 4]] if t >= 4 else []
                for q in range(KC):
                    p_ = run("pe", "xnT_pe", lambda e, q=q, ps=ps, ring=ring, i=i: e.transpose(
                        ps[:, q * P:(q + 1) * P], ring[:, i, q * P:(q + 1) * P], ident), k, t_mask, *free)
                t_xnT.append(run("act", "xnT", lambda e, ps=ps, t=t: e.activation(
                    xnT[:, :, t * P:(t + 1) * P], ps.rearrange("p (k n) -> p k n", k=KC), ACT.Copy), p_))
            d = dma("sp", f"xnd{c % 2}", xn_dram[a * P:b * P, :].rearrange("(t p) d -> p t d", p=P), ring, k)
            t_xplus = run("pool", "xplus", lambda e: e.tensor_tensor(
                X[:, a:b, :], X[:, a:b, :], ring, ALU.add), k)
            ring_free[c % 2] = [d, p_, t_xplus]
            for _ in range(FILLS if c >= 1 else 0):
                fill()
        t_xnd = [ring_free[0][0], ring_free[1][0]]
        t_ring_done = ring_free[0] + ring_free[1]

        while fills:
            fill()

        tmp_i = dst_f.bitcast(I32)
        k = run("dve", "etab", lambda e: e.tensor_scalar(
            tmp_i, raw_src, 6, 6, ALU.logical_shift_right, ALU.logical_shift_left), t_edges)
        k = run("dve", "etab", lambda e: e.tensor_copy(src_hi, tmp_i), k)
        k = run("dve", "etab", lambda e: e.tensor_scalar(tmp_i, raw_src, 63, None, ALU.bitwise_and), k)
        k = run("dve", "etab", lambda e: e.tensor_copy(src_lo, tmp_i), k)
        run("dve", "etab", lambda e: e.tensor_copy(src_f, raw_src))
        k = run("dve", "etab", lambda e: e.tensor_copy(dst_f, raw_dst), k)
        t_split = k
        k = run("dve", "etab", lambda e: e.tensor_reduce(least, raw_dstq, AX.X, ALU.min), k)
        k = run("dve", "etab", lambda e: e.tensor_scalar(least, least, float(NP_ - P), None, ALU.min), k)
        for h in range(2):
            k2 = run("dve", "etab", lambda e: e.tensor_scalar(
                diag[:, h, :], ident, least[:, h:h + 1], None, ALU.mult), k, t_mask)
        p_ = run("pe", "etab_pe", lambda e: e.matmul(
            bank[2][:, 0:2 * P], ones[:, :], diag.rearrange("p a b -> p (a b)"), start=True, stop=True), k2)
        run("dve", "etab", lambda e: e.tensor_copy(base_row, bank[2][:, 0:2 * P]), p_)
        t_base = run("dve", "etab", lambda e: e.tensor_copy(base_i, bank[2][:, 0:2 * P]))
        evac = {}
        for n, (rows, col) in enumerate(((src_f, src_c), (raw_w, w_c), (dst_f, dst_c))):
            for h in range(2):
                g0, g1 = (0, 4) if h == 0 else (4, EG)
                use = 2 * n + h
                ps = bank[use % 2]
                for g in range(g0, g1):
                    p_ = run("pe", "etab_pe", lambda e: e.transpose(
                        ps[:, (g - g0) * P:(g - g0 + 1) * P], rows[:, g, :], ident), t_split, t_edges,
                        *([evac[use - 2]] if use >= 2 else []))
                evac[use] = run("dve", "etab", lambda e: e.tensor_copy(col[:, g0 * P:g1 * P], ps[:, 0:(g1 - g0) * P]), p_)
        t_cols = evac[5]
        run("dve", "etab", lambda e: e.tensor_scalar(trash_minus, src_c, -1.0, trash_col, ALU.mult, ALU.add),
            t_cols, t_iota)
        t_tables = run("dve", "etab", lambda e: e.tensor_tensor(
            dst_rel.rearrange("p (q j) -> p q j", j=QUAD), dst_c.rearrange("p (q j) -> p q j", j=QUAD),
            base_row[:, 0:EG * P // QUAD].unsqueeze(2).broadcast_to((P, EG * P // QUAD, QUAD)), ALU.subtract), t_base)

        tmp_c = S.rearrange("p a b -> p (a b)")[:, 0:EG * P]
        k = run("dve", "miss", lambda e: e.tensor_scalar(tmp_c, dst_rel, float(P), None, ALU.is_ge), t_tables)
        k = run("dve", "miss", lambda e: e.scalar_tensor_tensor(
            out=tmp_c, in0=dst_rel, scalar=0.0, in1=tmp_c, op0=ALU.is_lt, op1=ALU.add), k)
        k = run("dve", "miss", lambda e: e.tensor_reduce(missed, tmp_c[:, 0:ET], AX.X, ALU.add), k)
        p_ = run("pe", "missp", lambda e: e.matmul(bank[2][:, 0:1], ones[:, :], missed, start=True, stop=True), k, t_base)
        t_miss = run("dve", "miss", lambda e: e.tensor_copy(missed_i, bank[2][:, 0:1]), p_)
        t_tables = t_miss

        t_sel, t_dup, t_oh, t_idx, t_bt, t_Bs, t_sum, t_row, t_put, t_win = ({} for _ in range(10))

        def tiles(q):
            return range(q * QUAD, min((q + 1) * QUAD, ET))

        def spread(q, dep=()):
            for t in tiles(q):
                ps = bank[q % 2][:, (t % QUAD) * P:(t % QUAD + 1) * P]
                row = ident_b[:, t % P:t % P + 1].broadcast_to((P, P))
                run("pe", None, lambda e: e.matmul(ps, row, src_hi[:, t // P, :], start=True, stop=False),
                    t_tables, t_identb, *([t_sel[q - 2]] if q >= 2 else []), *dep)
                k = run("pe", "spread", lambda e: e.matmul(ps, row, src_lo[:, t // P, :], start=False, stop=True))
            return k

        def select(q):
            n, lo = len(tiles(q)), q * QUAD
            at = (q % S_QUADS) * QUAD
            t_sel[q] = run("dve", "select", lambda e: e.tensor_tensor(
                S[:, at:at + n, :], bank[q % 2][:, 0:n * P].rearrange("p (a b) -> p a b", a=n),
                src_c[:, lo:lo + n].unsqueeze(2).broadcast_to((P, n, P)), ALU.is_equal),
                t_spread[q], *([t_bt[q - S_QUADS]] if q >= S_QUADS else []))
            for t in tiles(q):
                t_oh[q] = run("dve", "oh", lambda e: e.tensor_scalar(
                    OH[:, t % (2 * QUAD), :], iota_p, dst_rel[:, t:t + 1], w_c[:, t:t + 1], ALU.is_equal, ALU.mult),
                    *([t_bt[q - 2]] if q >= 2 else []))
            for t in tiles(q):
                t_dup[q] = run("dve", "dup", lambda e: e.scalar_tensor_tensor(
                    out=unread[:, t % QUAD, :], in0=S[:, t % (S_QUADS * QUAD), :], scalar=1.0, in1=after_, op0=ALU.mult, op1=ALU.mult,
                    accum_out=dup[:, t:t + 1]), t_sel[q])

        def indices(q):
            lo, hi = tiles(q)[0], tiles(q)[-1] + 1
            k = run("dve", "idx", lambda e: e.scalar_tensor_tensor(
                out=dup[:, lo:hi], in0=dup[:, lo:hi], scalar=1.0, in1=trash_minus[:, lo:hi],
                op0=ALU.min, op1=ALU.mult), t_dup[q])
            t_idx[q] = run("dve", "idx", lambda e: e.tensor_tensor(put_i[:, lo:hi], dup[:, lo:hi], src_c[:, lo:hi], ALU.add), k)

        def window(q):
            wait("sp", t_base, *t_xnd, *([t_sum[q - 3]] if q >= 3 else []), *t_ring_done)
            row = nc.sync.value_load(base_i[0:1, q:q + 1], min_val=0, max_val=NP_ - P)
            t_win[q] = dma("sp", f"win{q % 3}", win[:, q % 3, :], xn_dram[bass.ds(row, P), :])

        def between(q):
            n = len(tiles(q))
            for t in tiles(q):
                t_bt[q] = run("pe", "bt", lambda e: e.matmul(
                    bank[2][:, (t % QUAD) * P:(t % QUAD + 1) * P], OH[:, t % (2 * QUAD), :],
                    S[:, t % (S_QUADS * QUAD), :], start=True, stop=True),
                    t_oh[q], t_sel[q], *([t_Bs[q - 1]] if q else [t_base]))
            t_Bs[q] = run("act", "Bs", lambda e: e.activation(
                B[:, (q % 2) * QUAD:(q % 2) * QUAD + n, :].rearrange("p a b -> p (a b)"), bank[2][:, 0:n * P], ACT.Copy),
                t_bt[q], *([t_sum[q - 2]] if q >= 2 else []))

        def combine(q):
            for h, t in enumerate(tiles(q)[::2]):
                ps = bank[3 + h]
                for u in (t, t + 1):
                    t_sum[q] = run("pe", "sum", lambda e: e.matmul(
                        ps[:, (u - t) * D:(u - t + 1) * D], B[:, u % (2 * QUAD), :], win[:, q % 3, :],
                        start=True, stop=True), t_Bs[q], t_win[q], *([t_row[t - QUAD]] if q else []))
                t_row[t] = t_row[t + 1] = run("act", "row", lambda e: e.activation(
                    M[:, t % (2 * QUAD):t % (2 * QUAD) + 2, :].rearrange("p a b -> p (a b)"), ps[:, :], ACT.Copy),
                    t_sum[q], *([t_put[t - 2 * QUAD], t_put[t + 1 - 2 * QUAD]] if q >= 2 else []))

        acc_of = [t % (N_ACC - 1) if t < EARLY else t % N_ACC for t in range(ET)]
        last_put = {}

        def put(t):
            i = acc_of[t]
            t_put[t] = last_put[i] = run("pool", f"put{i}", lambda e: e.indirect_dma_start(
                acc_dram[i], bass.IndirectOffsetOnAxis(put_i[:, t:t + 1], 0), M[:, t % (2 * QUAD), :], None,
                compute_op=ALU.add),
                t_row[t], t_idx[t // QUAD], t_acc0[i], *([last_put[i]] if i in last_put else []), by=16)

        def mix():
            t_acc, t_kvn, t_cp, t_fr = [], {}, {}, {}
            first = [t_w, *t_ring_done, t_xnT[-1], t_tables, t_identb]
            for row, row_b in ((bkv, bkv_b), (b2row, b2_b)):
                n = row.shape[1]
                p1, r = kvd.bitcast(BF16)[:, 0:n], kvq[:, 0:n]
                k = run("dve", "bias", lambda e: e.tensor_copy(p1, row), *first)
                run("dve", "bias", lambda e: e.tensor_scalar(row_b, p1, ident[:, 0:1], None, ALU.mult), k)
                k = run("dve", "bias", lambda e: e.tensor_tensor(r, row, p1, ALU.subtract), k)
                k = run("dve", "bias", lambda e: e.tensor_copy(p1, r), k)
                run("dve", "bias", lambda e: e.scalar_tensor_tensor(
                    out=row_b, in0=p1, scalar=ident[:, 1:2], in1=row_b, op0=ALU.mult, op1=ALU.add), k)
                k = run("dve", "bias", lambda e: e.tensor_tensor(r, r, p1, ALU.subtract), k)
                k = run("dve", "bias", lambda e: e.scalar_tensor_tensor(
                    out=row_b, in0=r, scalar=ident[:, 2:3], in1=row_b, op0=ALU.mult, op1=ALU.add), k)
                t_bias = k
            yield

            def kv_add(t):
                rows = TAIL if t == NT - 1 else P
                for g in range(2):
                    k = run("pe", "kvacc", lambda e: e.matmul(
                        bank[6 + g][:, 0:P], kvn[0:rows, t % 2, g * P:(g + 1) * P],
                        kvn[0:rows, t % 2, D + g * P:D + (g + 1) * P], start=(t == 0), stop=False),
                        t_kvn[t])
                    for i in range(2):
                        k = run("pe", "kvacc", lambda e: e.matmul(
                            bank[6 + g][:, P + i:P + i + 1], kvn[0:rows, t % 2, i * D + g * P:i * D + (g + 1) * P],
                            ones[0:rows, 0:1], start=False, stop=(t == NT - 1 and i == 1)))
                t_acc.append(k)

            for t in range(NT):
                ps = bank[5][:, :]
                for q in range(KC):
                    run("pe", None, lambda e: e.matmul(
                        ps, xnT[:, q, t * P:(t + 1) * P], Wqkv[:, q, D:3 * D], start=(q == 0), stop=False),
                        *first, *([t_cp[t - 1]] if t else []))
                p_ = run("pe", "kvp", lambda e: e.matmul(ps, ones_b, bkv_b, start=False, stop=True), t_bias)
                t_cp[t] = run("act", "kvcp", lambda e: e.activation(kvs[:, t % 2, :], ps, ACT.Copy),
                              p_, *([t_fr[t - 2]] if t >= 2 else []))
                yield
                g3 = kvs[:, t % 2, :].rearrange("p (g d) -> p g d", d=HD)
                d3 = kvd.rearrange("p (g d) -> p g d", d=HD)
                q3 = kvq.rearrange("p (g d) -> p g d", d=HD)
                k = run("dve", "kvln", lambda e: e.tensor_reduce(ksum, g3, AX.X, ALU.add), t_cp[t])
                k = run("dve", "kvln", lambda e: e.scalar_tensor_tensor(
                    out=d3, in0=ksum.unsqueeze(2).broadcast_to((P, 16, HD)), scalar=-1.0 / HD, in1=g3,
                    op0=ALU.mult, op1=ALU.add), k)
                t_fr[t] = k
                k = run("act", "kvsq", lambda e: e.activation(kvq, kvd, ACT.Square), k)
                yield
                k = run("dve", "kvln", lambda e: e.tensor_reduce(kvar, q3, AX.X, ALU.add), k)
                k = run("act", "kvsq", lambda e: e.activation(kve, kvar, ACT.Sqrt, bias=eps_col, scale=1.0 / HD), k)
                yield
                k = run("dve", "kvln", lambda e: e.reciprocal(krs, kve), k)
                k = run("dve", "kvln", lambda e: e.tensor_tensor(
                    kvn[:, t % 2, :].rearrange("p (g d) -> p g d", d=HD), d3,
                    krs.unsqueeze(2).broadcast_to((P, 16, HD)), ALU.mult), k, *([t_acc[t - 2]] if t >= 2 else []))
                t_kvn[t] = k
                if t:
                    kv_add(t - 1)
                yield
            kv_add(NT - 1)
            four = lambda v: v.unsqueeze(1).broadcast_to((P, 4, HD))
            heads4 = lambda v: v.rearrange("p (h d) -> p h d", d=HD)
            gv, bv = four(kvln[:, 0, 1, :]), four(kvln[:, 1, 1, :])
            kcol = ksum[:, 0:2]
            k = t_kvn[NT - 1]
            for i in range(2):
                k = run("dve", "KV", lambda e: e.scalar_tensor_tensor(
                    out=heads4(kvq[:, 0:P]), in0=four(kvln[:, i, 0, :]), scalar=1.0, in1=heads4(ident),
                    op0=ALU.mult, op1=ALU.mult, accum_out=kcol[:, i:i + 1]), k, t_acc[-1])
            k0 = run("dve", "KV", lambda e: e.memset(KV, 0.0))
            for g in range(2):
                sums = kvar[:, 2 * g:2 * g + 2]
                k = run("dve", "KV", lambda e: e.tensor_copy(sums, bank[6 + g][:, P:P + 2]), k, k0)
                k = run("dve", "KV", lambda e: e.tensor_scalar(kvd[:, 0:P], ident, sums[:, 1:2], None, ALU.mult), k)
                p_ = run("pe", "svp", lambda e: e.matmul(
                    bank[5][:, g * P:(g + 1) * P], ones[:, :], kvd[:, 0:P], start=True, stop=True), k, t_cp[NT - 1])
                R, T = kvs[:, g, 0:P], kvs[:, g, P:2 * P]
                k1 = run("dve", "KV", lambda e: e.tensor_tensor(heads4(R), heads4(bank[5][:, g * P:(g + 1) * P]), gv, ALU.mult), p_)
                k1 = run("dve", "KV", lambda e: e.scalar_tensor_tensor(
                    out=heads4(R), in0=bv, scalar=float(N), in1=heads4(R), op0=ALU.mult, op1=ALU.add), k1)
                k = run("dve", "KV", lambda e: e.tensor_tensor(heads4(T), heads4(bank[6 + g][:, 0:P]), gv, ALU.mult))
                k = run("dve", "KV", lambda e: e.scalar_tensor_tensor(
                    out=heads4(T), in0=bv, scalar=sums[:, 0:1], in1=heads4(T), op0=ALU.mult, op1=ALU.add), k)
                k = run("dve", "KV", lambda e: e.tensor_scalar(T, T, kcol[:, 0:1], None, ALU.mult), k)
                k = run("dve", "KV", lambda e: e.scalar_tensor_tensor(
                    out=T, in0=R, scalar=kcol[:, 1:2], in1=T, op0=ALU.mult, op1=ALU.add), k, k1)
                for h in range(4):
                    r = slice(h * HD, (h + 1) * HD)
                    t_KV = run("dve", "KV", lambda e: e.tensor_scalar(KV[r, g, r], T[r, r], 1.0 / N, None, ALU.mult), k)
                yield
            t_kv_done.append(True)

            uses = []

            def next_bank():
                n = len(uses)
                return bank[5 + n % 3], ([uses[n - 3]] if n >= 3 else [t_KV, t_cp[NT - 1]])

            t_retp, t_hp, t_fp = {}, {}, {}
            for c in range(NCH):
                lo, hi = c * CH, min((c + 1) * CH, NP_)
                w = hi - lo
                t_q, t_ret, t_h = {}, {}, {}
                for m in range(KC):
                    ps, free = next_bank()
                    for q in range(KC):
                        p_ = run("pe", "mq", lambda e: e.matmul(
                            ps[:, 0:w], Wqkv[:, q, m * P:(m + 1) * P], xnT[:, q, lo:hi],
                            start=(q == 0), stop=(q == KC - 1)), *free)
                    t_q[m] = run("act", "mqa", lambda e: e.activation(
                        qT[:, m, 0:w], ps[:, 0:w], ACT.Identity, bias=cols[:, 0, m:m + 1]), p_,
                        *([t_retp[c - 1, m]] if c else []))
                    uses.append(t_q[m])
                    yield
                for m in range(KC):
                    ps, free = next_bank()
                    t_retp[c, m] = run("pe", "mo", lambda e: e.matmul(
                        ps[:, 0:w], KV[:, m, :], qT[:, m, 0:w], start=True, stop=True), t_q[m], *free)
                    t_ret[m] = run("dve", "mret", lambda e: e.tensor_tensor(
                        ret[:, m, 0:w], ps[:, 0:w], xnT[:, m, lo:hi], ALU.add), t_retp[c, m],
                        *([t_hp[c - 1]] if c else []))
                    uses.append(t_ret[m])
                    yield
                for m in range(KC):
                    ps, free = next_bank()
                    for q in range(KC):
                        t_hp[c] = run("pe", "mh", lambda e: e.matmul(
                            ps[:, 0:w], Wm1[:, q, m * P:(m + 1) * P], ret[:, q, 0:w],
                            start=(q == 0), stop=(q == KC - 1)), t_ret[q], *free)
                    t_h[m] = run("act", "mha", lambda e: e.activation(
                        hT_mix[:, m, 0:w], ps[:, 0:w], ACT.Gelu, bias=cols[:, 1, m:m + 1]), t_hp[c],
                        *([t_fp[c - 1]] if c else []))
                    uses.append(t_h[m])
                    yield
                for j in range(w // P):
                    t = c * 4 + j
                    ps, free = next_bank()
                    for q in range(KC):
                        run("pe", None, lambda e: e.matmul(
                            ps[:, 0:D], hT_mix[:, q, j * P:(j + 1) * P], Wm2[:, q, :], start=(q == 0), stop=False),
                            t_h[q], *free)
                    t_fp[c] = run("pe", "mfp", lambda e: e.matmul(ps[:, 0:D], ones_b, b2_b, start=False, stop=True))
                    uses.append(run("dve", "mfin", lambda e: e.tensor_tensor(
                        X[:, t, :], X[:, t, :], ps[:, 0:D], ALU.add), t_fp[c], t_xplus))
                    if j % 2:
                        yield
            t_mix_done.extend([uses[-1], t_hp[NCH - 1], t_fp[NCH - 1], t_h[1]])
            while True:
                yield

        t_mix_done, t_kv_done = [], []
        mixer = mix()
        for q in range(3):
            window(q)
        quat = [[(0, 1), (1, 1), (2, 1), (3, 1)], [(1, -1), (0, 1), (3, 1), (2, -1)],
                [(2, -1), (3, -1), (0, 1), (1, 1)], [(3, -1), (2, 1), (1, -1), (0, 1)]]
        Q4 = D // 4
        for i, wd in enumerate((w_gnn1, w_gnn2)):
            for a in range(4):
                for b in range(4):
                    t_hr = dma("sp", "hraw", Hm[i][(a % 2) * Q4:(a % 2 + 1) * Q4, a // 2, b * Q4:(b + 1) * Q4],
                               wd[:, quat[a][b][0] * Q4:(quat[a][b][0] + 1) * Q4])
        t_spread = {q: spread(q) for q in range(2)}
        select(0)
        t_spread[2] = spread(2)
        select(1)
        indices(0)
        for _ in range(MIX_FIRST):
            next(mixer)
        between(0)
        due = 0.0
        for q in range(NQ):
            if q + 3 < NQ:
                t_spread[q + 3] = spread(q + 3)
            if q + 2 < NQ:
                select(q + 2)
            if q + 1 < NQ:
                indices(q + 1)
            due += MIX_DENSE if t_kv_done else MIX_KV
            half = due / 2
            while due > half and due >= 1:
                next(mixer)
                due -= 1
            if q + 1 < NQ:
                between(q + 1)
            combine(q)
            if q + 3 < NQ:
                window(q + 3)
            for t in tiles(q):
                put(t)
            while due >= 1:
                next(mixer)
                due -= 1
        while not t_mix_done:
            next(mixer)
        for i in range(2):
            for a in range(4):
                for b in range(4):
                    if quat[a][b][1] < 0:
                        block = Hm[i][(a % 2) * Q4:(a % 2 + 1) * Q4, a // 2, b * Q4:(b + 1) * Q4]
                        t_H = run("dve", "ham", lambda e: e.tensor_scalar(block, block, -1.0, None, ALU.mult), t_hr)


        all_put = list(last_put.values())
        w_missed, tmp_c = S.rearrange("p a b -> p (a b)")[:, 0:EG * P], M.rearrange("p a b -> p (a b)")[:, 0:EG * P]
        dst_ci = B.rearrange("p a b -> p (a b)")[:, 0:EG * P].bitcast(I32)
        every = ("sp", "act", "pool", "dve", "pe")
        for name in every:
            wait(name, *all_put, t_sum[NQ - 1], t_miss)
        second = {n: pr.sem("second_" + n) for n in ("table", "spread", "select", "sum", "row")}
        got = [pr.sem(f"second_got{i}") for i in range(3)]
        added = [pr.sem(f"second_put{i}") for i in range(N_ACC)]

        def if_missed(e):
            return e.If(e.value_load(missed_i[0:1, 0:1], min_val=0, max_val=E) != 0)

        def wait_added(e, t):
            e.wait_ge(added[t % N_ACC], 16 * (t // N_ACC + 1))


        with nc.Block() as block:
            @block.tensor
            def _(e):
                with if_missed(e):
                    def sum_missed(t):
                        e.wait_ge(second["select"], t + 1)
                        e.wait_ge(got[t % 3], 16 * (t // 3 + 1))
                        if t >= 2:
                            e.wait_ge(second["row"], t - 1)
                        e.matmul(bank[3 + t % 2][:, 0:D], OH[:, t % 2, :], win[:, t % 3, :],
                                 start=True, stop=True).then_inc(second["sum"], 1)
                    for t in range(ET):
                        if t >= 2:
                            e.wait_ge(second["select"], t - 1)
                        row = ident_b[:, t % P:t % P + 1].broadcast_to((P, P))
                        e.matmul(bank[t % 2][:, 0:P], row, src_hi[:, t // P, :], start=True, stop=False)
                        e.matmul(bank[t % 2][:, 0:P], row, src_lo[:, t // P, :], start=False, stop=True)\
                            .then_inc(second["spread"], 1)
                        if t:
                            sum_missed(t - 1)
                    sum_missed(ET - 1)

            @block.vector
            def _(e):
                with if_missed(e):
                    step = second["table"]
                    e.tensor_scalar(tmp_c, dst_rel, float(P), None, ALU.is_ge).then_inc(step, 1)
                    e.wait_ge(step, 1)
                    e.scalar_tensor_tensor(out=tmp_c, in0=dst_rel, scalar=0.0, in1=tmp_c,
                                           op0=ALU.is_lt, op1=ALU.add).then_inc(step, 1)
                    e.wait_ge(step, 2)
                    e.tensor_tensor(w_missed, w_c, tmp_c, ALU.mult).then_inc(step, 1)
                    e.wait_ge(step, 3)
                    e.tensor_tensor(
                        tmp_c.rearrange("p (q j) -> p q j", j=QUAD), dst_rel.rearrange("p (q j) -> p q j", j=QUAD),
                        base_i[:, 0:EG * P // QUAD].unsqueeze(2).broadcast_to((P, EG * P // QUAD, QUAD)),
                        ALU.add).then_inc(step, 1)
                    e.wait_ge(step, 4)
                    e.tensor_copy(dst_ci, tmp_c).then_inc(step, 1)
                    e.wait_ge(step, 5)
                    for t in range(ET):
                        e.wait_ge(second["spread"], t + 1)
                        if t >= 2:
                            e.wait_ge(second["sum"], t - 1)
                        e.tensor_scalar(OH[:, t % 2, :], bank[t % 2][:, 0:P], src_c[:, t:t + 1], w_missed[:, t:t + 1],
                                        ALU.is_equal, ALU.mult).then_inc(second["select"], 1)

            @block.scalar
            def _(e):
                with if_missed(e):
                    e.wait_ge(second["table"], 5)
                    for t in range(ET):
                        e.wait_ge(second["sum"], t + 1)
                        if t >= 2:
                            wait_added(e, t - 2)
                        e.activation(M[:, QUAD + t % 2, :], bank[3 + t % 2][:, 0:D], ACT.Copy).then_inc(second["row"], 1)

            @block.gpsimd
            def _(e):
                with if_missed(e):
                    def put_missed(t):
                        e.wait_ge(second["row"], t + 1)
                        if t >= N_ACC:
                            wait_added(e, t - N_ACC)
                        e.indirect_dma_start(acc_dram[t % N_ACC], bass.IndirectOffsetOnAxis(put_i[:, t:t + 1], 0),
                                             M[:, QUAD + t % 2, :], None, compute_op=ALU.add).then_inc(added[t % N_ACC], 16)
                    e.wait_ge(second["table"], 5)
                    for t in range(ET):
                        if t >= 3:
                            e.wait_ge(second["sum"], t - 2)
                        e.indirect_dma_start(win[:, t % 3, :], None, xn_dram,
                                             bass.IndirectOffsetOnAxis(dst_ci[:, t:t + 1], 0)).then_inc(got[t % 3], 16)
                        if t:
                            put_missed(t - 1)
                    put_missed(ET - 1)

            @block.sync
            def _(e):
                with if_missed(e):
                    for t in range(ET - N_ACC, ET):
                        wait_added(e, t)


        third.again()
        out1T = third(KC, NP_)
        newT = xnT
        third_free = all_put
        work.again()
        work(tmp_at)
        accs = work(3, N_ACC, 2 * D)
        bst = work(KC, NCH, 6)
        bmv = work(KC, 2)
        bsc = work(KC)
        bbi = work(KC)
        pairs = -(-NT // 2)
        t_newT, t_accp, t_o1 = {}, {}, []
        ready, turned_chunks, to_measure = [], [], []

        def first_product(c):
            lo, hi = c * CH, min((c + 1) * CH, NP_)
            w = hi - lo
            for m in range(KC):
                ps = bank[4 + (2 * c + m) % 4]
                for q in range(KC):
                    k = run("pe", "o1p", lambda e: e.matmul(
                        ps[:, 0:w], Hm[0][:, q, m * P:(m + 1) * P], newT[:, q, lo:hi],
                        start=(q == 0), stop=(q == KC - 1)), t_newT[min(4 * c + 3, NT - 1)], t_H,
                        *([t_o1[-4]] if len(t_o1) >= 4 else []))
                t_o1.append(run("act", "o1", lambda e: e.activation(out1T[:, m, lo:hi], ps[:, 0:w], ACT.Copy), k))
                to_measure.append((c, m, t_o1[-1]))

        def measure(c, m, after):
            lo, hi = c * CH, min((c + 1) * CH, N)
            return run("dve", "bst", lambda e: e.bn_stats(bst[:, m, c, :], out1T[:, m, lo:hi]), after)

        for u in range(pairs):
            n = min(2, NT - 2 * u)
            for i in range(N_ACC):
                t_load = dma("sp", f"accl{u % 3}", accs[:, u % 3, i, 0:n * D].rearrange("p (t d) -> p t d", d=D),
                             acc_dram[i][2 * u * P:(2 * u + n) * P, :].rearrange("(t p) d -> p t d", p=P),
                             *third_free, *t_mix_done, *([t_accp[u - 3]] if u >= 3 else [t_H]))
            k = run("dve", "accs", lambda e: e.tensor_tensor(
                accs[:, u % 3, 0:2, 0:n * D], accs[:, u % 3, 0:2, 0:n * D], accs[:, u % 3, 2:4, 0:n * D], ALU.add), t_load)
            k = run("dve", "accs", lambda e: e.tensor_tensor(
                accs[:, u % 3, 0, 0:n * D], accs[:, u % 3, 0, 0:n * D], accs[:, u % 3, 1, 0:n * D], ALU.add), k)
            for t in range(2 * u, 2 * u + n):
                ps = bank[t % 4][:, 0:2 * P]
                at = (t % 2) * D
                for q in range(KC):
                    t_accp[u] = run("pe", "newp", lambda e: e.transpose(
                        ps[:, q * P:(q + 1) * P], accs[:, u % 3, 0, at + q * P:at + (q + 1) * P], ident), k,
                        *([t_newT[t - 4]] if t >= 4 else []))
                t_newT[t] = run("act", "newT", lambda e: e.activation(
                    newT[:, :, t * P:(t + 1) * P], ps.rearrange("p (k n) -> p k n", k=KC), ACT.Copy), t_accp[u])
                if t % 4 == 3 or t == NT - 1:
                    ready.append(t // 4)
            while to_measure:
                measure(*to_measure.pop(0))
            while turned_chunks:
                first_product(turned_chunks.pop(0))
            turned_chunks += ready
            ready = []
        first_product(turned_chunks.pop(0))
        while to_measure:
            kb = measure(*to_measure.pop(0))
        p_, ka = t_o1[-1], t_o1[-1]
        for m in range(KC):
            k = run("dve", "bst", lambda e, m=m: e.bn_aggr(bmv[:, m, :], bst[:, m].rearrange("p a b -> p (a b)")), kb)
        k = run("dve", "bst", lambda e: e.tensor_scalar(bsc, bmv[:, :, 1], EPS, None, ALU.add), k)
        k = run("act", "bsq", lambda e: e.activation(bsc, bsc, ACT.Sqrt), k)
        k = run("dve", "bst", lambda e: e.reciprocal(bsc, bsc), k)
        k = run("dve", "bst", lambda e: e.tensor_tensor(bsc, bsc, cols[:, 2, :], ALU.mult), k)
        k = run("dve", "bst", lambda e: e.scalar_tensor_tensor(
            out=bbi, in0=bmv[:, :, 0], scalar=-1.0, in1=bsc, op0=ALU.mult, op1=ALU.mult), k)
        t_bn = run("dve", "bst", lambda e: e.tensor_tensor(bbi, bbi, cols[:, 3, :], ALU.add), k)
        t_stage4 = [t_bn, p_, ka]
        t_th = {}

        turned.again()
        xh2 = turned(2, CT, DX)
        W1 = turned(2, KC, H)
        W2 = turned(2, HC, D)
        work.again()
        xh = [xh2[:, 0], xh2[:, 1], work(CT, DX)]
        work.again()
        work(tmp_at)
        Wr = work(KC, NX)
        brow = work(NX)
        L = work(NT, NX)
        zT = work(2, KC, P)
        top = work(NT, 8)
        topi = work(NT, 8, dtype=U32)
        oh1 = work(NT, NX)
        oh2 = work(NT, NX)
        ohs = work(NT, NX)
        place = work(NT, NX)
        cnt = work(NT, NX)
        prob = work(NT, 2)
        psum_ = work(NT)
        idf = work(NT, 2)
        posf = work(NT, 2)
        pos_i = work(NT, 2, dtype=I32)
        pos_b = work(NT, 2, dtype=I32)
        pos_hi = work(NT, 2)
        pos_lo = work(NT, 2)
        token = work(NT, dtype=I32)
        token_b = work(NT, dtype=I32)
        token_hi = work(NT)
        token_lo = work(NT)
        tot = work(NX)
        toti = work(NX, dtype=I32)
        endf = work(NX)
        base = work(NX)
        tile_start = work(MT)
        tcmp = work(MT, NX)
        hot_lo = work(4, 2 * P // 2).bitcast(BF16).rearrange("p s (i n) -> p s i n", i=2)
        hot = work(4, 2 * LISTS // 2).bitcast(BF16).rearrange("p s (i n) -> p s i n", i=2)
        hot_hi = work(4, 4 * LISTS // 2).bitcast(BF16).rearrange("p s (i v n) -> p s i v n", i=2, v=2)
        iota_b = work(P // 2).bitcast(BF16)
        assert CT * DX <= KC * 5 * D
        slot_f = work(LISTS)
        slot_t = work(LISTS)

        dma("act", "xtra", xh_dram[TRASH:TRASH + P, :], zeros[:, 0:DX], *third_free)
        t_extra = dma("act", "xtra", sum_dram[TRASH:TRASH + P, :], zeros[:, 0:D])
        k = run("pool", "tok", lambda e: e.iota(token, [[P, NT]], base=0, channel_multiplier=1), t_bn)
        k2 = run("dve", "tokd", lambda e: e.tensor_scalar(
            token_b, token, 6, None, ALU.logical_shift_right), k, p_)
        k2 = run("dve", "tokd", lambda e: e.tensor_scalar(token_hi, token_b, float(-(TRASH // 64)), None, ALU.add), k2)
        k2 = run("dve", "tokd", lambda e: e.tensor_scalar(token_b, token, 63, None, ALU.bitwise_and), k2)
        run("dve", "tokd", lambda e: e.tensor_copy(token_lo, token_b), k2)
        t_tok = run("dve", "tokd", lambda e: e.tensor_copy(iota_b, iota_p))
        t_rw = run("dve", "brz", lambda e: e.memset(brow, 0.0), t_bn)
        dma("sp", "rw", brow[0:1, :], row_br.rearrange("(a n) -> a n", a=1), t_rw)
        t_rw = dma("sp", "rw", Wr, w_router.rearrange("(k p) n -> p k n", p=P))

        for c in range(NCH):
            lo, hi = c * CH, min((c + 1) * CH, NP_)
            for m in range(KC):
                t_th[c] = run("act", "tanh", lambda e: e.activation(
                    out1T[:, m, lo:hi], out1T[:, m, lo:hi], ACT.Tanh, bias=bbi[:, m:m + 1], scale=bsc[:, m:m + 1]),
                    *t_stage4)

        def group(g):
            return range(g * CT, (g + 1) * CT)

        def second_product(t):
            g, ps = t // CT, bank[t % 3][:, 0:D]
            for q in range(KC):
                k = run("pe", "o2p", lambda e: e.matmul(
                    ps, out1T[:, q, t * P:(t + 1) * P], Hm[1][:, q, :], start=(q == 0), stop=(q == KC - 1)),
                    t_th[t // 4], *([t_x2[t - 3]] if t >= 3 else []))
            t_x2[t] = run("dve", "x2", lambda e: e.tensor_tensor(X[:, t, :], X[:, t, :], ps, ALU.add), k)
            if t == group(g)[-1]:
                t_sumd[g] = dma("sp", "sumd", sum_dram[g * CT * P:(t + 1) * P, :].rearrange("(t p) d -> p t d", p=P),
                                X[:, g * CT:t + 1, :], t_x2[t])
            return k

        def first_norm(g, k):
            for t in group(g):
                t_z[t] = run("dve", "z", lambda e: e.tensor_scalar(
                    xh[g % 3][:, t - g * CT, 0:D], X[:, t, :], mv[:, t, 0:1], rstd[:, t:t + 1], ALU.subtract, ALU.mult),
                    k, *([t_xhd[g - 3]] if g >= 3 else []))

        def turn(t):
            g, ps = t // CT, bank[(3, 6, 7)[t % 3]][:, 0:2 * P]
            for q in range(KC):
                t_zp[g] = k = run("pe", "zp", lambda e: e.transpose(
                    ps[:, q * P:(q + 1) * P], xh[g % 3][:, t - g * CT, q * P:(q + 1) * P], ident), t_z[t],
                    *([t_zT[t - 3]] if t >= 3 else []))
            t_zT[t] = run("act", "zT", lambda e: e.activation(
                zT[:, t % 2], ps.rearrange("p (k n) -> p k n", k=KC), ACT.Copy), k,
                *([t_lg[t - 2]] if t >= 2 else []))

        def logit(t, g):
            pl = bank[4 + g % 2][:, (t - g * CT) * NX:(t - g * CT + 1) * NX]
            for q in range(KC):
                run("pe", None, lambda e: e.matmul(
                    pl, zT[:, t % 2, q, :], Wr[:, q, :], start=(q == 0), stop=False), t_zT[t], t_rw,
                    *([t_L[g - 2]] if g >= 2 else []))
            t_lg[t] = run("pe", "lg", lambda e: e.matmul(pl, ones[:, :], brow, start=False, stop=True))

        def second_norm(g, k):
            a = g * CT
            for t in group(g):
                run("dve", "xh", lambda e: e.tensor_scalar(
                    xh[g % 3][:, t - a, 0:D], xh[g % 3][:, t - a, 0:D], mv[:, t, 0:1], rstd[:, t:t + 1],
                    ALU.subtract, ALU.mult), k, t_zp[g])

        def route(g):
            a, b = g * CT, (g + 1) * CT
            t_L[g] = run("dve", "L", lambda e: e.tensor_copy(
                L[:, a:b, :].rearrange("p a b -> p (a b)"), bank[4 + g % 2][:, 0:CT * NX]), t_lg[b - 1])
            t_top = [run("dve", "max", lambda e: e.max(top[:, t, :], L[:, t, :]), t_L[g]) for t in group(g)]
            for t in group(g):
                k = run("dve", "max", lambda e: e.max_index(topi[:, t, :], top[:, t, :], L[:, t, :]), t_top[t - a])
            k1 = run("dve", "sm", lambda e: e.tensor_tensor(
                L[:, a:b], L[:, a:b], top[:, a:b, 0:1].broadcast_to((P, CT, NX)), ALU.subtract), k)
            k1 = run("dve", "sm", lambda e: e.tensor_tensor(
                prob[:, a:b], top[:, a:b, 0:2], top[:, a:b, 0:1].broadcast_to((P, CT, 2)), ALU.subtract))
            run("dve", "rt", lambda e: e.tensor_copy(xh[g % 3][:, :, D + 2:D + 4], topi[:, a:b, 0:2]))
            t_idf[g] = run("dve", "rt", lambda e: e.tensor_copy(idf[:, a:b], topi[:, a:b, 0:2]))
            run("act", None, lambda e: e.activation(L[:, a:b], L[:, a:b], ACT.Exp), k1)
            t_exp[g] = run("act", "sma", lambda e: e.activation(prob[:, a:b], prob[:, a:b], ACT.Exp))

        def weigh(g):
            a, b = g * CT, (g + 1) * CT
            k = run("dve", "sm", lambda e: e.tensor_reduce(psum_[:, a:b], L[:, a:b], AX.X, ALU.add), t_exp[g])
            k = run("dve", "sm", lambda e: e.reciprocal(psum_[:, a:b], psum_[:, a:b]), k)
            k = run("dve", "sm", lambda e: e.tensor_tensor(
                prob[:, a:b], prob[:, a:b], psum_[:, a:b].unsqueeze(2).broadcast_to((P, CT, 2)), ALU.mult), k)
            k = run("dve", "sm", lambda e: e.tensor_tensor(psum_[:, a:b], prob[:, a:b, 0], prob[:, a:b, 1], ALU.add), k)
            k = run("dve", "sm", lambda e: e.reciprocal(psum_[:, a:b], psum_[:, a:b]), k)
            k = run("dve", "sm", lambda e: e.tensor_tensor(
                xh[g % 3][:, :, D:D + 2], prob[:, a:b], psum_[:, a:b].unsqueeze(2).broadcast_to((P, CT, 2)), ALU.mult), k)
            t_xhd[g] = dma("sp", f"xhd{g % 3}", xh_dram[a * P:b * P, :].rearrange("(t p) d -> p t d", p=P),
                           xh[g % 3], k, t_idf[g])

        t_z, t_zp, t_zT, t_lg, t_L, t_idf, t_exp, t_xhd, t_sumd, t_st, t_x2 = ({} for _ in range(11))
        G = NT // CT
        root1 = {}
        for g in range(2):
            for t in group(g):
                second_product(t)
                t_st[g] = row_aggregate(t, row_stats(X[:, t, :], t, t_x2[t]))
            root1[g] = norm_root(g * CT, (g + 1) * CT, t_st[g])
        first_norm(0, norm_inverse(0, CT, root1[0]))
        for g in range(G):
            a, b = g * CT, (g + 1) * CT
            if g + 1 < G:
                first_norm(g + 1, norm_inverse(b, b + CT, root1[g + 1]))
            for t in group(g):
                ahead = t + 2 * CT
                if g + 2 < G:
                    t_o2p = second_product(ahead)
                turn(t)
                if t > a:
                    logit(t - 1, g)
                part2 = row_stats(xh[g % 3][:, t - a, 0:D], t, t_z[t])
                if g + 2 < G:
                    part1 = row_stats(X[:, ahead, :], ahead, t_x2[ahead])
                k = row_aggregate(t, part2)
                if g + 2 < G:
                    t_st[g + 2] = row_aggregate(ahead, part1)
            logit(b - 1, g)
            root2 = norm_root(a, b, k)
            if g + 2 < G:
                root1[g + 2] = norm_root(b + CT, b + 2 * CT, t_st[g + 2])
            if g:
                weigh(g - 1)
            route(g)
            second_norm(g, norm_inverse(a, b, root2))
        t_oh = []
        for i, oh in enumerate((oh1, oh2)):
            t_oh.append(run("dve", "rt", lambda e: e.tensor_tensor(
                oh, iota8.unsqueeze(1).broadcast_to((P, NT, NX)),
                idf[:, :, i:i + 1].broadcast_to((P, NT, NX)), ALU.is_equal), t_idf[G - 1]))
        k = run("dve", "rt", lambda e: e.tensor_tensor(ohs, oh1, oh2, ALU.add), *t_oh)
        flat = ohs.rearrange("p a b -> p (a b)")
        run("pe", None, lambda e: e.matmul(bank[0][:, 0:NT * NX], ones[:, :], flat, start=True, stop=True), k)
        p_ = run("pe", "rank", lambda e: e.matmul(bank[1][:, 0:NT * NX], before, flat, start=True, stop=True))
        weigh(G - 1)
        k = run("dve", "rt", lambda e: e.tensor_copy(cnt.rearrange("p a b -> p (a b)"), bank[0][:, 0:NT * NX]), p_)
        for x_ in range(NX):
            k2 = run("dve", "rt", lambda e: e.tensor_tensor_scan(
                place[:, :, x_], ones[:, 0:NT], cnt[:, :, x_], 0.0, ALU.mult, ALU.add), k)
        k = run("dve", "rt", lambda e: e.tensor_scalar(toti, place[:, NT - 1, :], float(SLOTS - 1), None, ALU.add), k2)
        k = run("dve", "rt", lambda e: e.tensor_scalar(
            toti, toti, SLOTS.bit_length() - 1, None, ALU.logical_shift_right), k)
        k = run("dve", "rt", lambda e: e.tensor_scalar(tot, toti, float(SLOTS), None, ALU.mult), k)
        k = run("dve", "rt", lambda e: e.tensor_tensor_scan(endf, ones[:, 0:NX], tot, 0.0, ALU.mult, ALU.add), k)
        k2 = run("pool", "tst", lambda e: e.iota(tile_start, [[SLOTS, MT]], base=0, channel_multiplier=0,
                                                 allow_small_or_imprecise_dtypes=True), t_bn)
        k2 = run("dve", "rt", lambda e: e.tensor_tensor(
            tcmp, tile_start.unsqueeze(2).broadcast_to((P, MT, NX)),
            endf.unsqueeze(1).broadcast_to((P, MT, NX)), ALU.is_ge), k, k2)
        k2 = run("dve", "rt", lambda e: e.tensor_reduce(tex, tcmp, AX.X, ALU.add), k2)
        k2 = run("dve", "rt", lambda e: e.tensor_scalar(tex, tex, float(NX - 1), None, ALU.min), k2)
        t_tex = run("dve", "rt", lambda e: e.tensor_copy(tex_i, tex), k2)
        k = run("dve", "rt", lambda e: e.tensor_tensor(base, endf, tot, ALU.subtract), k)
        k = run("dve", "rt", lambda e: e.tensor_tensor(place, place, cnt, ALU.subtract), k)
        k = run("dve", "rt", lambda e: e.tensor_tensor(
            place, place, bank[1][:, 0:NT * NX].rearrange("p (a b) -> p a b", b=NX), ALU.add), k)
        k = run("dve", "rt", lambda e: e.tensor_tensor(
            place, place, base.unsqueeze(1).broadcast_to((P, NT, NX)), ALU.add), k)
        for i, oh in enumerate((oh1, oh2)):
            kk = run("dve", "rt", lambda e: e.tensor_tensor(ohs, oh, place, ALU.mult), k, p_)
            k = run("dve", "rt", lambda e: e.tensor_reduce(posf[:, :, i], ohs, AX.X, ALU.add), kk)
        k = run("dve", "rt", lambda e: e.tensor_copy(pos_i, posf), k)
        k1 = run("dve", "rt", lambda e: e.tensor_scalar(pos_b, pos_i, 7, None, ALU.logical_shift_right), k)
        k1 = run("dve", "rt", lambda e: e.tensor_copy(pos_hi, pos_b), k1)
        k1 = run("dve", "rt", lambda e: e.tensor_scalar(pos_b, pos_i, P - 1, None, ALU.bitwise_and), k1)
        t_pos = run("dve", "rt", lambda e: e.tensor_copy(pos_lo, pos_b), k1)
        t_list = {}
        for t in range(NT):
            s = t % 4
            k = run("dve", "hot", lambda e: e.tensor_tensor(
                hot[:, s], iota_b[:, 0:LISTS].unsqueeze(1).broadcast_to((P, 2, LISTS)),
                pos_hi[:, t, :].unsqueeze(2).broadcast_to((P, 2, LISTS)), ALU.is_equal), t_pos, t_tok,
                *([t_list[t - 4]] if t >= 4 else []))
            for v, part in enumerate((token_hi, token_lo)):
                k2 = run("act", "hota", lambda e: e.activation(
                    hot_hi[:, s, :, v, :], hot[:, s], ACT.Copy, scale=part[:, t:t + 1]), k,
                    *([t_list[t - 4]] if t >= 4 else []))
            k = run("dve", "hot", lambda e: e.tensor_tensor(
                hot_lo[:, s], iota_b.unsqueeze(1).broadcast_to((P, 2, P)),
                pos_lo[:, t, :].unsqueeze(2).broadcast_to((P, 2, P)), ALU.is_equal))
            for i in range(2):
                t_list[t] = run("pe", "list", lambda e: e.matmul(
                    bank[7][:, 0:2 * LISTS], hot_lo[:, s, i, :], hot_hi[:, s, i].rearrange("p v n -> p (v n)"),
                    start=(t == 0 and i == 0), stop=(t == NT - 1 and i == 1)), k, k2,
                    t_zT[NT - 1], t_zT[NT - 2], t_zT[NT - 3])
        k = run("dve", "slot", lambda e: e.tensor_scalar(
            slot_f, bank[7][:, 0:LISTS], 64.0, float(TRASH), ALU.mult, ALU.add), t_list[NT - 1])
        k = run("dve", "slot", lambda e: e.tensor_tensor(slot_f, slot_f, bank[7][:, LISTS:2 * LISTS], ALU.add), k)
        k = run("dve", "slot", lambda e: e.tensor_scalar(
            slot_t, slot_f, float(TRASH), trash_col, ALU.is_equal, ALU.mult), k)
        t_slot = run("dve", "slot", lambda e: e.tensor_tensor(slot_i, slot_f, slot_t, ALU.max), k)

        late.close()
        up = ctx.enter_context(nc.sbuf_tensor("up_parts", [P, 4 * KC * H + 2 * 2 * KC * SLOTS], F32R))
        down = ctx.enter_context(nc.sbuf_tensor("down_parts", [P, 4 * HC * D + 2 * HC * SLOTS], F32R))

        def parts(tensor, at, n, a, b):
            return tensor[:, at:at + n * a * b].rearrange("p (n a b) -> p n a b", n=n, a=a)
        W1s = parts(up, 0, 4, KC, H)
        xTs = parts(up, 4 * KC * H, 4, KC, SLOTS)
        W2s = parts(down, 0, 4, HC, D)
        hTs = parts(down, 4 * HC * D, 2, HC, SLOTS)
        node.again()
        xe = node(2, 2, DX)
        ecol = node(3, 2 * KC + HC)
        erow = node(3, D)
        xf = node(KC, SLOTS)
        hf = node(2, 2 * SLOTS)
        yb = node(2, 2, D)
        wsel = node(2, 4)
        up_free = [t_o2p]
        parts_free = [t_slot, t_o2p, t_tex, t_list[NT - 1], t_xhd[G - 1], t_xhd[G - 2], t_xhd[G - 3], *t_exp.values()]
        node_free = [t_sumd[G - 1], t_z[NT - 1]]
        t_w1, t_w2, t_ec, t_xe, t_w1h, t_w2h, t_w1l, t_w2l, t_xf, t_xl, t_xp, t_l1, t_l2, t_g, t_hh, t_hl, t_y, t_ws, \
            t_add, t_wr = ({} for _ in range(20))

        def load(i):
            b = i % 2
            wait("sp", t_tex, *node_free, *([t_w1l[i - 2], t_w2l[i - 2]] if i >= 2 else []),
                 *([t_y[i - 3, 1]] if i >= 3 else []))
            x_ = nc.sync.value_load(tex_i[0:1, i:i + 1], min_val=0, max_val=NX - 1)
            t_w1[i] = dma("sp", f"w1{b}", W1[:, b], w_up[bass.ds(x_, 1), :, :].rearrange("a (k p) n -> p (a k) n", p=P))
            dma("sp", f"ec{i % 3}", ecol[:, i % 3, :], cols_expert[bass.ds(x_, 1), :, :].rearrange("a p n -> (a p) n"))
            t_ec[i] = dma("sp", f"ec{i % 3}", erow[:, i % 3, :], row_be[bass.ds(x_, 1), :].broadcast_to((P, D)))
            t_w2[i] = dma("sp", f"w2{b}", W2[:, b], w_down[bass.ds(x_, 1), :, :].rearrange("a (k p) n -> p (a k) n", p=P))

        def gather(i):
            for c in range(2):
                t_xe[i] = run("pool", f"xe{i % 2}", lambda e: e.indirect_dma_start(
                    xe[:, i % 2, c, :], None, xh_dram, bass.IndirectOffsetOnAxis(slot_i[:, 2 * i + c:2 * i + c + 1], 0)),
                    t_slot, t_extra, t_xhd[G - 1], t_xhd[G - 2], t_xhd[G - 3], *node_free,
                    *([t_xp[i - 2], t_wr[i - 2]] if i >= 2 else []), by=16)

        def high(i, W, Ws, loaded, done, free):
            b = i % 2
            w = W[:, b].rearrange("p a b -> p (a b)")
            s = Ws[:, 2 * b].rearrange("p a b -> p (a b)")
            for a in range(0, KC * H, CH):
                done[i] = run("act", "whigh", lambda e: e.activation(s[:, a:a + CH], w[:, a:a + CH], ACT.Copy),
                              loaded[i], *free)

        def low(i, W, Ws, high_done, done, j, free=()):
            b = i % 2
            w = W[:, b].rearrange("p a b -> p (a b)")[:, j * CH:(j + 1) * CH]
            hi_ = Ws[:, 2 * b].rearrange("p a b -> p (a b)")[:, j * CH:(j + 1) * CH].bitcast(F32)
            lo_ = Ws[:, 2 * b + 1].rearrange("p a b -> p (a b)")[:, j * CH:(j + 1) * CH]
            done[i] = run("dve", "wlow", lambda e: e.tensor_tensor(lo_, w, hi_, ALU.subtract), high_done[i], *free)

        def rows_in(i):
            b = i % 2
            for q in range(KC):
                for c in range(2):
                    t_xp[i] = run("pe", "xeT", lambda e: e.transpose(
                        bank[0][:, q * SLOTS + c * P:q * SLOTS + (c + 1) * P], xe[:, b, c, q * P:(q + 1) * P], ident),
                        t_xe[i], *([t_xf[i - 1]] if i else [t_slot]))
            for q in range(KC):
                t_xf[i] = run("act", "xf", lambda e: e.activation(
                    xf[:, q, :], bank[0][:, q * SLOTS:(q + 1) * SLOTS], ACT.Identity,
                    bias=ecol[:, i % 3, KC + q:KC + q + 1], scale=ecol[:, i % 3, q:q + 1]), t_xp[i], t_ec[i],
                    *([t_xl[i - 1]] if i else []))
            k = run("dve", "xl", lambda e: e.tensor_copy(xTs[:, 2 * b], xf), t_xf[i], *([t_l1[i - 2]] if i >= 2 else parts_free))
            t_xl[i] = run("dve", "xl", lambda e: e.tensor_tensor(xTs[:, 2 * b + 1], xf, xTs[:, 2 * b].bitcast(F32), ALU.subtract), k)
            k = run("dve", "wsel", lambda e: e.tensor_scalar(
                wsel[:, b, :].rearrange("p (c n) -> p c n", n=2), xe[:, b, :, D + 2:D + 4], tex[:, i:i + 1], None, ALU.is_equal),
                t_xe[i], *([t_y[i - 2, 1]] if i >= 2 else []))
            k = run("dve", "wsel", lambda e: e.tensor_tensor(
                wsel[:, b, :].rearrange("p (c n) -> p c n", n=2), wsel[:, b, :].rearrange("p (c n) -> p c n", n=2),
                xe[:, b, :, D:D + 2], ALU.mult), k)
            t_wr[i] = k
            t_ws[i] = run("dve", "wsel", lambda e: e.tensor_tensor(
                wsel[:, b, 0:4:2], wsel[:, b, 0:4:2], wsel[:, b, 1:4:2], ALU.add), k)

        load(0)
        load(1)
        gather(0)
        gather(1)
        high(0, W1, W1s, t_w1, t_w1h, up_free)
        for j in range(4):
            low(0, W1, W1s, t_w1h, t_w1l, j, up_free)
        rows_in(0)
        high(0, W2, W2s, t_w2, t_w2h, parts_free)
        high(1, W1, W1s, t_w1, t_w1h, up_free)
        for j in range(4):
            low(0, W2, W2s, t_w2h, t_w2l, j)
        for i in range(MT):
            b = i % 2
            for h in range(HC):
                n = i * HC + h
                ps = bank[1 + (h // 2) % 4][:, (h % 2) * SLOTS:(h % 2 + 1) * SLOTS]
                terms = [(q, wp, xp) for q in range(KC) for wp, xp in ((0, 0), (0, 1), (1, 0))]
                for q, wp, xp in terms:
                    t_l1[i] = run("pe", "l1", lambda e: e.matmul(
                        ps, W1s[:, 2 * b + wp, q, h * P:(h + 1) * P], xTs[:, 2 * b + xp, q, :],
                        start=((q, wp, xp) == terms[0]), stop=((q, wp, xp) == terms[-1])),
                        t_xl[i], t_w1l[i], t_w1h[i], *([t_g[n - 8 + 1 - h % 2]] if i else []))
                if h % 2 == 0:
                    continue
                j = h // 2
                for u in (h - 1, h):
                    t_g[i * HC + u] = run("act", "g", lambda e: e.activation(
                        hf[:, j % 2, (u % 2) * SLOTS:(u % 2 + 1) * SLOTS],
                        bank[1 + j % 4][:, (u % 2) * SLOTS:(u % 2 + 1) * SLOTS], ACT.Gelu,
                        bias=ecol[:, i % 3, 2 * KC + u:2 * KC + u + 1]), t_l1[i],
                        *([t_hl[4 * i + j - 2]] if 4 * i + j >= 2 else []))
                two = hTs[:, :, h - 1:h + 1, :].rearrange("p n a b -> p n (a b)")
                t_hh[i, j] = run("act", "hh", lambda e: e.activation(two[:, 0], hf[:, j % 2, :], ACT.Copy),
                                 t_g[n], *([t_l2[i - 1]] if i else parts_free))
                t_hl[4 * i + j] = run("dve", "hl", lambda e: e.tensor_tensor(
                    two[:, 1], hf[:, j % 2, :], two[:, 0].bitcast(F32), ALU.subtract), t_hh[i, j],
                    *([t_l2[i - 1]] if i else []))
                if i + 1 < MT:
                    low(i + 1, W1, W1s, t_w1h, t_w1l, j)
            if i + 1 < MT:
                rows_in(i + 1)
                high(i + 1, W2, W2s, t_w2, t_w2h, [])
            if i + 2 < MT:
                load(i + 2)
                gather(i + 2)
                high(i + 2, W1, W1s, t_w1, t_w1h, [t_l1[i]])
            if i + 1 < MT:
                for j in range(4):
                    low(i + 1, W2, W2s, t_w2h, t_w2l, j)
            for h in range(HC):
                for c in range(2):
                    for hp, wp in ((0, 0), (0, 1), (1, 0)):
                        t_l2[i] = run("pe", "l2", lambda e: e.matmul(
                            bank[5 + c][:, 0:D], hTs[:, hp, h, c * P:(c + 1) * P], W2s[:, 2 * b + wp, h, :],
                            start=(h == 0 and hp == 0 and wp == 0), stop=(h == HC - 1 and hp == 1)),
                            t_hl[4 * i + h // 2], t_w2l[i], *([t_y[i - 1, c]] if i else []))
            for c in range(2):
                k = run("dve", "yadd", lambda e: e.tensor_tensor(yb[:, b, c, :], bank[5 + c][:, 0:D], erow[:, i % 3, :], ALU.add),
                        t_l2[i], t_ec[i], *([t_add[2 * i - 4 + c]] if i >= 2 else []))
                t_y[i, c] = run("dve", "yadd", lambda e: e.tensor_scalar(
                    yb[:, b, c, :], yb[:, b, c, :], wsel[:, b, 2 * c:2 * c + 1], None, ALU.mult), k, t_ws[i])
                n = 2 * i + c
                t_add[n] = run("pool", "add", lambda e: e.indirect_dma_start(
                    sum_dram, bass.IndirectOffsetOnAxis(slot_i[:, n:n + 1], 0), yb[:, b, c, :], None,
                    compute_op=ALU.add), t_y[i, c], *([t_add[n - 1]] if n else [t_sumd[G - 1]]), by=16)

        pieces = 4
        step = N * D // pieces
        for i in range(pieces):
            o_, s_ = (a.rearrange("n d -> (n d)")[i * step:(i + 1) * step].rearrange("(a b) -> a b", a=80)
                      for a in (out, sum_dram))
            k = dma(("sp", "act")[i % 2], "out", o_, s_, t_add[2 * MT - 1])
        wait("sp", k)
        wait("act", k)


def kernel(x, src, dst, edge_weight, L0_gnn_weight1, L0_gnn_weight2, L0_gnn_gamma, L0_gnn_beta, L0_mix_w_qkv,
           L0_mix_b_qkv, L0_mix_kln_g, L0_mix_kln_b, L0_mix_vln_g, L0_mix_vln_b, L0_mix_w1, L0_mix_b1, L0_mix_w2,
           L0_mix_b2, L0_ffn_Wr, L0_ffn_br, L0_ffn_ln_g, L0_ffn_ln_b, L0_ffn_W1, L0_ffn_b1, L0_ffn_W2, L0_ffn_b2):
    import numpy as np
    import concourse.bacc as bacc
    from concourse.bass_utils import run_bass_kernel_spmd

    D, heads = 256, 8
    hd = D // heads

    def col(v):
        return np.asarray(v).reshape(-1, P).T
    bq3 = np.asarray(L0_mix_b_qkv).reshape(heads, 3, hd)
    NX = L0_ffn_W1.shape[0]
    arrays = {
        "x": x, "src": src, "dst": dst, "ew": edge_weight, "w_gnn1": L0_gnn_weight1, "w_gnn2": L0_gnn_weight2,
        "w_qkv": np.asarray(L0_mix_w_qkv).reshape(D, heads, 3, hd).transpose(0, 2, 1, 3).reshape(D, 3 * D),
        "row_bkv": bq3[:, 1:].transpose(1, 0, 2).reshape(2 * D),
        "kv_ln": np.concatenate([np.asarray(v) for v in (L0_mix_kln_g, L0_mix_vln_g, L0_mix_kln_b, L0_mix_vln_b)]),
        "w_mix1": L0_mix_w1, "w_mix2": L0_mix_w2,
        "cols_mix": np.concatenate([col(bq3[:, 0].reshape(D)), col(L0_mix_b1), col(L0_gnn_gamma), col(L0_gnn_beta)], 1),
        "row_b2": L0_mix_b2, "w_router": L0_ffn_Wr, "row_br": L0_ffn_br, "w_up": L0_ffn_W1, "w_down": L0_ffn_W2,
        "cols_expert": np.concatenate([np.asarray(v).reshape(NX, -1, P).transpose(0, 2, 1)
                                       for v in (L0_ffn_ln_g, L0_ffn_ln_b, L0_ffn_b1)], 2),
        "row_be": L0_ffn_b2,
    }
    arrays = {f"in_{n}": np.ascontiguousarray(a) for n, a in arrays.items()}
    nc = bacc.Bacc("TRN2", target_bir_lowering=False, num_devices=1)
    args = [nc.dram_tensor(n, a.shape, mybir.dt.from_np(a.dtype), kind="ExternalInput").ap() for n, a in arrays.items()]
    out = nc.dram_tensor("out", tuple(x.shape), F32, kind="ExternalOutput").ap()
    gps_layer(nc, *args, out)
    r = run_bass_kernel_spmd(nc, [arrays], core_ids=[0])
    return r.results[0]["out"]
```
